# Optimizing a Trainium2 kernel written in Bass

```python
import numpy as np
import jax
import jax.numpy as jnp

def _softmax(x, axis=-1):
    return jax.nn.softmax(x, axis=axis)

def _gelu(x):
    return jax.nn.gelu(x, approximate=True)

def _silu(x):
    return jax.nn.silu(x)

def _sigmoid(x):
    return jax.nn.sigmoid(x)

def _layernorm(x, axis=-1, eps=1e-05):
    m = jnp.mean(x, axis=axis, keepdims=True)
    v = jnp.var(x, axis=axis, keepdims=True)
    return (x - m) / jnp.sqrt(v + eps)

def _scatter_add(tgt, idx, src, axis=0):
    return tgt.at[idx].add(src)

def _segment_sum(src, seg, n):
    return jax.ops.segment_sum(src, seg, n)
kernel_name = 'mk_macaron_d2_jaxref_r8_daa5a9'

def setup_inputs(seed: int=0):
    np.random.seed(seed)
    _w = jnp.asarray

    def _L0_attn_setup():
        import math
        import jax, jax.numpy as jnp
        import numpy as np
        from jax.scipy.special import xlogy, gammaln

        def get_positional_embed(seq_len, feature_size):
            distances = jnp.arange(-seq_len + 1, seq_len, dtype=jnp.float32)
            n = feature_size // 6
            absd = jnp.abs(distances)[:, None]
            max_range = math.log(seq_len) / math.log(2.0)
            half_life = 2.0 ** jnp.linspace(3.0, max_range, n)
            feat_exp = jnp.exp(-math.log(2.0) / half_life[None, :] * absd)
            center_widths = 2.0 ** jnp.arange(1, n + 1, dtype=jnp.float32) - 1.0
            feat_cm = (center_widths[None, :] > absd).astype(jnp.float32)
            stddev = seq_len / (2.0 * n)
            start_mean = seq_len / n
            mean = jnp.linspace(start_mean, float(seq_len), n)[None, :]
            conc = (mean / stddev) ** 2
            rate = mean / stddev ** 2
            log_unnorm = xlogy(conc - 1.0, absd) - rate * absd
            log_norm = gammaln(conc) - conc * jnp.log(rate)
            probs = jnp.exp(log_unnorm - log_norm) + 1e-08
            feat_gamma = probs / jnp.max(probs, axis=-1, keepdims=True)
            emb = jnp.concatenate([feat_exp, feat_cm, feat_gamma], axis=-1)
            emb = jnp.concatenate([emb, jnp.sign(distances)[:, None] * emb], axis=-1)
            return emb

        def relative_shift(x):
            b, h, t1, t2m1 = x.shape
            x = jnp.pad(x, ((0, 0), (0, 0), (0, 0), (1, 0)))
            t2 = t2m1 + 1
            x = x.reshape(b, h, t2, t1)
            x = x[:, :, 1:, :]
            x = x.reshape(b, h, t1, t2 - 1)
            return x[..., :(t2 + 1) // 2]
        key = jax.random.key(seed)
        ks = jax.random.split(key, 9)
        B, L, D = (2, 128, 128)
        H, Dk, Dv = (8, 128, 128)
        R = 192
        sq = math.sqrt(2.0 / (D + Dk))
        sv = math.sqrt(2.0 / (D + Dv))
        return {'q': jax.random.normal(ks[0], (B, L, D), jnp.float32), 'w_qs': jax.random.normal(ks[1], (D, H * Dk), jnp.float32) * sq, 'w_ks': jax.random.normal(ks[2], (D, H * Dk), jnp.float32) * sq, 'w_vs': jax.random.normal(ks[3], (D, H * Dv), jnp.float32) * sv, 'w_rel_pos_k': jax.random.normal(ks[4], (R, H * Dk), jnp.float32) * 0.05, 'rel_embed_bias': jax.random.normal(ks[5], (1, H, 1, Dk), jnp.float32), 'rel_pos_bias': jax.random.normal(ks[6], (1, H, 1, Dk), jnp.float32), 'w_out': jax.random.normal(ks[7], (H * Dv, D), jnp.float32) * 0.02, 'b_out': jax.random.normal(ks[8], (D,), jnp.float32) * 0.02}
    _L0_attn_in = _L0_attn_setup()

    def _L0_ffn_setup():
        import jax, jax.numpy as jnp
        import numpy as np
        DIM = 128
        DEPTH = 2
        HEADS = 8
        DIM_HEAD = 64
        WINDOW = 64
        INNER = HEADS * DIM_HEAD
        HID = int(DIM * 4 * 2 / 3)
        B, N = (2, 1024)
        QK_SCALE = 8.0

        def shift_token(t):
            t1, t2 = jnp.split(t, 2, axis=-1)
            t2 = jnp.pad(t2, ((0, 0), (1, 0), (0, 0)))[:, :-1]
            return jnp.concatenate([t1, t2], axis=-1)

        def l2norm(t):
            return t / jnp.clip(jnp.linalg.norm(t, axis=-1, keepdims=True), 1e-12)

        def rotate_half(x):
            x1, x2 = jnp.split(x, 2, axis=-1)
            return jnp.concatenate([-x2, x1], axis=-1)

        def rotary_xpos(q, k):
            n = q.shape[-2]
            half_idx = jnp.arange(0, DIM_HEAD, 2, dtype=jnp.float32)
            inv_freq = 1.0 / 10000.0 ** (half_idx / DIM_HEAD)
            t = jnp.arange(n, dtype=jnp.float32)
            freqs = t[:, None] * inv_freq[None, :]
            freqs = jnp.concatenate([freqs, freqs], axis=-1)
            base = (half_idx + 0.4 * DIM_HEAD) / (1.4 * DIM_HEAD)
            power = (t - n // 2) / float(WINDOW // 2)
            scale = base[None, :] ** power[:, None]
            scale = jnp.concatenate([scale, scale], axis=-1)
            cos, sin = (jnp.cos(freqs), jnp.sin(freqs))
            q = q * cos * scale + rotate_half(q) * sin * scale
            k = k * cos / scale + rotate_half(k) * sin / scale
            return (q, k)

        def local_attention(q, k, v):
            b, h, n, d = q.shape
            w = n // WINDOW
            bq = q.reshape(b, h, w, WINDOW, d) * QK_SCALE
            bk = k.reshape(b, h, w, WINDOW, d)
            bv = v.reshape(b, h, w, WINDOW, d)

            def look_around(t):
                p = jnp.pad(t, ((0, 0), (0, 0), (1, 0), (0, 0), (0, 0)))
                return jnp.concatenate([p[:, :, :w], p[:, :, 1:]], axis=3)
            bk, bv = (look_around(bk), look_around(bv))
            bt = jnp.arange(n).reshape(w, WINDOW)
            btp = jnp.pad(bt, ((1, 0), (0, 0)), constant_values=-1)
            btk = jnp.concatenate([btp[:w], btp[1:]], axis=1)
            sim = jnp.einsum('bhwid,bhwjd->bhwij', bq, bk)
            i = bt[:, :, None]
            j = btk[:, None, :]
            mask = (i < j) | (i > j + WINDOW) | (j == -1)
            sim = jnp.where(mask, -jnp.finfo(sim.dtype).max, sim)
            attn = jax.nn.softmax(sim, axis=-1)
            out = jnp.einsum('bhwij,bhwjd->bhwid', attn, bv)
            return out.reshape(b, h, n, d)

        def _layer(x, wqkv, qs, ksc, wo, lg, lb, w1, b1, w2, b2):
            b, n, _ = x.shape
            h = shift_token(x)
            qkv = h @ wqkv
            q, k, v = jnp.split(qkv, 3, axis=-1)
            to_heads = lambda t: t.reshape(b, n, HEADS, DIM_HEAD).transpose(0, 2, 1, 3)
            q, k, v = (to_heads(q), to_heads(k), to_heads(v))
            q = l2norm(q) * qs
            k = l2norm(k) * ksc
            q, k = rotary_xpos(q, k)
            o = local_attention(q, k, v)
            o = o.transpose(0, 2, 1, 3).reshape(b, n, INNER)
            x = x + o @ wo
            h = shift_token(x)
            mu = h.mean(-1, keepdims=True)
            var = h.var(-1, keepdims=True)
            h = (h - mu) / jnp.sqrt(var + 1e-05) * lg + lb
            h = h @ w1 + b1
            a, g = jnp.split(h, 2, axis=-1)
            h = a * jax.nn.gelu(g, approximate=False)
            x = x + h @ w2 + b2
            return x
        key = jax.random.key(seed)
        ks = jax.random.split(key, 6)
        return {'x': jax.random.normal(ks[0], (B, N, DIM), jnp.float32), 'wqkv': jax.random.normal(ks[1], (DEPTH, DIM, 3 * INNER), jnp.float32) * 0.02, 'q_scale': jnp.ones((DEPTH, DIM_HEAD), jnp.float32), 'k_scale': jnp.ones((DEPTH, DIM_HEAD), jnp.float32), 'wo': jax.random.normal(ks[2], (DEPTH, INNER, DIM), jnp.float32) * 0.02, 'ln_g': jnp.ones((DEPTH, DIM), jnp.float32), 'ln_b': jnp.zeros((DEPTH, DIM), jnp.float32), 'w1': jax.random.normal(ks[3], (DEPTH, DIM, 2 * HID), jnp.float32) * 0.02, 'b1': jnp.zeros((DEPTH, 2 * HID), jnp.float32), 'w2': jax.random.normal(ks[4], (DEPTH, HID, DIM), jnp.float32) * 0.02, 'b2': jnp.zeros((DEPTH, DIM), jnp.float32)}
    _L0_ffn_in = _L0_ffn_setup()

    def _L1_attn_setup():
        import jax, jax.numpy as jnp
        import numpy as np
        BN, L, DM = (2, 128, 128)
        D_STATE, D_CONV, EXPAND = (16, 4, 2)
        D_INNER = DM * EXPAND
        key = jax.random.key(seed)
        ks = jax.random.split(key, 12)
        s = lambda fan: 1.0 / np.sqrt(fan)
        x = jax.random.normal(ks[0], (BN, L, DM), jnp.float32)
        in_w = jax.random.normal(ks[1], (DM, 2 * D_INNER), jnp.float32) * s(DM)
        in_b = jnp.zeros((2 * D_INNER,), jnp.float32)
        conv_w = jax.random.normal(ks[2], (D_CONV, 1, D_INNER), jnp.float32) * s(D_CONV)
        conv_b = jnp.zeros((D_INNER,), jnp.float32)
        A = -jax.random.uniform(ks[3], (D_INNER, D_STATE), jnp.float32, 0.1, 1.0)
        Dp = jnp.ones((D_INNER,), jnp.float32)
        B_w = jax.random.normal(ks[4], (D_INNER, D_STATE), jnp.float32) * s(D_INNER)
        B_b = jnp.zeros((D_STATE,), jnp.float32)
        C_w = jax.random.normal(ks[5], (D_INNER, D_STATE), jnp.float32) * s(D_INNER)
        C_b = jnp.zeros((D_STATE,), jnp.float32)
        dt_w = jax.random.normal(ks[6], (D_INNER, D_INNER), jnp.float32) * s(D_INNER)
        dt_b = jnp.full((D_INNER,), -4.0, jnp.float32)
        out_w = jax.random.normal(ks[7], (D_INNER, DM), jnp.float32) * s(D_INNER)
        out_b = jnp.zeros((DM,), jnp.float32)
        return {'x': x, 'in_w': in_w, 'in_b': in_b, 'conv_w': conv_w, 'conv_b': conv_b, 'A': A, 'Dp': Dp, 'B_w': B_w, 'B_b': B_b, 'C_w': C_w, 'C_b': C_b, 'dt_w': dt_w, 'dt_b': dt_b, 'out_w': out_w, 'out_b': out_b}
    _L1_attn_in = _L1_attn_setup()

    def _L1_ffn_setup():
        import jax, jax.numpy as jnp
        import numpy as np
        TOP_K = 8
        key = jax.random.key(seed)
        ks = jax.random.split(key, 6)
        B, S, D, F, E = (2, 128, 128, 64, 64)
        x = jax.random.normal(ks[0], (B, S, D), dtype=jnp.float32)
        centroids = jax.random.normal(ks[1], (E, D), dtype=jnp.float32) * 0.05
        expert_biases = jnp.zeros((E,), dtype=jnp.float32)
        Ws_up = jax.random.normal(ks[2], (D, F), dtype=jnp.float32) / np.sqrt(D)
        Ws_down = jax.random.normal(ks[3], (F, D), dtype=jnp.float32) / np.sqrt(F)
        W_up = jax.random.normal(ks[4], (E, D, F), dtype=jnp.float32) / np.sqrt(D)
        W_down = jax.random.normal(ks[5], (E, F, D), dtype=jnp.float32) / np.sqrt(F)
        return {'x': x, 'centroids': centroids, 'expert_biases': expert_biases, 'Ws_up': Ws_up, 'Ws_down': Ws_down, 'W_up': W_up, 'W_down': W_down}
    _L1_ffn_in = _L1_ffn_setup()
    _d = {'L0_attn_q': _L0_attn_in['q'], 'L0_attn_w_qs': _L0_attn_in['w_qs'], 'L0_attn_w_ks': _L0_attn_in['w_ks'], 'L0_attn_w_vs': _L0_attn_in['w_vs'], 'L0_attn_w_rel_pos_k': _L0_attn_in['w_rel_pos_k'], 'L0_attn_rel_embed_bias': _L0_attn_in['rel_embed_bias'], 'L0_attn_rel_pos_bias': _L0_attn_in['rel_pos_bias'], 'L0_attn_w_out': _L0_attn_in['w_out'], 'L0_attn_b_out': _L0_attn_in['b_out'], 'L0_ffn_wqkv': _L0_ffn_in['wqkv'], 'L0_ffn_q_scale': _L0_ffn_in['q_scale'], 'L0_ffn_k_scale': _L0_ffn_in['k_scale'], 'L0_ffn_wo': _L0_ffn_in['wo'], 'L0_ffn_ln_g': _L0_ffn_in['ln_g'], 'L0_ffn_ln_b': _L0_ffn_in['ln_b'], 'L0_ffn_w1': _L0_ffn_in['w1'], 'L0_ffn_b1': _L0_ffn_in['b1'], 'L0_ffn_w2': _L0_ffn_in['w2'], 'L0_ffn_b2': _L0_ffn_in['b2'], 'L1_attn_in_w': _L1_attn_in['in_w'], 'L1_attn_in_b': _L1_attn_in['in_b'], 'L1_attn_conv_w': _L1_attn_in['conv_w'], 'L1_attn_conv_b': _L1_attn_in['conv_b'], 'L1_attn_A': _L1_attn_in['A'], 'L1_attn_Dp': _L1_attn_in['Dp'], 'L1_attn_B_w': _L1_attn_in['B_w'], 'L1_attn_B_b': _L1_attn_in['B_b'], 'L1_attn_C_w': _L1_attn_in['C_w'], 'L1_attn_C_b': _L1_attn_in['C_b'], 'L1_attn_dt_w': _L1_attn_in['dt_w'], 'L1_attn_dt_b': _L1_attn_in['dt_b'], 'L1_attn_out_w': _L1_attn_in['out_w'], 'L1_attn_out_b': _L1_attn_in['out_b'], 'L1_ffn_centroids': _L1_ffn_in['centroids'], 'L1_ffn_expert_biases': _L1_ffn_in['expert_biases'], 'L1_ffn_Ws_up': _L1_ffn_in['Ws_up'], 'L1_ffn_Ws_down': _L1_ffn_in['Ws_down'], 'L1_ffn_W_up': _L1_ffn_in['W_up'], 'L1_ffn_W_down': _L1_ffn_in['W_down']}
    _x0 = _d['L0_attn_q']
    _d['L0_attn_q'] = jax.random.normal(jax.random.fold_in(jax.random.key(seed), 1), (16, 256, 128), dtype=_x0.dtype)
    del _x0
    return _d

def reference(L0_attn_q, L0_attn_w_qs, L0_attn_w_ks, L0_attn_w_vs, L0_attn_w_rel_pos_k, L0_attn_rel_embed_bias, L0_attn_rel_pos_bias, L0_attn_w_out, L0_attn_b_out, L0_ffn_wqkv, L0_ffn_q_scale, L0_ffn_k_scale, L0_ffn_wo, L0_ffn_ln_g, L0_ffn_ln_b, L0_ffn_w1, L0_ffn_b1, L0_ffn_w2, L0_ffn_b2, L1_attn_in_w, L1_attn_in_b, L1_attn_conv_w, L1_attn_conv_b, L1_attn_A, L1_attn_Dp, L1_attn_B_w, L1_attn_B_b, L1_attn_C_w, L1_attn_C_b, L1_attn_dt_w, L1_attn_dt_b, L1_attn_out_w, L1_attn_out_b, L1_ffn_centroids, L1_ffn_expert_biases, L1_ffn_Ws_up, L1_ffn_Ws_down, L1_ffn_W_up, L1_ffn_W_down):

    def _L0_attn_ref(q, w_qs, w_ks, w_vs, w_rel_pos_k, rel_embed_bias, rel_pos_bias, w_out, b_out):
        import math
        import jax, jax.numpy as jnp
        import numpy as np
        from jax.scipy.special import xlogy, gammaln

        def get_positional_embed(seq_len, feature_size):
            distances = jnp.arange(-seq_len + 1, seq_len, dtype=jnp.float32)
            n = feature_size // 6
            absd = jnp.abs(distances)[:, None]
            max_range = math.log(seq_len) / math.log(2.0)
            half_life = 2.0 ** jnp.linspace(3.0, max_range, n)
            feat_exp = jnp.exp(-math.log(2.0) / half_life[None, :] * absd)
            center_widths = 2.0 ** jnp.arange(1, n + 1, dtype=jnp.float32) - 1.0
            feat_cm = (center_widths[None, :] > absd).astype(jnp.float32)
            stddev = seq_len / (2.0 * n)
            start_mean = seq_len / n
            mean = jnp.linspace(start_mean, float(seq_len), n)[None, :]
            conc = (mean / stddev) ** 2
            rate = mean / stddev ** 2
            log_unnorm = xlogy(conc - 1.0, absd) - rate * absd
            log_norm = gammaln(conc) - conc * jnp.log(rate)
            probs = jnp.exp(log_unnorm - log_norm) + 1e-08
            feat_gamma = probs / jnp.max(probs, axis=-1, keepdims=True)
            emb = jnp.concatenate([feat_exp, feat_cm, feat_gamma], axis=-1)
            emb = jnp.concatenate([emb, jnp.sign(distances)[:, None] * emb], axis=-1)
            return emb

        def relative_shift(x):
            b, h, t1, t2m1 = x.shape
            x = jnp.pad(x, ((0, 0), (0, 0), (0, 0), (1, 0)))
            t2 = t2m1 + 1
            x = x.reshape(b, h, t2, t1)
            x = x[:, :, 1:, :]
            x = x.reshape(b, h, t1, t2 - 1)
            return x[..., :(t2 + 1) // 2]
        B, L, _ = q.shape
        H, Dk = (rel_embed_bias.shape[1], rel_embed_bias.shape[3])
        Dv = w_vs.shape[1] // H
        scale = Dk ** (-0.5)
        Q = (q @ w_qs).reshape(B, L, H, Dk).transpose(0, 2, 1, 3) * scale
        K = (q @ w_ks).reshape(B, L, H, Dk).transpose(0, 2, 1, 3)
        V = (q @ w_vs).reshape(B, L, H, Dv).transpose(0, 2, 1, 3)
        attn = jnp.einsum('bnqd,bnkd->bnqk', Q + rel_embed_bias, K)
        positions = get_positional_embed(L, w_rel_pos_k.shape[0])
        rel_k = (positions @ w_rel_pos_k).reshape(-1, H, Dk).transpose(1, 0, 2)
        attn_pos = jnp.einsum('bnqd,nkd->bnqk', Q + rel_pos_bias, rel_k)
        attn_pos = relative_shift(attn_pos)
        a = jax.nn.softmax(attn + attn_pos, axis=-1)
        out = jnp.einsum('bnqk,bnkd->bnqd', a, V)
        out = out.transpose(0, 2, 1, 3).reshape(B, L, H * Dv)
        return out @ w_out + b_out

    def _L0_ffn_ref(x, wqkv, q_scale, k_scale, wo, ln_g, ln_b, w1, b1, w2, b2):
        import jax, jax.numpy as jnp
        import numpy as np
        DIM = 128
        DEPTH = 2
        HEADS = 8
        DIM_HEAD = 64
        WINDOW = 64
        INNER = HEADS * DIM_HEAD
        HID = int(DIM * 4 * 2 / 3)
        B, N = (2, 1024)
        QK_SCALE = 8.0

        def shift_token(t):
            t1, t2 = jnp.split(t, 2, axis=-1)
            t2 = jnp.pad(t2, ((0, 0), (1, 0), (0, 0)))[:, :-1]
            return jnp.concatenate([t1, t2], axis=-1)

        def l2norm(t):
            return t / jnp.clip(jnp.linalg.norm(t, axis=-1, keepdims=True), 1e-12)

        def rotate_half(x):
            x1, x2 = jnp.split(x, 2, axis=-1)
            return jnp.concatenate([-x2, x1], axis=-1)

        def rotary_xpos(q, k):
            n = q.shape[-2]
            half_idx = jnp.arange(0, DIM_HEAD, 2, dtype=jnp.float32)
            inv_freq = 1.0 / 10000.0 ** (half_idx / DIM_HEAD)
            t = jnp.arange(n, dtype=jnp.float32)
            freqs = t[:, None] * inv_freq[None, :]
            freqs = jnp.concatenate([freqs, freqs], axis=-1)
            base = (half_idx + 0.4 * DIM_HEAD) / (1.4 * DIM_HEAD)
            power = (t - n // 2) / float(WINDOW // 2)
            scale = base[None, :] ** power[:, None]
            scale = jnp.concatenate([scale, scale], axis=-1)
            cos, sin = (jnp.cos(freqs), jnp.sin(freqs))
            q = q * cos * scale + rotate_half(q) * sin * scale
            k = k * cos / scale + rotate_half(k) * sin / scale
            return (q, k)

        def local_attention(q, k, v):
            b, h, n, d = q.shape
            w = n // WINDOW
            bq = q.reshape(b, h, w, WINDOW, d) * QK_SCALE
            bk = k.reshape(b, h, w, WINDOW, d)
            bv = v.reshape(b, h, w, WINDOW, d)

            def look_around(t):
                p = jnp.pad(t, ((0, 0), (0, 0), (1, 0), (0, 0), (0, 0)))
                return jnp.concatenate([p[:, :, :w], p[:, :, 1:]], axis=3)
            bk, bv = (look_around(bk), look_around(bv))
            bt = jnp.arange(n).reshape(w, WINDOW)
            btp = jnp.pad(bt, ((1, 0), (0, 0)), constant_values=-1)
            btk = jnp.concatenate([btp[:w], btp[1:]], axis=1)
            sim = jnp.einsum('bhwid,bhwjd->bhwij', bq, bk)
            i = bt[:, :, None]
            j = btk[:, None, :]
            mask = (i < j) | (i > j + WINDOW) | (j == -1)
            sim = jnp.where(mask, -jnp.finfo(sim.dtype).max, sim)
            attn = jax.nn.softmax(sim, axis=-1)
            out = jnp.einsum('bhwij,bhwjd->bhwid', attn, bv)
            return out.reshape(b, h, n, d)

        def _layer(x, wqkv, qs, ksc, wo, lg, lb, w1, b1, w2, b2):
            b, n, _ = x.shape
            h = shift_token(x)
            qkv = h @ wqkv
            q, k, v = jnp.split(qkv, 3, axis=-1)
            to_heads = lambda t: t.reshape(b, n, HEADS, DIM_HEAD).transpose(0, 2, 1, 3)
            q, k, v = (to_heads(q), to_heads(k), to_heads(v))
            q = l2norm(q) * qs
            k = l2norm(k) * ksc
            q, k = rotary_xpos(q, k)
            o = local_attention(q, k, v)
            o = o.transpose(0, 2, 1, 3).reshape(b, n, INNER)
            x = x + o @ wo
            h = shift_token(x)
            mu = h.mean(-1, keepdims=True)
            var = h.var(-1, keepdims=True)
            h = (h - mu) / jnp.sqrt(var + 1e-05) * lg + lb
            h = h @ w1 + b1
            a, g = jnp.split(h, 2, axis=-1)
            h = a * jax.nn.gelu(g, approximate=False)
            x = x + h @ w2 + b2
            return x
        for l in range(DEPTH):
            x = _layer(x, wqkv[l], q_scale[l], k_scale[l], wo[l], ln_g[l], ln_b[l], w1[l], b1[l], w2[l], b2[l])
        return x

    def _L1_attn_ref(x, in_w, in_b, conv_w, conv_b, A, Dp, B_w, B_b, C_w, C_b, dt_w, dt_b, out_w, out_b):
        import jax, jax.numpy as jnp
        import numpy as np
        BN, L, DM = (2, 128, 128)
        D_STATE, D_CONV, EXPAND = (16, 4, 2)
        D_INNER = DM * EXPAND
        Bn, Ln, _ = x.shape
        d_inner, d_state = A.shape
        xp = x @ in_w + in_b
        x_z, gate = jnp.split(xp, 2, axis=-1)
        x_conv = jax.lax.conv_general_dilated(x_z, conv_w, window_strides=(1,), padding='SAME', dimension_numbers=('NWC', 'WIO', 'NWC'), feature_group_count=d_inner) + conv_b
        x_conv = jax.nn.silu(x_conv)
        Bm = x_conv @ B_w + B_b
        Cm = x_conv @ C_w + C_b
        dt = jax.nn.softplus(x_conv @ dt_w + dt_b)
        dA = jnp.exp(dt[..., None] * A[None, None])
        dB = dt[..., None] * Bm[..., None, :]

        def scan_fn(h, inp):
            x_t, dA_t, dB_t, C_t = inp
            h = dA_t * h + dB_t * x_t[..., None]
            y_t = jnp.sum(h * C_t[:, None, :], axis=-1)
            return (h, y_t)
        h0 = jnp.zeros((Bn, d_inner, d_state), x.dtype)
        tm = lambda t: jnp.swapaxes(t, 0, 1)
        _, y = jax.lax.scan(scan_fn, h0, (tm(x_conv), tm(dA), tm(dB), tm(Cm)))
        y = jnp.swapaxes(y, 0, 1)
        y = y + x_conv * Dp
        y = y * jax.nn.silu(gate)
        return y @ out_w + out_b

    def _L1_ffn_ref(x, centroids, expert_biases, Ws_up, Ws_down, W_up, W_down):
        import jax, jax.numpy as jnp
        import numpy as np
        TOP_K = 8
        B, S, D = x.shape
        E = centroids.shape[0]
        T = B * S
        xf = x.reshape(T, D)
        shared = jax.nn.silu(xf @ Ws_up) @ Ws_down
        aff = xf @ centroids.T
        biased = aff + expert_biases
        _, idx = jax.lax.top_k(biased, TOP_K)
        sel = jnp.take_along_axis(aff, idx, axis=1)
        w = jax.nn.sigmoid(sel)
        w = w / (jnp.sum(w, axis=-1, keepdims=True) + 1e-08)
        cw = jnp.zeros((T, E), dtype=x.dtype).at[jnp.arange(T)[:, None], idx].add(w)
        h = jax.nn.silu(jnp.einsum('td,edf->etf', xf, W_up))
        y = jnp.einsum('etf,efd->etd', h, W_down)
        routed = jnp.einsum('etd,te->td', y, cw)
        return (shared + routed).reshape(B, S, D)
    x = L0_attn_q
    x = x + 0.5 * _L0_ffn_ref(_layernorm(x, axis=-1), L0_ffn_wqkv, L0_ffn_q_scale, L0_ffn_k_scale, L0_ffn_wo, L0_ffn_ln_g, L0_ffn_ln_b, L0_ffn_w1, L0_ffn_b1, L0_ffn_w2, L0_ffn_b2)
    x = x + _L0_attn_ref(_layernorm(x, axis=-1), L0_attn_w_qs, L0_attn_w_ks, L0_attn_w_vs, L0_attn_w_rel_pos_k, L0_attn_rel_embed_bias, L0_attn_rel_pos_bias, L0_attn_w_out, L0_attn_b_out)
    x = x + 0.5 * _L0_ffn_ref(_layernorm(x, axis=-1), L0_ffn_wqkv, L0_ffn_q_scale, L0_ffn_k_scale, L0_ffn_wo, L0_ffn_ln_g, L0_ffn_ln_b, L0_ffn_w1, L0_ffn_b1, L0_ffn_w2, L0_ffn_b2)
    x = x + 0.5 * _L1_ffn_ref(_layernorm(x, axis=-1), L1_ffn_centroids, L1_ffn_expert_biases, L1_ffn_Ws_up, L1_ffn_Ws_down, L1_ffn_W_up, L1_ffn_W_down)
    x = x + _L1_attn_ref(_layernorm(x, axis=-1), L1_attn_in_w, L1_attn_in_b, L1_attn_conv_w, L1_attn_conv_b, L1_attn_A, L1_attn_Dp, L1_attn_B_w, L1_attn_B_b, L1_attn_C_w, L1_attn_C_b, L1_attn_dt_w, L1_attn_dt_b, L1_attn_out_w, L1_attn_out_b)
    x = x + 0.5 * _L1_ffn_ref(_layernorm(x, axis=-1), L1_ffn_centroids, L1_ffn_expert_biases, L1_ffn_Ws_up, L1_ffn_Ws_down, L1_ffn_W_up, L1_ffn_W_down)
    return x

_drawn_inputs = setup_inputs


def setup_inputs(seed=0):
    import zlib

    import numpy as np

    out = dict(_drawn_inputs(seed))
    spreads = {'L0_ffn_q_scale': (1.0, 0.6),
     'L0_ffn_k_scale': (1.0, 0.6),
     'L0_ffn_ln_g': (1.0, 0.6),
     'L0_ffn_ln_b': (0.0, 0.8),
     'L0_ffn_b1': (0.0, 0.8),
     'L0_ffn_b2': (0.0, 0.1),
     'L1_attn_in_b': (0.0, 0.402),
     'L1_attn_conv_b': (0.0, 0.435),
     'L1_attn_Dp': (1.0, 0.6),
     'L1_attn_B_b': (0.0, 0.454),
     'L1_attn_C_b': (0.0, 0.306),
     'L1_attn_dt_b': (-4.0, 0.6),
     'L1_attn_out_b': (0.0, 0.349),
     'L1_ffn_expert_biases': (0.0, 0.386)}
    factors = {'L0_attn_b_out': 3.536, 'L0_ffn_w1': 3.878, 'L0_ffn_w2': 3.759, 'L1_attn_dt_w': 3.302}
    for name, (base, spread) in spreads.items():
        noise = np.random.default_rng([zlib.crc32(name.encode()), seed]).standard_normal(out[name].shape)
        drawn = base * np.exp(spread * noise) if base else spread * noise
        out[name] = jnp.asarray(drawn.astype(out[name].dtype))
    for name, factor in factors.items():
        out[name] = (out[name] * factor).astype(out[name].dtype)
    return out
```

```python
import math
from contextlib import ExitStack

import numpy as np

import concourse.bass as bass
from concourse import mybir

F32 = mybir.dt.float32
BF16 = mybir.dt.bfloat16
ALU = mybir.AluOpType
ACT = mybir.ActivationFunctionType
AX = mybir.AxisListType.X

BATCH, SEQ, DIM = 16, 256, 128
GROUP_SEQS = 2
TOK = GROUP_SEQS * SEQ
TILES = TOK // 128
GROUPS = BATCH // GROUP_SEQS
STAGES = ("ffn", "attn", "ffn", "moe", "mamba", "moe")

DEPTH, LH, LD, WINDOW = 2, 8, 64, 64
INNER = LH * LD
HID = 341
HC = [(c * 128, min(128, HID - c * 128)) for c in range(3)]
AH, AD, REL = 8, 128, 192
EXPERTS, EF, TOP_K = 64, 64, 8
PAIRS = EXPERTS // 2
CH, STATES, CONV = 256, 16, 4
NEG = -3.0e38


class Signal:

    def __init__(self, sem):
        self.sem, self.n = sem, 0

    def mark(self, instruction):
        instruction.then_inc(self.sem, 1)
        self.n += 1
        return self.n


class Chain(Signal):

    def __init__(self, engine, sem):
        super().__init__(sem)
        self.engine = engine

    def link(self, instruction):
        self.engine.wait_ge(self.sem, self.mark(instruction))


class Buffers:
    pass


def allocate(nc, ctx):
    b = Buffers()

    def sb(name, shape, dt=F32):
        t = ctx.enter_context(nc.sbuf_tensor(name, shape, dt))
        return t

    b.ident = sb("ident", [128, 128])
    b.ident_bf = sb("ident_bf", [128, 128], BF16)
    b.mean_w = sb("mean_w", [128, 128])
    b.eps = sb("eps", [128, 1])
    b.mask_f = sb("mask_f", [128, 320])
    b.mask_bf = sb("mask_bf", [128, 320], BF16)
    b.fold64 = sb("fold64", [128, 64])
    b.pair_sel = sb("pair_sel", [128, PAIRS, 2, 64], BF16)
    b.fold32 = sb("fold32", [128, 32])
    b.state_sel = sb("state_sel", [96, 32, 128], BF16)
    b.rope = sb("rope", [128, 4, 2, 64])
    b.x = sb("x", [128, TOK])
    b.y = sb("y", [128, TOK])
    b.xn = sb("xn", [128, TOK])
    b.cent = sb("cent", [128, TOK])
    b.sq = sb("sq", [128, TOK])
    b.rstd = sb("rstd", [128, TOK])
    b.rows = sb("rows", [128, TILES, 128])
    b.wqkv = sb("wqkv", [128, DEPTH, 3 * INNER])
    b.wo = sb("wo", [128, DEPTH, 4, DIM])
    b.w1 = sb("w1", [128, DEPTH, 2 * HID])
    b.w2 = sb("w2", [128, DEPTH, 3, DIM])
    b.qk_scale = sb("qk_scale", [128, 2, DEPTH, 64])
    b.rope_w = sb("rope_w", [128, DEPTH, 4, 2, 64])
    b.wq = sb("wq", [128, AH * AD])
    b.wk = sb("wk", [128, AH * AD])
    b.wv = sb("wv", [128, AH * AD])
    b.w_out = sb("w_out", [128, AH, DIM])
    b.rel_k = sb("rel_k", [128, AH, 512])
    b.w_up = sb("w_up", [128, EXPERTS * EF])
    b.w_down = sb("w_down", [128, PAIRS, DIM])
    b.ws_up = sb("ws_up", [128, EF])
    b.ws_down = sb("ws_down", [EF, DIM])
    b.centroids = sb("centroids", [EXPERTS, DIM])
    b.centroids_t = sb("centroids_t", [128, EXPERTS])
    b.expert_bias = sb("expert_bias", [128, EXPERTS])
    b.in_w = sb("in_w", [128, 2 * CH])
    b.A = sb("A", [128, 2, STATES])
    b.bc_w = sb("bc_w", [128, 2, 2 * STATES])
    b.dt_w = sb("dt_w", [128, 2, CH])
    b.ssm_out_w = sb("ssm_out_w", [128, 2, DIM])
    b.vec_rows = sb("vec_rows", [128, 128])
    b.vec_cols = sb("vec_cols", [128, 128])
    b.vec_at = {}
    b.work = sb("work", [128, WORK])
    b.psum = ctx.enter_context(nc.psum_tensor("psum", [128, 8 * 512], F32))
    return b


WORK = 17152


def bank(b, i, n=1):
    return b.psum[:, i * 512:(i + n) * 512]


def vec(b, name, n=128):
    at = b.vec_at[name]
    return b.vec_cols[0:n, at:at + 1]


class Carve:

    def __init__(self, b):
        self.b, self.at = b, 0

    def __call__(self, columns, dt=F32):
        words = columns if dt == F32 else columns // 2
        piece = self.b.work[:, self.at:self.at + words]
        self.at += words
        assert self.at <= WORK, self.at
        return piece if dt == F32 else piece.bitcast(dt)


def weights(nc, b, A):
    with ExitStack() as ctx:
        sem = lambda name: ctx.enter_context(nc.semaphore(name))
        loaded, zeroed, made, copied, products = sem("weights_loaded"), sem("rows_zeroed"), sem("setup_made"), sem("setup_copied"), sem("setup_products")
        carve = Carve(b)
        pos = carve(2 * 512).rearrange("p (c n) -> p c n", c=2)
        w_rel = carve(2 * AH * AD).rearrange("p (c n) -> p c n", c=2)
        vectors = []

        def vectors_of(name, source):
            for k in range(source.shape[0]):
                b.vec_at[name, k] = len(vectors)
                vectors.append(source[k:k + 1, :])

        rows_of = lambda ap: ap.rearrange("(c p) -> c p", p=128)
        row = lambda ap: ap.rearrange("(a p) -> a p", a=1)
        vectors_of("rel_embed", A["L0_attn_rel_embed_bias"].rearrange("a h b p -> (a b h) p"))
        vectors_of("rel_pos", A["L0_attn_rel_pos_bias"].rearrange("a h b p -> (a b h) p"))
        vectors_of("b_out", row(A["L0_attn_b_out"]))
        vectors_of("in_b", rows_of(A["L1_attn_in_b"]))
        vectors_of("conv_w", A["L1_attn_conv_w"].rearrange("k a (c p) -> (k a c) p", p=128))
        vectors_of("conv_b", rows_of(A["L1_attn_conv_b"]))
        vectors_of("Dp", rows_of(A["L1_attn_Dp"]))
        vectors_of("dt_b", rows_of(A["L1_attn_dt_b"]))
        vectors_of("ssm_out_b", row(A["L1_attn_out_b"]))
        vectors_of("ln_g", A["L0_ffn_ln_g"])
        vectors_of("ln_b", A["L0_ffn_ln_b"])
        vectors_of("b2", A["L0_ffn_b2"])
        for c, (at, n) in enumerate(HC):
            vectors_of(("b1_value", c), A["L0_ffn_b1"][:, at:at + n])
            vectors_of(("b1_gate", c), A["L0_ffn_b1"][:, HID + at:HID + at + n])
        bc_row = len(vectors)
        b.vec_at["bc_b", 0] = bc_row
        loads = [
            (b.ident[:], A["const_ident"]), (b.fold64[:], A["const_fold64"]), (b.fold32[:], A["const_fold32"]),
            (b.mask_f[:], A["const_mask"]), (b.rope[:], A["const_rope"]),
            (b.wqkv[:], A["L0_ffn_wqkv"].rearrange("l p n -> p l n")),
            (b.w1[:], A["L0_ffn_w1"].rearrange("l p n -> p l n")),
            (b.wq[:], A["L0_attn_w_qs"]), (b.wk[:], A["L0_attn_w_ks"]), (b.wv[:], A["L0_attn_w_vs"]),
            (b.w_out[:], A["L0_attn_w_out"].rearrange("(h p) n -> p h n", p=128)),
            (pos[:, 0, :], A["const_pos"][0:128, :]), (pos[0:64, 1, :], A["const_pos"][128:192, :]),
            (w_rel[:, 0, :], A["L0_attn_w_rel_pos_k"][0:128, :]), (w_rel[0:64, 1, :], A["L0_attn_w_rel_pos_k"][128:192, :]),
            (b.w_up[:].rearrange("p (e f) -> p e f", f=EF), A["L1_ffn_W_up"].rearrange("e p f -> p e f")),
            (b.w_down[:], A["L1_ffn_W_down"].rearrange("(q a) f n -> (a f) q n", a=2)),
            (b.ws_up[:], A["L1_ffn_Ws_up"]), (b.ws_down[:], A["L1_ffn_Ws_down"]),
            (b.centroids[:], A["L1_ffn_centroids"]),
            (b.expert_bias[:], A["L1_ffn_expert_biases"].partition_broadcast(128)),
            (b.in_w[:], A["L1_attn_in_w"]),
            (b.A[:], A["L1_attn_A"].rearrange("(c p) s -> p c s", p=128)),
            (b.bc_w[:, :, 0:STATES], A["L1_attn_B_w"].rearrange("(c p) s -> p c s", p=128)),
            (b.bc_w[:, :, STATES:], A["L1_attn_C_w"].rearrange("(c p) s -> p c s", p=128)),
            (b.dt_w[:], A["L1_attn_dt_w"].rearrange("(c p) n -> p c n", p=128)),
            (b.ssm_out_w[:], A["L1_attn_out_w"].rearrange("(c p) n -> p c n", p=128)),
        ]
        for l in range(DEPTH):
            loads += [
                (b.wo[:, l], A["L0_ffn_wo"][l].rearrange("(c p) n -> p c n", p=128)),
                (b.qk_scale[:, 0, l], A["L0_ffn_q_scale"][l].partition_broadcast(128)),
                (b.qk_scale[:, 1, l], A["L0_ffn_k_scale"][l].partition_broadcast(128)),
            ]
            for c, (at, n) in enumerate(HC):
                loads += [(b.w2[0:n, l, c], A["L0_ffn_w2"][l, at:at + n, :])]

        late = [(b.vec_rows[k:k + 1, 0:src.shape[1]], src) for k, src in enumerate(vectors)]
        late += [(b.vec_rows[bc_row:bc_row + 1, 0:STATES], row(A["L1_attn_B_b"])),
                 (b.vec_rows[bc_row:bc_row + 1, STATES:2 * STATES], row(A["L1_attn_C_b"]))]
        n_loads = len(loads) + len(late)

        with nc.Block() as block:
            @block.sync
            def _(sp):
                for dst, src in loads[0::2]:
                    sp.dma_start(dst, src).then_inc(loaded, 16)
                sp.wait_ge(zeroed, 1)
                for dst, src in late:
                    sp.dma_start(dst, src).then_inc(loaded, 16)

            @block.gpsimd
            def _(pool):
                pool.memset(b.vec_rows[:], 0.0).then_inc(zeroed, 1)
                pool.memset(b.mean_w[:], 1.0 / DIM)
                pool.memset(b.eps[:], 1e-5)

            @block.scalar
            def _(act):
                for dst, src in loads[1::2]:
                    act.dma_start(dst, src).then_inc(loaded, 16)
                for h in range(AH):
                    act.wait_ge(products, h + 2)
                    nc.scalar.copy(b.rel_k[:, h, :], bank(b, h)).then_inc(copied, 1)

            @block.tensor
            def _(pe):
                pe.wait_ge(loaded, 16 * n_loads)
                nc.tensor.transpose(bank(b, 0)[:, 0:EXPERTS], b.centroids[:], b.ident[0:EXPERTS, 0:EXPERTS])
                nc.tensor.transpose(bank(b, 1)[:, 0:128], b.vec_rows[:], b.ident[:]).then_inc(products, 1)
                pe.wait_ge(made, 1)
                for h in range(AH):
                    nc.tensor.matmul(bank(b, h), w_rel[:, 0, h * AD:(h + 1) * AD], pos[:, 0, :], start=True, stop=False)
                    nc.tensor.matmul(bank(b, h), w_rel[0:64, 1, h * AD:(h + 1) * AD], pos[0:64, 1, :],
                                     start=False, stop=True).then_inc(products, 1)

            @block.vector
            def _(dve):
                dve.wait_ge(loaded, 16 * n_loads)
                dve.wait_ge(products, 1)
                nc.vector.tensor_copy(b.centroids_t[:], bank(b, 0)[:, 0:EXPERTS])
                nc.vector.tensor_copy(b.vec_cols[:], bank(b, 1)[:, 0:128]).then_inc(made, 1)
                nc.vector.tensor_copy(b.ident_bf[:], b.ident[:])
                nc.vector.tensor_copy(b.mask_bf[:], b.mask_f[:])
                for p in range(PAIRS):
                    nc.vector.tensor_copy(b.pair_sel[:, p], b.fold64[:, 2 * p:2 * p + 2].unsqueeze(2).broadcast_to([128, 2, 64]))
                for s in range(32):
                    nc.vector.tensor_copy(b.state_sel[:, s, :], b.fold32[0:96, s:s + 1].broadcast_to([96, 128]))
                for l in range(DEPTH):
                    for qk in range(2):
                        sc = b.qk_scale[:, qk, l]
                        for s in range(2):
                            nc.vector.tensor_tensor(b.rope_w[:, l, 2 * qk, s], b.rope[:, 2 * qk, s], sc, ALU.mult)
                            nc.vector.tensor_tensor(b.rope_w[:, l, 2 * qk + 1, s, 0:32], b.rope[:, 2 * qk + 1, s, 0:32], sc[:, 32:64], ALU.mult)
                            nc.vector.tensor_tensor(b.rope_w[:, l, 2 * qk + 1, s, 32:64], b.rope[:, 2 * qk + 1, s, 32:64], sc[:, 0:32], ALU.mult)


class Norm:

    def __init__(self, nc, b, sem):
        self.nc, self.b = nc, b
        self.mean, self.centred, self.squared, self.variance, self.root, self.inverse, self.done = (
            sem(n) for n in ("mean_ready", "centred_ready", "squares_ready", "variance_ready",
                             "deviation_ready", "rstd_ready", "norm_done"))

    def tensor(self, pe, src, banks):
        b = self.b
        self.nc.tensor.matmul(bank(b, banks[0]), b.mean_w[:], src, start=True, stop=True).then_inc(self.mean, 1)
        pe.wait_ge(self.squared, 1)
        self.nc.tensor.matmul(bank(b, banks[1]), b.mean_w[:], b.sq[:], start=True, stop=True).then_inc(self.variance, 1)

    def vector(self, dve, src, dst, banks):
        b, v = self.b, self.nc.vector
        dve.wait_ge(self.mean, 1)
        v.tensor_tensor(b.cent[:], src, bank(b, banks[0]), ALU.subtract).then_inc(self.centred, 1)
        dve.wait_ge(self.root, 1)
        v.reciprocal(b.rstd[:], b.rstd[:]).then_inc(self.inverse, 1)
        dve.wait_ge(self.inverse, 1)
        v.tensor_tensor(dst, b.cent[:], b.rstd[:], ALU.mult).then_inc(self.done, 1)

    def scalar(self, act, banks):
        b = self.b
        act.wait_ge(self.centred, 1)
        self.nc.scalar.activation(b.sq[:], b.cent[:], ACT.Square).then_inc(self.squared, 1)
        act.wait_ge(self.variance, 1)
        self.nc.scalar.activation(b.rstd[:], bank(b, banks[1]), ACT.Sqrt, bias=b.eps[:]).then_inc(self.root, 1)


class Semaphores:

    def __init__(self, nc):
        self.nc, self.ctx, self.held = nc, ExitStack(), []
        with nc.semaphore("lowest") as lowest:
            self.first = lowest.num

    def stage(self, prefix):
        def sem(name):
            self.held.append(self.ctx.enter_context(self.nc.semaphore(f"{prefix}_{name}", num=self.first + len(self.held))))
            return self.held[-1]
        return sem

    def clear(self):
        self.nc.all_engine_barrier(sems_to_clear=range(self.first, self.first + len(self.held)))
        self.ctx.close()
        self.held = []
        self.ctx = ExitStack()


def load_tokens(nc, b, sem, src, g):
    rows_in, turned, copied = sem("rows_in"), sem("rows_turned"), sem("x_copied")
    with nc.Block() as block:
        @block.sync
        def _(sp):
            sp.dma_start(b.rows[:], src[bass.ds(g * TOK, TOK), :].rearrange("(t p) d -> p t d", p=128)).then_inc(rows_in, 16)

        @block.tensor
        def _(pe):
            pe.wait_ge(rows_in, 16)
            for t in range(TILES):
                ins = nc.tensor.transpose(bank(b, 0)[:, t * 128:(t + 1) * 128], b.rows[:, t, :], b.ident[:])
            ins.then_inc(turned, 1)

        @block.vector
        def _(dve):
            dve.wait_ge(turned, 1)
            nc.vector.tensor_copy(b.x[:], bank(b, 0)).then_inc(copied, 1)


def store_tokens(nc, b, sem, dst, g):
    turned, copied, rows_out = sem("out_turned"), sem("out_copied"), sem("rows_out")
    with nc.Block() as block:
        @block.sync
        def _(sp):
            sp.wait_ge(copied, 1)
            sp.dma_start(dst[bass.ds(g * TOK, TOK), :].rearrange("(t p) d -> p t d", p=128), b.rows[:]).then_inc(rows_out, 16)
            sp.wait_ge(rows_out, 16)

        @block.tensor
        def _(pe):
            for t in range(TILES):
                ins = nc.tensor.transpose(bank(b, 0)[:, t * 128:(t + 1) * 128], b.x[:, t * 128:(t + 1) * 128], b.ident[:])
            ins.then_inc(turned, 1)

        @block.vector
        def _(dve):
            dve.wait_ge(turned, 1)
            nc.vector.tensor_copy(b.rows[:], bank(b, 0).rearrange("p (t d) -> p t d", t=TILES)).then_inc(copied, 1)


def moe_stage(nc, b, sem):
    norm = Norm(nc, b, sem)
    affinity, routed, split_turned, split_copied = sem("affinity_ready"), sem("routing_split"), sem("split_turned"), sem("split_copied")
    sig, up, spread, silu, gated, down, vec = (sem("sigmoid_ready"), sem("up_ready"), sem("weight_spread"),
                                               sem("silu_ready"), sem("gated_ready"), sem("down_ready"), sem("vector_steps"))
    carve = Carve(b)
    tiles = lambda n, dt=F32: carve(TILES * n, dt).rearrange("p (t e) -> p t e", t=TILES)
    biased, rest, chosen, prob = tiles(EXPERTS), tiles(EXPERTS), tiles(EXPERTS), tiles(EXPERTS)
    top = tiles(TOP_K)
    total, inverse = carve(TILES), carve(TILES)
    parts = tiles(3 * EXPERTS + 64, BF16)
    high_mid, low = carve(TOK, BF16), carve(TOK, BF16)
    act_h = [carve(TOK) for _ in range(3)]
    gate_h = [carve(TOK) for _ in range(3)]
    UP, SPREAD, SUM, ROUTE = 0, 3, 6, 7
    STEPS = PAIRS + 1
    aff = bank(b, ROUTE)[:, 0:TILES * EXPERTS].rearrange("p (t e) -> p t e", t=TILES)
    with nc.Block() as block:
        @block.tensor
        def _(pe):
            norm.tensor(pe, b.x[:], (0, 1))
            pe.wait_ge(norm.done, 1)
            for t in range(TILES):
                ins = nc.tensor.matmul(aff[:, t, :], b.xn[:, t * 128:(t + 1) * 128], b.centroids_t[:], start=True, stop=True)
            ins.then_inc(affinity, 1)

            def up_step(p):
                if p >= 3:
                    pe.wait_ge(silu, p - 2)
                rows = 128 if p < PAIRS else EF
                w = b.w_up[:, p * 128:(p + 1) * 128] if p < PAIRS else b.ws_up[:]
                nc.tensor.matmul(bank(b, UP + p % 3)[0:rows], w, b.xn[:], start=True, stop=True).then_inc(up, 1)

            def spread_step(p):
                if p >= 3:
                    pe.wait_ge(gated, p - 2)
                nc.tensor.matmul(bank(b, SPREAD + p % 3), b.pair_sel[:, p], high_mid, start=True, stop=False)
                nc.tensor.matmul(bank(b, SPREAD + p % 3), b.pair_sel[0:64, p], low[0:64], start=False, stop=True).then_inc(spread, 1)

            for p in range(3):
                up_step(p)
            pe.wait_ge(routed, 1)
            hm = bank(b, SPREAD).bitcast(BF16)
            lo = bank(b, SPREAD + 1).bitcast(BF16)
            for t in range(TILES):
                nc.tensor.transpose(hm[:, t * 128:(t + 1) * 128], parts[:, t, 0:128], b.ident_bf[:])
            for t in range(TILES):
                ins = nc.tensor.transpose(lo[:, t * 128:(t + 1) * 128], parts[:, t, 128:256], b.ident_bf[:])
            ins.then_inc(split_turned, 1)
            pe.wait_ge(split_copied, 1)
            for p in range(2):
                spread_step(p)
            for p in range(STEPS):
                if p + 3 < STEPS:
                    up_step(p + 3)
                if p + 2 < PAIRS:
                    spread_step(p + 2)
                if p < PAIRS:
                    pe.wait_ge(gated, p + 1)
                    nc.tensor.matmul(bank(b, SUM), b.w_down[:, p], gate_h[p % 3], start=p == 0, stop=False).then_inc(down, 1)
                else:
                    pe.wait_ge(silu, p + 1)
                    nc.tensor.matmul(bank(b, SUM), b.ws_down[:], act_h[p % 3][0:EF], start=False, stop=True).then_inc(down, 1)

        @block.scalar
        def _(act):
            norm.scalar(act, (0, 1))
            act.wait_ge(vec, 1)
            nc.scalar.activation(prob[:], aff[:], ACT.Sigmoid).then_inc(sig, 1)
            for p in range(STEPS):
                rows = 128 if p < PAIRS else EF
                act.wait_ge(up, p + 1)
                if p >= 3:
                    act.wait_ge(gated, p - 2)
                nc.scalar.activation(act_h[p % 3][0:rows], bank(b, UP + p % 3)[0:rows], ACT.Silu).then_inc(silu, 1)

        @block.vector
        def _(dve):
            v = nc.vector
            norm.vector(dve, b.x[:], b.xn[:], (0, 1))
            steps = Chain(dve, vec)
            dve.wait_ge(affinity, 1)
            steps.link(v.tensor_tensor(biased[:], aff[:], b.expert_bias[:].unsqueeze(1).broadcast_to([128, TILES, EXPERTS]), ALU.add))
            for t in range(TILES):
                steps.link(v.max(top[:, t, :], biased[:, t, :]))
                steps.link(v.match_replace(rest[:, t, :], top[:, t, :], biased[:, t, :], NEG))
            steps.link(v.tensor_tensor(chosen[:], rest[:], biased[:], ALU.not_equal))
            dve.wait_ge(sig, 1)
            steps.link(v.tensor_tensor(prob[:], prob[:], chosen[:], ALU.mult))
            steps.link(v.tensor_reduce(total, prob[:], AX, ALU.add))
            steps.link(v.tensor_scalar(total, total, 1e-8, None, ALU.add))
            steps.link(v.reciprocal(inverse, total))
            steps.link(v.tensor_tensor(prob[:], prob[:], inverse.unsqueeze(2).broadcast_to([128, TILES, EXPERTS]), ALU.mult))
            E = EXPERTS
            steps.link(v.tensor_copy(parts[:, :, 0:E], prob[:]))
            steps.link(v.tensor_tensor(prob[:], prob[:], parts[:, :, 0:E], ALU.subtract))
            steps.link(v.tensor_copy(parts[:, :, E:2 * E], prob[:]))
            steps.link(v.tensor_tensor(prob[:], prob[:], parts[:, :, E:2 * E], ALU.subtract))
            v.tensor_copy(parts[:, :, 3 * E:4 * E], prob[:])
            v.tensor_copy(parts[:, :, 2 * E:3 * E], prob[:]).then_inc(routed, 1)
            dve.wait_ge(split_turned, 1)
            v.tensor_copy(high_mid, bank(b, SPREAD).bitcast(BF16)[:, 0:TOK])
            v.tensor_copy(low, bank(b, SPREAD + 1).bitcast(BF16)[:, 0:TOK]).then_inc(split_copied, 1)
            for p in range(PAIRS):
                dve.wait_ge(silu, p + 1)
                dve.wait_ge(spread, p + 1)
                if p >= 3:
                    dve.wait_ge(down, p - 2)
                v.tensor_tensor(gate_h[p % 3], act_h[p % 3], bank(b, SPREAD + p % 3), ALU.mult).then_inc(gated, 1)
            dve.wait_ge(down, STEPS)
            v.scalar_tensor_tensor(out=b.x[:], in0=bank(b, SUM), scalar=0.5, in1=b.x[:], op0=ALU.mult, op1=ALU.add)
def attn_stage(nc, b, sem, scratch):
    norm = Norm(nc, b, sem)
    v_ready, v_copied_a, v_copied_v = sem("v_ready"), sem("v_copied_scalar"), sem("v_copied_vector")
    q_ready, k_ready, q_biased, k_copied = sem("q_ready"), sem("k_ready"), sem("q_biased"), sem("k_copied")
    p_ready, p_copied, p_stored, p_loaded = sem("distance_scores_ready"), sem("distance_scores_copied"), sem("distance_scores_stored"), sem("position_scores_loaded")
    s_ready, summed, maxed, exped, normed = sem("scores_ready"), sem("scores_summed"), sem("scores_maxed"), sem("scores_exped"), sem("probs_normed")
    turned, t_copied, o_ready, o_copied, projected = sem("probs_turned"), sem("probs_copied"), sem("heads_ready"), sem("heads_copied"), sem("projected")
    inverted = sem("sums_inverted")
    carve = Carve(b)
    v_sb = carve(TILES * AH * AD).rearrange("p (t n) -> p t n", t=TILES)
    two = lambda n: [carve(n) for _ in range(2)]
    q_e, q_p, k_t = two(TOK), two(TOK), two(TOK)
    pos = [t.rearrange("p (t k) -> p t k", t=TILES) for t in two(TILES * SEQ)]
    probs = [t.rearrange("p (t k) -> p t k", t=TILES) for t in two(TILES * SEQ)]
    dist = [t.rearrange("p (t k) -> p t k", t=TILES) for t in two(TILES * 384)]
    probs_t = carve(GROUP_SEQS * 2 * SEQ).rearrange("p (s c q) -> p s c q", s=GROUP_SEQS, c=2)
    o_t = carve(TOK)
    neg_max, sums, inv = (carve(2 * TILES).rearrange("p (a t) -> p a t", a=2) for _ in range(3))
    half = AH * AD // 2

    def shifted(slot):
        return bass.AP(tensor=scratch.tensor, offset=slot * TILES * 128 * 384 + 127,
                       ap=[[383, 128], [128 * 384, TILES], [1, SEQ]])

    with nc.Block() as block:
        @block.tensor
        def _(pe):
            norm.tensor(pe, b.x[:], (0, 1))
            pe.wait_ge(norm.done, 1)
            for n in range(2 * TILES):
                if n >= 4:
                    pe.wait_ge(v_copied_v if n % 2 else v_copied_a, (n - 4) // 2 + 1)
                t, side = n // 2, n % 2
                nc.tensor.matmul(bank(b, 4 + n % 4), b.xn[:, t * 128:(t + 1) * 128], b.wv[:, side * half:(side + 1) * half],
                                 start=True, stop=True).then_inc(v_ready, 1)

            def queries_keys(h):
                w = slice(h * AD, (h + 1) * AD)
                if h >= 1:
                    pe.wait_ge(q_biased, h)
                nc.tensor.matmul(bank(b, 0), b.wq[:, w], b.xn[:], start=True, stop=True).then_inc(q_ready, 1)
                if h >= 1:
                    pe.wait_ge(k_copied, h)
                nc.tensor.matmul(bank(b, 1), b.wk[:, w], b.xn[:], start=True, stop=True).then_inc(k_ready, 1)
                pe.wait_ge(q_biased, h + 1)
                for t in range(TILES):
                    n = h * TILES + t
                    if n >= 2:
                        pe.wait_ge(p_copied, n - 1)
                    first = 128 if t % 2 == 0 else 0
                    nc.tensor.matmul(bank(b, 2 + n % 2)[:, 0:384], q_p[h % 2][:, t * 128:(t + 1) * 128],
                                     b.rel_k[:, h, first:first + 384], start=True, stop=True).then_inc(p_ready, 1)

            def scores(h):
                pe.wait_ge(k_copied, h + 1)
                for s in range(GROUP_SEQS):
                    if h >= 1:
                        pe.wait_ge(summed, GROUP_SEQS * (h - 1) + s + 1)
                    elif s == 0:
                        pe.wait_ge(v_copied_a, TILES)
                        pe.wait_ge(v_copied_v, TILES)
                    for t in range(2):
                        at = (2 * s + t) * 128
                        ins = nc.tensor.matmul(bank(b, 4 + s)[:, t * SEQ:(t + 1) * SEQ], q_e[h % 2][:, at:at + 128],
                                               k_t[h % 2][:, s * SEQ:(s + 1) * SEQ], start=True, stop=True)
                    ins.then_inc(s_ready, 1)

            def values(h):
                for s in range(GROUP_SEQS):
                    n = GROUP_SEQS * h + s
                    pe.wait_ge(normed, n + 1)
                    if n >= 1:
                        pe.wait_ge(t_copied, n)
                    for t in range(2):
                        for c in range(2):
                            ins = nc.tensor.transpose(bank(b, 6)[:, c * SEQ + t * 128:c * SEQ + (t + 1) * 128],
                                                      probs[h % 2][:, 2 * s + t, c * 128:(c + 1) * 128], b.ident[:])
                    ins.then_inc(turned, 1)
                for s in range(GROUP_SEQS):
                    pe.wait_ge(t_copied, GROUP_SEQS * h + s + 1)
                    for c in range(2):
                        ins = nc.tensor.matmul(bank(b, 1)[:, s * SEQ:(s + 1) * SEQ], v_sb[:, 2 * s + c, h * AD:(h + 1) * AD],
                                               probs_t[:, s, c], start=c == 0, stop=c == 1)
                ins.then_inc(o_ready, 1)
                pe.wait_ge(o_copied, h + 1)
                nc.tensor.matmul(bank(b, 7), b.w_out[:, h], o_t, start=h == 0, stop=h == AH - 1).then_inc(projected, 1)

            for i in range(AH + 2):
                if i < AH:
                    queries_keys(i)
                if 1 <= i <= AH:
                    scores(i - 1)
                if i >= 2:
                    values(i - 2)

        @block.sync
        def _(sp):
            for h in range(AH):
                slot = h % 2
                sp.wait_ge(p_copied, TILES * (h + 1))
                if h >= 2:
                    sp.wait_ge(p_loaded, 16 * (h - 1))
                sp.dma_start(scratch[slot].rearrange("t p k -> p t k"), dist[slot]).then_inc(p_stored, 16)
                sp.wait_ge(p_stored, 16 * (h + 1))
                if h >= 2:
                    sp.wait_ge(summed, GROUP_SEQS * (h - 1))
                sp.dma_start(pos[slot], shifted(slot)).then_inc(p_loaded, 16)

        @block.scalar
        def _(act):
            norm.scalar(act, (0, 1))
            for n in range(0, 2 * TILES, 2):
                act.wait_ge(v_ready, n + 1)
                nc.scalar.copy(v_sb[:, n // 2, 0:half], bank(b, 4 + n % 4)).then_inc(v_copied_a, 1)

            def biased(h):
                act.wait_ge(q_ready, h + 1)
                if h >= 2:
                    act.wait_ge(s_ready, GROUP_SEQS * (h - 1))
                scale = AD ** -0.5
                nc.scalar.activation(q_p[h % 2], bank(b, 0), ACT.Identity, bias=vec(b, ("rel_pos", h)), scale=scale)
                nc.scalar.activation(q_e[h % 2], bank(b, 0), ACT.Identity, bias=vec(b, ("rel_embed", h)), scale=scale).then_inc(q_biased, 1)

            def distances(h):
                if h >= 2:
                    act.wait_ge(p_stored, 16 * (h - 1))
                for t in range(TILES):
                    n = h * TILES + t
                    act.wait_ge(p_ready, n + 1)
                    nc.scalar.copy(dist[h % 2][:, t, :], bank(b, 2 + n % 2)[:, 0:384]).then_inc(p_copied, 1)

            def exps(h):
                for s in range(GROUP_SEQS):
                    act.wait_ge(maxed, GROUP_SEQS * h + s + 1)
                    for t in range(2 * s, 2 * s + 2):
                        ins = nc.scalar.activation(probs[h % 2][:, t, :], probs[h % 2][:, t, :], ACT.Exp, bias=neg_max[:, h % 2, t:t + 1],
                                                   accum_out=sums[:, h % 2, t:t + 1])
                    ins.then_inc(exped, 1)

            for i in range(AH + 1):
                if i < AH:
                    biased(i)
                    distances(i)
                if i >= 1:
                    exps(i - 1)

        @block.vector
        def _(dve):
            v = nc.vector
            norm.vector(dve, b.x[:], b.xn[:], (0, 1))
            for n in range(1, 2 * TILES, 2):
                dve.wait_ge(v_ready, n + 1)
                v.tensor_copy(v_sb[:, n // 2, half:], bank(b, 4 + n % 4)).then_inc(v_copied_v, 1)

            def keys(h):
                dve.wait_ge(k_ready, h + 1)
                if h >= 2:
                    dve.wait_ge(s_ready, GROUP_SEQS * (h - 1))
                v.tensor_copy(k_t[h % 2], bank(b, 1)).then_inc(k_copied, 1)

            def sums_and_maxima(h):
                dve.wait_ge(p_loaded, 16 * (h + 1))
                if h >= 2:
                    dve.wait_ge(turned, GROUP_SEQS * (h - 1))
                for s in range(GROUP_SEQS):
                    n = GROUP_SEQS * h + s
                    dve.wait_ge(s_ready, n + 1)
                    pair = probs[h % 2][:, 2 * s:2 * s + 2, :]
                    v.tensor_tensor(pair, bank(b, 4 + s).rearrange("p (t k) -> p t k", t=2),
                                    pos[h % 2][:, 2 * s:2 * s + 2, :], ALU.add).then_inc(summed, 1)
                    dve.wait_ge(summed, n + 1)
                    v.tensor_reduce(neg_max[:, h % 2, 2 * s:2 * s + 2], pair, AX, ALU.max, negate=True).then_inc(maxed, 1)

            def normalise(h):
                for s in range(GROUP_SEQS):
                    n = GROUP_SEQS * h + s
                    dve.wait_ge(exped, n + 1)
                    v.reciprocal(inv[:, h % 2, 2 * s:2 * s + 2], sums[:, h % 2, 2 * s:2 * s + 2]).then_inc(inverted, 1)
                    dve.wait_ge(inverted, n + 1)
                    for t in range(2 * s, 2 * s + 2):
                        ins = v.tensor_scalar(probs[h % 2][:, t, :], probs[h % 2][:, t, :], inv[:, h % 2, t:t + 1], None, ALU.mult)
                    ins.then_inc(normed, 1)

            def turned_out(h):
                for s in range(GROUP_SEQS):
                    n = GROUP_SEQS * h + s
                    dve.wait_ge(turned, n + 1)
                    if h >= 1:
                        dve.wait_ge(o_ready, h)
                    v.tensor_copy(probs_t[:, s], bank(b, 6).rearrange("p (c q) -> p c q", c=2)).then_inc(t_copied, 1)
                dve.wait_ge(o_ready, h + 1)
                if h >= 1:
                    dve.wait_ge(projected, h)
                v.tensor_copy(o_t, bank(b, 1)).then_inc(o_copied, 1)

            for i in range(AH + 2):
                if i < AH:
                    keys(i)
                if 1 <= i <= AH:
                    sums_and_maxima(i - 1)
                if i >= 2:
                    turned_out(i - 2)
                if 1 <= i <= AH:
                    normalise(i - 1)
            dve.wait_ge(projected, AH)
            v.scalar_tensor_tensor(out=b.x[:], in0=bank(b, 7), scalar=vec(b, ("b_out", 0)), in1=b.x[:], op0=ALU.add, op1=ALU.add)


def norm_block(nc, b, sem, src, dst):
    norm = Norm(nc, b, sem)
    with nc.Block() as block:
        @block.tensor
        def _(pe):
            norm.tensor(pe, src, (0, 1))

        @block.scalar
        def _(act):
            norm.scalar(act, (0, 1))

        @block.vector
        def _(dve):
            norm.vector(dve, src, dst, (0, 1))


def ffn_stage(nc, b, stage_sem):
    prefixed = lambda prefix: (lambda name: stage_sem(f"{prefix}_{name}"))
    norm_block(nc, b, prefixed("entry"), b.x[:], b.y[:])
    for l in range(DEPTH):
        ffn_layer(nc, b, prefixed(f"layer{l}"), l)


def ffn_layer(nc, b, sem, l):
    norm = Norm(nc, b, sem)
    shifted, qk_ready, v_ready = sem("shifted"), sem("qk_ready"), sem("v_ready")
    squared, v_copied, inv_norm = sem("qk_squared"), sem("v_copied"), sem("inverse_norms")
    summed, clipped, rooted, split, rotated = sem("squares_summed"), sem("sums_clipped"), sem("lengths_ready"), sem("rotary_parts_ready"), sem("rotated")
    zeroed, added, qk_turned, q_copied, k_copied = sem("weights_zeroed"), sem("parts_added"), sem("qk_turned"), sem("q_copied"), sem("k_copied")
    s_ready, maxed, exped, p_turned = sem("scores_ready"), sem("scores_maxed"), sem("scores_exped"), sem("probs_turned")
    p_copied_a, p_copied_v = sem("probs_copied_scalar"), sem("probs_copied_vector")
    o_ready, inverted, scaled, o_turned, ot_copied = sem("heads_ready"), sem("sums_inverted"), sem("heads_scaled"), sem("heads_turned"), sem("heads_copied")
    mixed, y_ready, hidden, gelu, gated, out = sem("mixed"), sem("y_ready"), sem("hidden_ready"), sem("gelu_ready"), sem("gated"), sem("down_ready")
    affine = sem("affine_done")
    carve = Carve(b)
    h_t = b.xn[:]
    h3 = h_t.rearrange("p (s n) -> p s n", s=GROUP_SEQS)
    y3 = b.y[:].rearrange("p (s n) -> p s n", s=GROUP_SEQS)
    two = lambda n: [carve(n) for _ in range(2)]
    q_t, k_t = (carve(4 * TOK).rearrange("p (j n) -> p j n", j=4) for _ in range(2))
    v_sb = carve(TILES * INNER).rearrange("p (t n) -> p t n", t=TILES)
    squares, cosine, sine = carve(2 * INNER), two(2 * INNER), two(2 * INNER)
    probs_near = [t.rearrange("p (h k) -> p h k", h=4) for t in two(4 * 128)]
    probs_wide = [t.rearrange("p (h k) -> p h k", h=4) for t in two(4 * SEQ)]
    lens = [t.rearrange("p (a n) -> p a n", a=4) for t in two(4 * 16)]
    neg_max, sums = (carve(TILES * LH).rearrange("p (t h) -> p t h", t=TILES) for _ in range(2))
    probs_t = [t.rearrange("p (h c q) -> p h c q", h=4, c=2) for t in cosine]
    heads = [t[:, 0:INNER] for t in sine]
    gelu_t = q_t
    gated_t = k_t
    heads_all = two(2 * TOK)
    o_t = [heads_all[j // 2][:, (j % 2) * TOK:(j % 2 + 1) * TOK] for j in range(4)]
    UNITS = 2 * TILES
    SLOT_HEADS = (0, 2, 1, 3)

    def span(t):
        return (0, 128) if t % 2 == 0 else (64, 192)

    def score_banks(u):
        return bank(b, 2 * (u % 2), 2).rearrange("p (h k) -> p h k", h=4)

    def prob_of(u):
        return (probs_wide if (u // 2) % 2 else probs_near)[u % 2]

    with nc.Block() as block:
        @block.tensor
        def _(pe):
            w = b.wqkv[:, l]
            pe.wait_ge(shifted, 1)

            def project(t):
                if t >= 2:
                    pe.wait_ge(split, t - 1)
                at = 2 * (t % 2)
                lhs = h_t[:, t * 128:(t + 1) * 128]
                nc.tensor.matmul(bank(b, at), lhs, w[:, 0:INNER], start=True, stop=True)
                nc.tensor.matmul(bank(b, at + 1), lhs, w[:, INNER:2 * INNER], start=True, stop=True).then_inc(qk_ready, 1)
                if t >= 1:
                    pe.wait_ge(v_copied, t)
                nc.tensor.matmul(bank(b, 4), lhs, w[:, 2 * INNER:], start=True, stop=True).then_inc(v_ready, 1)

            def turn(t):
                pe.wait_ge(rotated, t + 1)
                if t >= 1:
                    pe.wait_ge(q_copied, t)
                    pe.wait_ge(k_copied, t)
                for j in range(8):
                    ins = nc.tensor.transpose(bank(b, 5 + j // 4)[:, (j % 4) * 128:(j % 4 + 1) * 128],
                                              cosine[t % 2][:, j * 128:(j + 1) * 128], b.ident[:])
                ins.then_inc(qk_turned, 1)

            project(0)
            project(1)
            for t in range(TILES):
                if t + 2 < TILES:
                    project(t + 2)
                turn(t)

            def scores(u):
                t, half = u // 2, u % 2
                first, n = span(t)
                if u < 2:
                    pe.wait_ge(split, TILES)
                else:
                    pe.wait_ge(exped, u - 1)
                keys = (t // 2) * SEQ + first
                mask = b.mask_bf[:, 0:128] if t % 2 == 0 else b.mask_bf[:, 128:320]
                for k in range(2):
                    nc.tensor.matmul(score_banks(u)[:, 2 * k:2 * k + 2, first:first + n], b.ident_bf[:],
                                     mask.unsqueeze(1).broadcast_to([128, 2, n]), start=True, stop=False)
                for i in (0, 2, 1, 3):
                    head = 4 * half + SLOT_HEADS[i]
                    rows = slice(64 * (head % 2), 64 * (head % 2) + 64)
                    ins = nc.tensor.matmul(score_banks(u)[:, i, first:first + n], q_t[rows, head // 2, t * 128:(t + 1) * 128],
                                           k_t[rows, head // 2, keys:keys + n], start=False, stop=i % 2 == 1)
                ins.then_inc(s_ready, 1)

            def turn_probs(u):
                t = u // 2
                pe.wait_ge(exped, u + 1)
                if u >= 1:
                    pe.wait_ge(p_copied_a, u)
                    pe.wait_ge(p_copied_v, u)
                chunks = 1 + t % 2
                for i in range(4):
                    for c in range(chunks):
                        ins = nc.tensor.transpose(bank(b, 4 + i // 2)[:, (i % 2) * 256 + c * 128:(i % 2) * 256 + (c + 1) * 128],
                                                  prob_of(u)[:, i, c * 128:(c + 1) * 128], b.ident[:])
                ins.then_inc(p_turned, 1)

            def values(u):
                t, half = u // 2, u % 2
                pe.wait_ge(p_copied_a, u + 1)
                pe.wait_ge(p_copied_v, u + 1)
                if half == 0 and t >= 1:
                    pe.wait_ge(scaled, t)
                chunks = 1 + t % 2
                for i in range(4):
                    head = 4 * half + SLOT_HEADS[i]
                    for c in range(chunks):
                        ins = nc.tensor.matmul(bank(b, 6)[:, head * LD:(head + 1) * LD], probs_t[u % 2][:, i, c],
                                               v_sb[:, 2 * (t // 2) + c, head * LD:(head + 1) * LD], start=c == 0, stop=c == chunks - 1)
                ins.then_inc(o_ready, 1)

            def turn_heads(t):
                pe.wait_ge(scaled, t + 1)
                if t >= 1:
                    pe.wait_ge(ot_copied, t)
                for j in range(4):
                    ins = nc.tensor.transpose(bank(b, 7)[:, j * 128:(j + 1) * 128], heads[t % 2][:, j * 128:(j + 1) * 128], b.ident[:])
                ins.then_inc(o_turned, 1)

            pe.wait_ge(q_copied, TILES)
            pe.wait_ge(k_copied, TILES)
            pe.wait_ge(v_copied, TILES)
            scores(0)
            for u in range(UNITS + 1):
                if u + 1 < UNITS:
                    scores(u + 1)
                if u < UNITS:
                    turn_probs(u)
                if u % 2 == 1 and u >= 3:
                    turn_heads((u - 3) // 2)
                if u >= 1:
                    values(u - 1)
            turn_heads(TILES - 1)
            pe.wait_ge(ot_copied, TILES)
            for j in range(4):
                ins = nc.tensor.matmul(bank(b, 0), b.wo[:, l, j], o_t[j], start=j == 0, stop=j == 3)
            ins.then_inc(mixed, 1)
            pe.wait_ge(shifted, 2)
            norm.tensor(pe, h_t, (1, 2))
            pe.wait_ge(affine, 1)
            banks = [3, 4, 5, 6, 7, 0]
            for n, part in enumerate(("gate0", "value0", "gate1", "value1", "gate2", "value2")):
                at, rows = HC[n // 2]
                first = at + (HID if n % 2 == 0 else 0)
                nc.tensor.matmul(bank(b, banks[n])[0:rows], b.w1[:, l, first:first + rows], b.sq[:], start=True, stop=True).then_inc(hidden, 1)
            for c in range(3):
                rows = HC[c][1]
                pe.wait_ge(gated, c + 1)
                ins = nc.tensor.matmul(bank(b, 1), b.w2[0:rows, l, c], gated_t[0:rows, c], start=c == 0, stop=c == 2)
            ins.then_inc(out, 1)

        @block.scalar
        def _(act):
            for t in range(TILES + 1):
                if t < TILES:
                    act.wait_ge(qk_ready, t + 1)
                    if t >= 1:
                        act.wait_ge(summed, t)
                    nc.scalar.activation(squares, bank(b, 2 * (t % 2), 2), ACT.Square).then_inc(squared, 1)
                    act.wait_ge(v_ready, t + 1)
                    nc.scalar.copy(v_sb[:, t], bank(b, 4)).then_inc(v_copied, 1)
                    act.wait_ge(clipped, t + 1)
                    nc.scalar.activation(lens[t % 2][:, 1], lens[t % 2][:, 0], ACT.Sqrt).then_inc(rooted, 1)
                if t >= 1:
                    at = slice((t - 1) * 128, t * 128)
                    act.wait_ge(qk_turned, t)
                    nc.scalar.copy(q_t[:, :, at], bank(b, 5).rearrange("p (j n) -> p j n", j=4)).then_inc(q_copied, 1)

            def exps(u):
                t, half = u // 2, u % 2
                first, n = span(t)
                act.wait_ge(maxed, u + 1)
                if u >= 2:
                    act.wait_ge(p_turned, u - 1)
                for i in range(4):
                    head = 4 * half + SLOT_HEADS[i]
                    ins = nc.scalar.activation(prob_of(u)[:, i, first:first + n], score_banks(u)[:, i, first:first + n], ACT.Exp,
                                               bias=neg_max[:, t, 4 * half + i:4 * half + i + 1], accum_out=sums[:, t, head:head + 1])
                ins.then_inc(exped, 1)

            def copy_probs(u):
                act.wait_ge(p_turned, u + 1)
                if u >= 2:
                    act.wait_ge(o_ready, u - 1)
                c = 1 + (u // 2) % 2
                nc.scalar.copy(probs_t[u % 2][:, 0:2, 0:c], bank(b, 4).rearrange("p (h c q) -> p h c q", h=2, c=2)[:, :, 0:c]).then_inc(p_copied_a, 1)

            exps(0)
            for u in range(UNITS):
                if u + 1 < UNITS:
                    exps(u + 1)
                copy_probs(u)
            norm.scalar(act, (1, 2))
            for c in range(3):
                rows = HC[c][1]
                act.wait_ge(hidden, 2 * c + 1)
                nc.scalar.activation(gelu_t[0:rows, c], bank(b, [3, 5, 7][c])[0:rows], ACT.Gelu, bias=vec(b, (("b1_gate", c), l), rows)).then_inc(gelu, 1)

        @block.gpsimd
        def _(pool):
            pool.memset(probs_wide[0][:, :, 0:64], 0.0)
            pool.memset(probs_wide[1][:, :, 0:64], 0.0).then_inc(zeroed, 1)
            for t in range(TILES):
                pool.wait_ge(split, t + 1)
                pool.tensor_tensor(cosine[t % 2], cosine[t % 2], sine[t % 2], ALU.add).then_inc(added, 1)
                pool.wait_ge(added, t + 1)
                pool.wait_ge(inv_norm, t + 1)
                both = cosine[t % 2].rearrange("p (h d) -> p h d", d=LD)
                pool.tensor_tensor(both, both, lens[t % 2][:, 2].unsqueeze(2).broadcast_to([128, 16, LD]), ALU.mult).then_inc(rotated, 1)

        @block.vector
        def _(dve):
            v = nc.vector

            def shift(n):
                v.tensor_copy(h3[0:64], y3[0:64])
                v.memset(h3[64:128, :, 0:1], 0.0)
                v.tensor_copy(h3[64:128, :, 1:], y3[64:128, :, :SEQ - 1]).then_inc(shifted, 1)

            shift(1)
            for t in range(TILES + 1):
                if t < TILES:
                    at, s, n = 2 * (t % 2), t % 2, lens[t % 2]
                    dve.wait_ge(squared, t + 1)
                    v.tensor_reduce(n[:, 3], squares.rearrange("p (h d) -> p h d", d=LD), AX, ALU.add).then_inc(summed, 1)
                    dve.wait_ge(summed, t + 1)
                    v.tensor_scalar(n[:, 0], n[:, 3], 1e-24, None, ALU.max).then_inc(clipped, 1)
                    if t >= 2:
                        dve.wait_ge(qk_turned, t - 1)
                    for k in range(2):
                        qk = bank(b, at + k).rearrange("p (h d) -> p h d", d=LD)
                        c8, s8 = (x[t % 2][:, k * INNER:(k + 1) * INNER].rearrange("p (h d) -> p h d", d=LD) for x in (cosine, sine))
                        table = lambda n, x0, x1: b.rope_w[:, l, n, s, x0:x1].unsqueeze(1).broadcast_to([128, LH, x1 - x0])
                        v.tensor_tensor(c8, qk, table(2 * k, 0, LD), ALU.mult)
                        v.tensor_tensor(s8[:, :, 0:32], qk[:, :, 32:64], table(2 * k + 1, 0, 32), ALU.mult)
                        ins = v.tensor_tensor(s8[:, :, 32:64], qk[:, :, 0:32], table(2 * k + 1, 32, 64), ALU.mult)
                    ins.then_inc(split, 1)
                    dve.wait_ge(rooted, t + 1)
                    v.reciprocal(n[:, 2], n[:, 1]).then_inc(inv_norm, 1)
                if t >= 1:
                    dve.wait_ge(qk_turned, t)
                    v.tensor_copy(k_t[:, :, (t - 1) * 128:t * 128], bank(b, 6).rearrange("p (j n) -> p j n", j=4)).then_inc(k_copied, 1)

            def maxima(u):
                t, half = u // 2, u % 2
                first, n = span(t)
                dve.wait_ge(s_ready, u + 1)
                v.tensor_reduce(neg_max[:, t, 4 * half:4 * half + 4], score_banks(u)[:, :, first:first + n], AX, ALU.max, negate=True).then_inc(maxed, 1)

            def copy_probs(u):
                dve.wait_ge(p_turned, u + 1)
                if u >= 2:
                    dve.wait_ge(o_ready, u - 1)
                c = 1 + (u // 2) % 2
                v.tensor_copy(probs_t[u % 2][:, 2:4, 0:c], bank(b, 5).rearrange("p (h c q) -> p h c q", h=2, c=2)[:, :, 0:c]).then_inc(p_copied_v, 1)

            def scale_heads(t):
                dve.wait_ge(o_ready, 2 * t + 2)
                v.reciprocal(sums[:, t], sums[:, t]).then_inc(inverted, 1)
                dve.wait_ge(inverted, t + 1)
                if t >= 2:
                    dve.wait_ge(o_turned, t - 1)
                v.tensor_tensor(heads[t % 2].rearrange("p (h d) -> p h d", d=LD), bank(b, 6).rearrange("p (h d) -> p h d", d=LD),
                                sums[:, t].unsqueeze(2).broadcast_to([128, LH, LD]), ALU.mult).then_inc(scaled, 1)

            def copy_heads(t):
                dve.wait_ge(o_turned, t + 1)
                for k in range(2):
                    ins = v.tensor_copy(heads_all[k].rearrange("p (j n) -> p j n", j=2)[:, :, t * 128:(t + 1) * 128],
                                        bank(b, 7)[:, k * 256:(k + 1) * 256].rearrange("p (j n) -> p j n", j=2))
                ins.then_inc(ot_copied, 1)

            maxima(0)
            for u in range(UNITS + 1):
                if u + 1 < UNITS:
                    maxima(u + 1)
                if u < UNITS:
                    copy_probs(u)
                if u % 2 == 1 and u >= 3:
                    copy_heads((u - 3) // 2)
                if u % 2 == 0 and u >= 2:
                    scale_heads((u - 2) // 2)
            copy_heads(TILES - 1)
            dve.wait_ge(mixed, 1)
            v.tensor_tensor(b.y[:], b.y[:], bank(b, 0), ALU.add).then_inc(y_ready, 1)
            dve.wait_ge(y_ready, 1)
            shift(2)
            dve.wait_ge(shifted, 2)
            norm.vector(dve, h_t, b.xn[:], (1, 2))
            dve.wait_ge(norm.done, 1)
            v.tensor_scalar(b.sq[:], b.xn[:], vec(b, ("ln_g", l)), vec(b, ("ln_b", l)), ALU.mult, ALU.add).then_inc(affine, 1)
            for c in range(3):
                rows = HC[c][1]
                dve.wait_ge(hidden, 2 * c + 2)
                dve.wait_ge(gelu, c + 1)
                v.scalar_tensor_tensor(out=gated_t[0:rows, c], in0=bank(b, [4, 6, 0][c])[0:rows], scalar=vec(b, (("b1_value", c), l), rows),
                                       in1=gelu_t[0:rows, c], op0=ALU.add, op1=ALU.mult).then_inc(gated, 1)
            dve.wait_ge(out, 1)
            v.scalar_tensor_tensor(out=b.y[:], in0=bank(b, 1), scalar=vec(b, ("b2", l)), in1=b.y[:], op0=ALU.add, op1=ALU.add).then_inc(y_ready, 1)
            if l == DEPTH - 1:
                dve.wait_ge(y_ready, 2)
                v.scalar_tensor_tensor(out=b.x[:], in0=b.y[:], scalar=0.5, in1=b.x[:], op0=ALU.mult, op1=ALU.add)


def mamba_stage(nc, b, sem):
    norm = Norm(nc, b, sem)
    padded, projected, z_ready, gate_ready = sem("conv_padded"), sem("projected"), sem("conv_input_ready"), sem("gate_ready")
    conv_steps, conv_ready, x_ready, mixed = sem("conv_steps"), sem("conv_ready"), sem("conv_output_ready"), sem("dt_b_c_ready")
    dt_in, exped, plus_one, logged, rounding, pool_steps = (sem("dt_input_ready"), sem("softplus_exp"), sem("softplus_sum"),
                                                            sem("softplus_log"), sem("softplus_rounding"), sem("gpsimd_steps"))
    act_steps, dt_ready, u_ready, split_steps, split_ready = sem("scalar_steps"), sem("dt_ready"), sem("u_ready"), sem("split_steps"), sem("split_ready")
    spread, decay, driven, scanned, weighted, added = (sem("b_c_spread"), sem("decay_ready"), sem("drive_ready"),
                                                       sem("scanned"), sem("weighted_ready"), sem("state_added"))
    tail, y_ready, out = sem("tail_steps"), sem("gated_ready"), sem("out_ready")
    carve = Carve(b)
    W = 1 + SEQ + 2
    z = carve(2 * GROUP_SEQS * W).rearrange("p (c s w) -> p c s w", c=2, s=GROUP_SEQS)
    chunked = lambda: carve(2 * TOK).rearrange("p (c n) -> p c n", c=2)
    gate, conv, x_c, dt, u, e, w = (chunked() for _ in range(7))
    bc, rest = carve(TOK), carve(TOK)
    high, mid, parts = (carve(TOK, BF16) for _ in range(3))
    three = lambda: [carve(TOK) for _ in range(3)]
    decays, drives, hidden, weights_ = three(), three(), three(), three()
    N = 2 * STATES
    with nc.Block() as block:
        @block.tensor
        def _(pe):
            norm.tensor(pe, b.x[:], (0, 1))
            pe.wait_ge(norm.done, 1)
            for c in range(4):
                nc.tensor.matmul(bank(b, 2 + c), b.in_w[:, c * 128:(c + 1) * 128], b.xn[:], start=True, stop=True).then_inc(projected, 1)
            pe.wait_ge(x_ready, 2)
            for k in range(2):
                ins = nc.tensor.matmul(bank(b, 6)[0:2 * STATES], b.bc_w[:, k], x_c[:, k], start=k == 0, stop=k == 1)
            ins.then_inc(mixed, 1)
            for c in range(2):
                for k in range(2):
                    ins = nc.tensor.matmul(bank(b, 2 + c), b.dt_w[:, k, c * 128:(c + 1) * 128], x_c[:, k], start=k == 0, stop=k == 1)
                ins.then_inc(mixed, 1)
            pe.wait_ge(split_ready, 1)
            pe.wait_ge(dt_in, 1)

            def spread_state(n):
                if n >= 2:
                    pe.wait_ge(driven, 2 * (n - 1))
                nc.tensor.matmul(bank(b, n % 2), b.state_sel[:, n], parts[0:96], start=True, stop=True).then_inc(spread, 1)
                if n >= 2:
                    pe.wait_ge(weighted, 2 * (n - 1))
                nc.tensor.matmul(bank(b, 2 + n % 2), b.state_sel[:, STATES + n], parts[0:96], start=True, stop=True).then_inc(spread, 1)

            spread_state(0)
            spread_state(1)
            for n in range(STATES):
                for c in range(2):
                    i = 2 * n + c
                    pe.wait_ge(weighted, i + 1)
                    nc.tensor.matmul(bank(b, 4 + c), b.ident[:], weights_[i % 3], start=n == 0, stop=n == STATES - 1).then_inc(added, 1)
                if n + 2 < STATES:
                    spread_state(n + 2)
            for k in range(2):
                pe.wait_ge(y_ready, k + 1)
                ins = nc.tensor.matmul(bank(b, 6), b.ssm_out_w[:, k], conv[:, k], start=k == 0, stop=k == 1)
            ins.then_inc(out, 1)

        @block.scalar
        def _(act):
            norm.scalar(act, (0, 1))
            act.wait_ge(padded, 1)
            for c in range(2):
                act.wait_ge(projected, c + 1)
                nc.scalar.activation(z[:, c, :, 1:1 + SEQ], bank(b, 2 + c).rearrange("p (s n) -> p s n", s=GROUP_SEQS), ACT.Identity,
                                     bias=vec(b, ("in_b", c))).then_inc(z_ready, 1)
            for c in range(2):
                act.wait_ge(projected, c + 3)
                nc.scalar.activation(gate[:, c], bank(b, 4 + c), ACT.Silu, bias=vec(b, ("in_b", 2 + c))).then_inc(gate_ready, 1)
            for c in range(2):
                act.wait_ge(conv_ready, c + 1)
                nc.scalar.activation(x_c[:, c], conv[:, c], ACT.Silu, bias=vec(b, ("conv_b", c))).then_inc(x_ready, 1)
            steps = Chain(act, act_steps)
            act.wait_ge(dt_in, 1)
            steps.link(nc.scalar.activation(e, dt, ACT.Abs))
            nc.scalar.activation(e, e, ACT.Exp, scale=-1.0).then_inc(exped, 1)
            act.wait_ge(plus_one, 1)
            nc.scalar.activation(u, w, ACT.Ln).then_inc(logged, 1)
            act.wait_ge(dt_ready, 1)
            for i in range(N):
                n, c = i // 2, i % 2
                if i >= 3:
                    act.wait_ge(scanned, i - 2)
                nc.scalar.activation(decays[i % 3], dt[:, c], ACT.Exp, scale=b.A[:, c, n:n + 1]).then_inc(decay, 1)

        @block.gpsimd
        def _(pool):
            pool.memset(z[:, :, :, 0:1], 0.0)
            pool.memset(z[:, :, :, 1 + SEQ:], 0.0).then_inc(padded, 1)
            pool.wait_ge(exped, 1)
            pool.tensor_scalar(w, e, 1.0, None, ALU.add).then_inc(plus_one, 1)
            pool.wait_ge(plus_one, 1)
            pool.tensor_scalar(conv, w, -1.0, None, ALU.add).then_inc(pool_steps, 1)
            pool.wait_ge(pool_steps, 1)
            pool.tensor_tensor(e, e, conv, ALU.subtract).then_inc(rounding, 1)

        @block.vector
        def _(dve):
            v = nc.vector
            norm.vector(dve, b.x[:], b.xn[:], (0, 1))
            dve.wait_ge(padded, 1)
            steps = Chain(dve, conv_steps)
            for c in range(2):
                dve.wait_ge(z_ready, c + 1)
                dst = conv[:, c].rearrange("p (s n) -> p s n", s=GROUP_SEQS)
                tap = lambda k: vec(b, ("conv_w", 2 * k + c))
                steps.link(v.tensor_scalar(dst, z[:, c, :, 0:SEQ], tap(0), None, ALU.mult))
                for k in range(1, CONV):
                    ins = v.scalar_tensor_tensor(out=dst, in0=z[:, c, :, k:k + SEQ], scalar=tap(k), in1=dst, op0=ALU.mult, op1=ALU.add)
                    if k < CONV - 1:
                        steps.link(ins)
                    else:
                        ins.then_inc(conv_ready, 1)
            split = Chain(dve, split_steps)
            dve.wait_ge(mixed, 1)
            s = slice(0, 2 * STATES)
            split.link(v.tensor_scalar(bc[s], bank(b, 6)[s], vec(b, ("bc_b", 0), 2 * STATES), None, ALU.add))
            split.link(v.tensor_copy(high[s], bc[s]))
            split.link(v.tensor_tensor(rest[s], bc[s], high[s], ALU.subtract))
            split.link(v.tensor_copy(mid[s], rest[s]))
            split.link(v.tensor_tensor(bc[s], rest[s], mid[s], ALU.subtract))
            v.tensor_copy(parts[0:32], high[s])
            v.tensor_copy(parts[32:64], mid[s])
            v.tensor_copy(parts[64:96], bc[s]).then_inc(split_ready, 1)
            dve.wait_ge(mixed, 3)
            for c in range(2):
                ins = v.tensor_scalar(dt[:, c], bank(b, 2 + c), vec(b, ("dt_b", c)), None, ALU.add)
            ins.then_inc(dt_in, 1)
            dve.wait_ge(logged, 1)
            dve.wait_ge(rounding, 1)
            split.link(v.scalar_tensor_tensor(out=dt, in0=dt, scalar=0.0, in1=e, op0=ALU.max, op1=ALU.add))
            v.tensor_tensor(dt, dt, u, ALU.add).then_inc(dt_ready, 1)
            dve.wait_ge(dt_ready, 1)
            v.tensor_tensor(u, dt, x_c, ALU.mult).then_inc(u_ready, 1)
            dve.wait_ge(u_ready, 1)
            for i in range(N + 2):
                if i < N:
                    n, c = i // 2, i % 2
                    dve.wait_ge(spread, 2 * n + 1)
                    v.tensor_tensor(drives[i % 3], u[:, c], bank(b, n % 2), ALU.mult).then_inc(driven, 1)
                if 1 <= i <= N:
                    j = i - 1
                    dve.wait_ge(driven, j + 1)
                    dve.wait_ge(decay, j + 1)
                    for q in range(GROUP_SEQS):
                        at = slice(q * SEQ, (q + 1) * SEQ)
                        ins = v.tensor_tensor_scan(hidden[j % 3][:, at], decays[j % 3][:, at], drives[j % 3][:, at], 0.0, ALU.mult, ALU.add)
                    ins.then_inc(scanned, 1)
                if i >= 2:
                    j = i - 2
                    n = j // 2
                    dve.wait_ge(scanned, j + 1)
                    dve.wait_ge(spread, 2 * n + 2)
                    if j >= 3:
                        dve.wait_ge(added, j - 2)
                    v.tensor_tensor(weights_[j % 3], hidden[j % 3], bank(b, 2 + n % 2), ALU.mult).then_inc(weighted, 1)
            dve.wait_ge(added, N)
            dve.wait_ge(gate_ready, 2)
            end = Chain(dve, tail)
            for c in range(2):
                end.link(v.scalar_tensor_tensor(out=conv[:, c], in0=x_c[:, c], scalar=vec(b, ("Dp", c)), in1=bank(b, 4 + c), op0=ALU.mult, op1=ALU.add))
                v.tensor_tensor(conv[:, c], conv[:, c], gate[:, c], ALU.mult).then_inc(y_ready, 1)
            dve.wait_ge(out, 1)
            v.scalar_tensor_tensor(out=b.x[:], in0=bank(b, 6), scalar=vec(b, ("ssm_out_b", 0)), in1=b.x[:], op0=ALU.add, op1=ALU.add)



def build_program(nc, A, out):
    with ExitStack() as ctx:
        b = allocate(nc, ctx)
        weights(nc, b, A)
        src = A["L0_attn_q"].rearrange("b n d -> (b n) d")
        dst = out.rearrange("b n d -> (b n) d")
        with nc.Fori(0, GROUPS) as g:
            sems = Semaphores(nc)
            load_tokens(nc, b, sems.stage("load"), src, g)
            for n, stage in enumerate(STAGES):
                sem = sems.stage(f"{stage}{n}")
                if stage == "ffn":
                    ffn_stage(nc, b, sem)
                if stage == "attn":
                    attn_stage(nc, b, sem, A["scratch"])
                if stage == "moe":
                    moe_stage(nc, b, sem)
                if stage == "mamba":
                    mamba_stage(nc, b, sem)
                sems.clear()
            store_tokens(nc, b, sems.stage("store"), dst, g)
            sems.clear()


def constants():
    f = np.float32
    p = np.arange(128)
    fold64 = (p[:, None] % 64 == np.arange(64)[None, :]).astype(f)
    fold32 = (p[:, None] % 32 == np.arange(32)[None, :]).astype(f)
    near = p[:, None] - np.arange(128)[None, :]
    wide = p[:, None] + 64 - np.arange(192)[None, :]
    mask = np.concatenate([np.where((d >= 0) & (d <= WINDOW), 0.0, NEG) for d in (near, wide)], axis=1).astype(f)
    half = np.arange(0, LD, 2, dtype=f)
    inv_freq = (f(1.0) / f(10000.0) ** (half / f(LD))).astype(f)
    t = np.arange(SEQ, dtype=f)
    freqs = np.concatenate([t[:, None] * inv_freq[None, :]] * 2, axis=1).astype(f)
    base = ((half + f(0.4 * LD)) / f(1.4 * LD)).astype(f)
    power = ((t - SEQ // 2) / f(WINDOW // 2)).astype(f)
    scale = np.concatenate([base[None, :] ** power[:, None]] * 2, axis=1).astype(f)
    sign = np.where(np.arange(LD) < LD // 2, -1.0, 1.0).astype(f)
    cos, sin = np.cos(freqs), np.sin(freqs) * sign
    rope = np.stack([cos * scale * 8, sin * scale * 8, cos / scale, sin / scale]).astype(f)
    rope = rope.reshape(4, 2, 128, LD).transpose(2, 0, 1, 3)
    dist = np.arange(-SEQ + 1, SEQ, dtype=np.float64)
    n = REL // 6
    absd = np.abs(dist)[:, None]
    half_life = 2.0 ** np.linspace(3.0, math.log(SEQ) / math.log(2.0), n)
    feat_exp = np.exp(-math.log(2.0) / half_life[None, :] * absd)
    widths = 2.0 ** np.arange(1, n + 1) - 1.0
    feat_cm = (widths[None, :] > absd).astype(np.float64)
    stddev = SEQ / (2.0 * n)
    mean = np.linspace(SEQ / n, float(SEQ), n)[None, :]
    conc, rate = (mean / stddev) ** 2, mean / stddev ** 2
    log_d = np.log(np.maximum(absd, 1e-300))
    log_norm = np.array([[math.lgamma(c) for c in conc[0]]]) - conc * np.log(rate)
    probs = np.where(absd > 0, np.exp((conc - 1.0) * log_d - rate * absd - log_norm), 0.0) + 1e-8
    feat_gamma = probs / probs.max(axis=-1, keepdims=True)
    emb = np.concatenate([feat_exp, feat_cm, feat_gamma], axis=-1)
    emb = np.concatenate([emb, np.sign(dist)[:, None] * emb], axis=-1)
    pos = np.zeros((REL, 2 * SEQ), f)
    pos[:, 0:2 * SEQ - 1] = emb.T
    return {"const_ident": np.eye(128, dtype=f), "const_fold64": fold64, "const_fold32": fold32, "const_mask": mask,
            "const_rope": np.ascontiguousarray(rope), "const_pos": pos}


def kernel(**inputs):
    import concourse.bacc as bacc
    from concourse.bass_utils import run_bass_kernel_spmd as run

    nc = bacc.Bacc("TRN2", target_bir_lowering=False, num_devices=1)
    arrays, A = {}, {}
    for name, a in {**inputs, **constants()}.items():
        a = np.ascontiguousarray(a)
        arrays[f"in_{name}"] = a
        A[name] = nc.dram_tensor(f"in_{name}", a.shape, mybir.dt.from_np(a.dtype), kind="ExternalInput").ap()
    A["scratch"] = nc.dram_tensor("position_scores", (2, TILES, 128, 384), F32, kind="Internal").ap()
    out = nc.dram_tensor("out", (BATCH, SEQ, DIM), F32, kind="ExternalOutput").ap()
    build_program(nc, A, out)
    result = run(nc, [arrays], core_ids=[0])
    return result.results[0]["out"]
```

```python
import math
from contextlib import ExitStack

import numpy as np

import concourse.bass as bass
from concourse import mybir

F32 = mybir.dt.float32
BF16 = mybir.dt.bfloat16
ALU = mybir.AluOpType
ACT = mybir.ActivationFunctionType
AX = mybir.AxisListType.X

BATCH, SEQ, DIM = 16, 256, 128
GROUP_SEQS = 2
TOK = GROUP_SEQS * SEQ
TILES = TOK // 128
GROUPS = BATCH // GROUP_SEQS
STAGES = ("ffn", "attn", "ffn", "moe", "mamba", "moe")

DEPTH, LH, LD, WINDOW = 2, 8, 64, 64
INNER = LH * LD
HID = 341
HC = [(c * 128, min(128, HID - c * 128)) for c in range(3)]
AH, AD, REL = 8, 128, 192
EXPERTS, EF, TOP_K = 64, 64, 8
PAIRS = EXPERTS // 2
CH, STATES, CONV = 256, 16, 4
NEG = -3.0e38
LENGTH_SCALE = 2.0 ** 16


class Signal:

    def __init__(self, sem):
        self.sem, self.n = sem, 0

    def mark(self, instruction):
        instruction.then_inc(self.sem, 1)
        self.n += 1
        return self.n


class Chain(Signal):

    def __init__(self, engine, sem):
        super().__init__(sem)
        self.engine = engine

    def link(self, instruction):
        self.engine.wait_ge(self.sem, self.mark(instruction))


class Buffers:
    pass


def allocate(nc, ctx):
    b = Buffers()

    def sb(name, shape, dt=F32):
        t = ctx.enter_context(nc.sbuf_tensor(name, shape, dt))
        return t

    b.ident = sb("ident", [128, 128])
    b.ident_bf = sb("ident_bf", [128, 128], BF16)
    b.mean_w = sb("mean_w", [128, 128])
    b.eps = sb("eps", [128, 1])
    b.mask_bf = sb("mask_bf", [128, 320], BF16)
    b.fold64 = sb("fold64", [128, 64])
    b.pair_sel = sb("pair_sel", [128, PAIRS, 2, 64], BF16)
    b.fold32 = sb("fold32", [128, 32])
    b.fold32_bf = sb("fold32_bf", [128, 32], BF16)
    b.x = sb("x", [128, TOK])
    b.x_late = sb("x_late", [128, TOK])
    b.y = sb("y", [128, TOK])
    b.xn = sb("xn", [128, TOK])
    b.cent = sb("cent", [128, TOK])
    b.sq = sb("sq", [128, TOK])
    b.rstd = sb("rstd", [128, TOK])
    b.rows = sb("rows", [128, TILES, 128])
    b.wqkv = sb("wqkv", [128, DEPTH, 3 * INNER])
    b.wo = sb("wo", [128, DEPTH, 4, DIM])
    b.w1 = sb("w1", [128, DEPTH, 2 * HID])
    b.w2 = sb("w2", [128, DEPTH, 3, DIM])
    b.rope_w = sb("rope_w", [128, DEPTH, 4, 2, 64])
    b.wq = sb("wq", [128, AH * AD])
    b.wk = sb("wk", [128, AH * AD])
    b.wv = sb("wv", [128, AH * AD])
    b.w_out = sb("w_out", [128, AH, DIM])
    b.rel_k = sb("rel_k", [128, AH, 512])
    b.w_up = sb("w_up", [128, EXPERTS * EF])
    b.w_down = sb("w_down", [128, PAIRS, DIM])
    b.ws_up = sb("ws_up", [128, EF])
    b.ws_down = sb("ws_down", [EF, DIM])
    b.centroids_t = sb("centroids_t", [128, EXPERTS])
    b.expert_bias = sb("expert_bias", [128, EXPERTS])
    b.in_w = sb("in_w", [128, 2 * CH])
    b.A = sb("A", [128, 2, STATES])
    b.bc_w = sb("bc_w", [128, 2, 2 * STATES])
    b.dt_w = sb("dt_w", [128, 2, CH])
    b.ssm_out_w = sb("ssm_out_w", [128, 2, DIM])
    b.vec_cols = sb("vec_cols", [128, 128])
    b.vec_at = {}
    b.work = sb("work", [128, WORK])
    b.psum = ctx.enter_context(nc.psum_tensor("psum", [128, 8 * 512], F32))
    return b


WORK = 20960


def bank(b, i, n=1):
    return b.psum[:, i * 512:(i + n) * 512]


def vec(b, name, n=128):
    at = b.vec_at[name]
    return b.vec_cols[0:n, at:at + 1]


class Carve:

    def __init__(self, b):
        self.b, self.at = b, 0

    def __call__(self, columns, dt=F32):
        words = columns if dt == F32 else columns // 2
        piece = self.b.work[:, self.at:self.at + words]
        self.at += words
        assert self.at <= WORK, self.at
        return piece if dt == F32 else piece.bitcast(dt)


def weights(nc, b, A):
    with ExitStack() as ctx:
        sem = lambda name: ctx.enter_context(nc.semaphore(name))
        loaded, zeroed, made, copied, products = sem("weights_loaded"), sem("rows_zeroed"), sem("setup_made"), sem("setup_copied"), sem("setup_products")
        carve = Carve(b)
        pos = carve(2 * 512).rearrange("p (c n) -> p c n", c=2)
        w_rel = carve(2 * AH * AD).rearrange("p (c n) -> p c n", c=2)
        mask_f, vec_rows = carve(320), carve(128)
        rope = carve(4 * 2 * LD).rearrange("p (k s d) -> p k s d", k=4, s=2)
        centroids = carve(DIM)[0:EXPERTS]
        qk_scale = carve(2 * DEPTH * LD).rearrange("p (k l d) -> p k l d", k=2, l=DEPTH)
        vectors = []

        def vectors_of(name, source):
            for k in range(source.shape[0]):
                b.vec_at[name, k] = len(vectors)
                vectors.append(source[k:k + 1, :])

        rows_of = lambda ap: ap.rearrange("(c p) -> c p", p=128)
        row = lambda ap: ap.rearrange("(a p) -> a p", a=1)
        vectors_of("rel_embed", A["L0_attn_rel_embed_bias"].rearrange("a h b p -> (a b h) p"))
        vectors_of("rel_pos", A["L0_attn_rel_pos_bias"].rearrange("a h b p -> (a b h) p"))
        vectors_of("b_out", row(A["L0_attn_b_out"]))
        vectors_of("in_b", rows_of(A["L1_attn_in_b"]))
        vectors_of("conv_w", A["L1_attn_conv_w"].rearrange("k a (c p) -> (k a c) p", p=128))
        vectors_of("conv_b", rows_of(A["L1_attn_conv_b"]))
        vectors_of("Dp", rows_of(A["L1_attn_Dp"]))
        vectors_of("dt_b", rows_of(A["L1_attn_dt_b"]))
        vectors_of("ssm_out_b", row(A["L1_attn_out_b"]))
        vectors_of("ln_g", A["L0_ffn_ln_g"])
        vectors_of("ln_b", A["L0_ffn_ln_b"])
        vectors_of("b2", A["L0_ffn_b2"])
        for c, (at, n) in enumerate(HC):
            vectors_of(("b1_value", c), A["L0_ffn_b1"][:, at:at + n])
            vectors_of(("b1_gate", c), A["L0_ffn_b1"][:, HID + at:HID + at + n])
        bc_row = len(vectors)
        b.vec_at["bc_b", 0] = bc_row
        loads = [
            (b.ident[:], A["const_ident"]), (b.fold64[:], A["const_fold64"]), (b.fold32[:], A["const_fold32"]),
            (mask_f, A["const_mask"]), (rope, A["const_rope"]),
            (b.wqkv[:], A["L0_ffn_wqkv"].rearrange("l p n -> p l n")),
            (b.w1[:], A["L0_ffn_w1"].rearrange("l p n -> p l n")),
            (b.wq[:], A["L0_attn_w_qs"]), (b.wk[:], A["L0_attn_w_ks"]), (b.wv[:], A["L0_attn_w_vs"]),
            (b.w_out[:], A["L0_attn_w_out"].rearrange("(h p) n -> p h n", p=128)),
            (pos[:, 0, :], A["const_pos"][0:128, :]), (pos[0:64, 1, :], A["const_pos"][128:192, :]),
            (w_rel[:, 0, :], A["L0_attn_w_rel_pos_k"][0:128, :]), (w_rel[0:64, 1, :], A["L0_attn_w_rel_pos_k"][128:192, :]),
            (b.w_up[:].rearrange("p (e f) -> p e f", f=EF), A["L1_ffn_W_up"].rearrange("e p f -> p e f")),
            (b.w_down[:], A["L1_ffn_W_down"].rearrange("(q a) f n -> (a f) q n", a=2)),
            (b.ws_up[:], A["L1_ffn_Ws_up"]), (b.ws_down[:], A["L1_ffn_Ws_down"]),
            (centroids, A["L1_ffn_centroids"]),
            (b.expert_bias[:], A["L1_ffn_expert_biases"].partition_broadcast(128)),
            (b.in_w[:], A["L1_attn_in_w"]),
            (b.A[:], A["L1_attn_A"].rearrange("(c p) s -> p c s", p=128)),
            (b.bc_w[:, :, 0:STATES], A["L1_attn_B_w"].rearrange("(c p) s -> p c s", p=128)),
            (b.bc_w[:, :, STATES:], A["L1_attn_C_w"].rearrange("(c p) s -> p c s", p=128)),
            (b.dt_w[:], A["L1_attn_dt_w"].rearrange("(c p) n -> p c n", p=128)),
            (b.ssm_out_w[:], A["L1_attn_out_w"].rearrange("(c p) n -> p c n", p=128)),
        ]
        for l in range(DEPTH):
            loads += [
                (b.wo[:, l], A["L0_ffn_wo"][l].rearrange("(c p) n -> p c n", p=128)),
                (qk_scale[:, 0, l], A["L0_ffn_q_scale"][l].partition_broadcast(128)),
                (qk_scale[:, 1, l], A["L0_ffn_k_scale"][l].partition_broadcast(128)),
            ]
            for c, (at, n) in enumerate(HC):
                loads += [(b.w2[0:n, l, c], A["L0_ffn_w2"][l, at:at + n, :])]

        late = [(vec_rows[k:k + 1, 0:src.shape[1]], src) for k, src in enumerate(vectors)]
        late += [(vec_rows[bc_row:bc_row + 1, 0:STATES], row(A["L1_attn_B_b"])),
                 (vec_rows[bc_row:bc_row + 1, STATES:2 * STATES], row(A["L1_attn_C_b"]))]
        n_loads = len(loads) + len(late)

        with nc.Block() as block:
            @block.sync
            def _(sp):
                for dst, src in loads[0::2]:
                    sp.dma_start(dst, src).then_inc(loaded, 16)
                sp.wait_ge(zeroed, 1)
                for dst, src in late:
                    sp.dma_start(dst, src).then_inc(loaded, 16)

            @block.gpsimd
            def _(pool):
                pool.memset(vec_rows, 0.0).then_inc(zeroed, 1)
                pool.memset(b.mean_w[:], 1.0 / DIM)
                pool.memset(b.eps[:], 1e-5)

            @block.scalar
            def _(act):
                for dst, src in loads[1::2]:
                    act.dma_start(dst, src).then_inc(loaded, 16)
                for h in range(AH):
                    act.wait_ge(products, h + 2)
                    nc.scalar.copy(b.rel_k[:, h, :], bank(b, h)).then_inc(copied, 1)

            @block.tensor
            def _(pe):
                pe.wait_ge(loaded, 16 * n_loads)
                nc.tensor.transpose(bank(b, 0)[:, 0:EXPERTS], centroids, b.ident[0:EXPERTS, 0:EXPERTS])
                nc.tensor.transpose(bank(b, 1)[:, 0:128], vec_rows, b.ident[:]).then_inc(products, 1)
                pe.wait_ge(made, 1)
                for h in range(AH):
                    nc.tensor.matmul(bank(b, h), w_rel[:, 0, h * AD:(h + 1) * AD], pos[:, 0, :], start=True, stop=False)
                    nc.tensor.matmul(bank(b, h), w_rel[0:64, 1, h * AD:(h + 1) * AD], pos[0:64, 1, :],
                                     start=False, stop=True).then_inc(products, 1)

            @block.vector
            def _(dve):
                dve.wait_ge(loaded, 16 * n_loads)
                dve.wait_ge(products, 1)
                nc.vector.tensor_copy(b.centroids_t[:], bank(b, 0)[:, 0:EXPERTS])
                nc.vector.tensor_copy(b.vec_cols[:], bank(b, 1)[:, 0:128]).then_inc(made, 1)
                nc.vector.tensor_copy(b.ident_bf[:], b.ident[:])
                nc.vector.tensor_copy(b.mask_bf[:], mask_f)
                for p in range(PAIRS):
                    nc.vector.tensor_copy(b.pair_sel[:, p], b.fold64[:, 2 * p:2 * p + 2].unsqueeze(2).broadcast_to([128, 2, 64]))
                nc.vector.tensor_copy(b.fold32_bf[:], b.fold32[:])
                for l in range(DEPTH):
                    for qk in range(2):
                        sc = qk_scale[:, qk, l]
                        for s in range(2):
                            nc.vector.tensor_tensor(b.rope_w[:, l, 2 * qk, s], rope[:, 2 * qk, s], sc, ALU.mult)
                            nc.vector.tensor_tensor(b.rope_w[:, l, 2 * qk + 1, s, 0:32], rope[:, 2 * qk + 1, s, 0:32], sc[:, 32:64], ALU.mult)
                            nc.vector.tensor_tensor(b.rope_w[:, l, 2 * qk + 1, s, 32:64], rope[:, 2 * qk + 1, s, 32:64], sc[:, 0:32], ALU.mult)


class Norm:

    def __init__(self, nc, b, sem, buffers=None):
        self.nc, self.b = nc, b
        self.cent, self.sq, self.rstd = buffers or (b.cent[:], b.sq[:], b.rstd[:])
        self.mean, self.centred, self.squared, self.variance, self.logged, self.inverse, self.done = (
            sem(n) for n in ("mean_ready", "centred_ready", "squares_ready", "variance_ready",
                             "log_variance_ready", "rstd_ready", "norm_done"))

    def tensor(self, pe, src, banks, steps=(0, 1)):
        b = self.b
        if 0 in steps:
            self.nc.tensor.matmul(bank(b, banks[0]), b.mean_w[:], src, start=True, stop=True).then_inc(self.mean, 1)
        if 1 in steps:
            pe.wait_ge(self.squared, 1)
            self.nc.tensor.matmul(bank(b, banks[1]), b.mean_w[:], self.sq, start=True, stop=True).then_inc(self.variance, 1)

    def vector(self, dve, src, dst, banks, steps=(0, 1)):
        b, v = self.b, self.nc.vector
        if 0 in steps:
            dve.wait_ge(self.mean, 1)
            v.tensor_tensor(self.cent, src, bank(b, banks[0]), ALU.subtract).then_inc(self.centred, 1)
        if 1 in steps:
            dve.wait_ge(self.inverse, 1)
            v.tensor_tensor(dst, self.cent, self.rstd, ALU.mult).then_inc(self.done, 1)

    def scalar(self, act, banks, steps=(0, 1)):
        b, s = self.b, self.nc.scalar
        if 0 in steps:
            act.wait_ge(self.centred, 1)
            s.activation(self.sq, self.cent, ACT.Square).then_inc(self.squared, 1)
        if 1 in steps:
            act.wait_ge(self.variance, 1)
            s.activation(self.rstd, bank(b, banks[1]), ACT.Ln, bias=b.eps[:]).then_inc(self.logged, 1)
            act.wait_ge(self.logged, 1)
            s.activation(self.rstd, self.rstd, ACT.Exp, scale=-0.5).then_inc(self.inverse, 1)


class Semaphores:

    def __init__(self, nc):
        self.nc, self.ctx, self.held = nc, ExitStack(), []
        with nc.semaphore("lowest") as lowest:
            self.first = lowest.num

    def stage(self, prefix):
        def sem(name):
            self.held.append(self.ctx.enter_context(self.nc.semaphore(f"{prefix}_{name}", num=self.first + len(self.held))))
            return self.held[-1]
        return sem

    def clear(self):
        self.nc.all_engine_barrier(sems_to_clear=range(self.first, self.first + len(self.held)))
        self.ctx.close()
        self.held = []
        self.ctx = ExitStack()


def load_tokens(nc, b, sem, src, g):
    rows_in, turned, copied = sem("rows_in"), sem("rows_turned"), sem("x_copied")
    with nc.Block() as block:
        @block.sync
        def _(sp):
            sp.dma_start(b.rows[:], src[bass.ds(g * TOK, TOK), :].rearrange("(t p) d -> p t d", p=128)).then_inc(rows_in, 16)

        @block.tensor
        def _(pe):
            pe.wait_ge(rows_in, 16)
            for t in range(TILES):
                ins = nc.tensor.transpose(bank(b, 0)[:, t * 128:(t + 1) * 128], b.rows[:, t, :], b.ident[:])
            ins.then_inc(turned, 1)

        @block.vector
        def _(dve):
            dve.wait_ge(turned, 1)
            nc.vector.tensor_copy(b.x[:], bank(b, 0)).then_inc(copied, 1)


def store_tokens(nc, b, sem, dst, g):
    turned, copied, rows_out = sem("out_turned"), sem("out_copied"), sem("rows_out")
    with nc.Block() as block:
        @block.sync
        def _(sp):
            sp.wait_ge(copied, 1)
            sp.dma_start(dst[bass.ds(g * TOK, TOK), :].rearrange("(t p) d -> p t d", p=128), b.rows[:]).then_inc(rows_out, 16)
            sp.wait_ge(rows_out, 16)

        @block.tensor
        def _(pe):
            for t in range(TILES):
                ins = nc.tensor.transpose(bank(b, 0)[:, t * 128:(t + 1) * 128], b.x_late[:, t * 128:(t + 1) * 128], b.ident[:])
            ins.then_inc(turned, 1)

        @block.vector
        def _(dve):
            dve.wait_ge(turned, 1)
            nc.vector.tensor_copy(b.rows[:], bank(b, 0).rearrange("p (t d) -> p t d", t=TILES)).then_inc(copied, 1)


class Beside:

    def __init__(self, guest):
        self.guest = guest
        self.at = {"tensor": 0, "scalar": 0, "vector": 0, "gpsimd": 0}

    def steps(self, part, n):
        first = self.at[part]
        last = min(first + n, self.guest.STEPS) if self.guest else first
        self.at[part] = last
        return range(first, last)

    def tensor(self, pe, n=1):
        for k in self.steps("tensor", n):
            self.guest.tensor(pe, k)

    def scalar(self, act, n=1):
        for k in self.steps("scalar", n):
            self.guest.scalar(act, k)

    def vector(self, dve, n=1):
        for k in self.steps("vector", n):
            self.guest.vector(dve, k)

    def gpsimd(self, pool, n=1):
        for k in self.steps("gpsimd", n):
            self.guest.gpsimd(pool, k)

    def rest(self, nc):
        if self.guest is None:
            return
        n = self.guest.STEPS
        with nc.Block() as block:
            @block.tensor
            def _(pe):
                self.tensor(pe, n)

            @block.scalar
            def _(act):
                self.scalar(act, n)

            @block.vector
            def _(dve):
                self.vector(dve, n)

            @block.gpsimd
            def _(pool):
                self.gpsimd(pool, n)


class Experts:

    BANKS = (5, 6, 7)
    PRELUDE = 5
    STEPS = PRELUDE + PAIRS + 3

    def __init__(self, nc, b, sem, carve):
        self.nc, self.b = nc, b
        (self.affinity, self.negated, self.chain, self.split, self.turned, self.copied) = (
            sem(n) for n in ("affinity_ready", "affinity_exp", "routing_steps", "routing_split", "split_turned", "split_copied"))
        (self.up, self.spread, self.tanh, self.silu, self.gated, self.down, self.done) = (
            sem(n) for n in ("up_ready", "weights_spread", "tanh_ready", "silu_ready", "gated_ready", "down_ready", "experts_done"))
        self.high_mid, self.low = carve(TOK, BF16), carve(TOK, BF16)
        self.xn = carve(TOK)
        gates, self.tanh_h = carve(2 * TOK), carve(TOK)
        self.gate_h = [gates[:, 0:TOK], gates[:, TOK:]]
        self.biased, self.rest, self.chosen, self.prob = (
            gates[:, n * TILES * EXPERTS:(n + 1) * TILES * EXPERTS].rearrange("p (t e) -> p t e", t=TILES) for n in range(4))
        self.parts = self.tanh_h.bitcast(BF16).rearrange("p (t e) -> p t e", t=TILES)
        self.top = carve(TILES * TOP_K).rearrange("p (t e) -> p t e", t=TILES)
        self.total, self.inverse = carve(TILES), carve(TILES)
        self.norm = Norm(nc, b, sem, (self.gate_h[0], self.gate_h[1], self.tanh_h))
        self.aff = bank(b, self.BANKS[1])[:, 0:TILES * EXPERTS].rearrange("p (t e) -> p t e", t=TILES)
        self.norm_banks = self.BANKS[0:2]

    def tensor(self, pe, k):
        nc, b = self.nc, self.b
        UP, SPREAD, SUM = (bank(b, n) for n in self.BANKS)
        if k < 2:
            self.norm.tensor(pe, b.x_late[:], self.norm_banks, steps=(k,))
        elif k == 2:
            pe.wait_ge(self.norm.done, 1)
            for t in range(TILES):
                ins = nc.tensor.matmul(self.aff[:, t, :], self.xn[:, t * 128:(t + 1) * 128], b.centroids_t[:], start=True, stop=True)
            ins.then_inc(self.affinity, 1)
        elif k == 4:
            pe.wait_ge(self.split, 1)
            high_mid, low = UP.bitcast(BF16), SUM.bitcast(BF16)
            for t in range(TILES):
                nc.tensor.transpose(high_mid[:, t * 128:(t + 1) * 128], self.parts[:, t, 0:128], b.ident_bf[:])
            for t in range(TILES):
                ins = nc.tensor.transpose(low[:, t * 128:(t + 1) * 128], self.parts[:, t, 128:256], b.ident_bf[:])
            ins.then_inc(self.turned, 1)
        elif self.PRELUDE <= k <= self.PRELUDE + PAIRS + 1:
            p = k - self.PRELUDE
            if p == 0:
                pe.wait_ge(self.copied, 1)
            elif p <= PAIRS:
                pe.wait_ge(self.gated, p)
            else:
                pe.wait_ge(self.silu, PAIRS + 1)
            if p < PAIRS:
                sel = b.pair_sel[:, p]
                nc.tensor.matmul(SPREAD, sel, self.high_mid, start=True, stop=False)
                nc.tensor.matmul(SPREAD, sel[0:64], self.low[0:64], start=False, stop=True).then_inc(self.spread, 1)
                nc.tensor.matmul(UP, b.w_up[:, p * 128:(p + 1) * 128], self.xn, start=True, stop=True).then_inc(self.up, 1)
            elif p == PAIRS:
                nc.tensor.matmul(UP[0:EF], b.ws_up[:], self.xn, start=True, stop=True).then_inc(self.up, 1)
            if 1 <= p <= PAIRS:
                nc.tensor.matmul(SUM, b.w_down[:, p - 1], self.gate_h[(p - 1) % 2], start=p == 1, stop=False).then_inc(self.down, 1)
            elif p == PAIRS + 1:
                nc.tensor.matmul(SUM, b.ws_down[:], self.gate_h[PAIRS % 2][0:EF], start=False, stop=True).then_inc(self.down, 1)

    def scalar(self, act, k):
        nc, b = self.nc, self.b
        if k < 2:
            self.norm.scalar(act, self.norm_banks, steps=(k,))
        elif k == 2:
            act.wait_ge(self.chain, 1)
            nc.scalar.activation(self.prob[:], self.aff[:], ACT.Exp, scale=-1.0).then_inc(self.negated, 1)
        elif self.PRELUDE <= k <= self.PRELUDE + PAIRS:
            p = k - self.PRELUDE
            rows = 128 if p < PAIRS else EF
            act.wait_ge(self.up, p + 1)
            nc.scalar.activation(self.tanh_h[0:rows], bank(b, self.BANKS[0])[0:rows], ACT.Tanh, scale=0.5).then_inc(self.tanh, 1)

    def gpsimd(self, pool, k):
        pass

    def vector(self, dve, k):
        nc, b = self.nc, self.b
        v, E = nc.vector, EXPERTS
        spread_out = lambda ap: ap.unsqueeze(2).broadcast_to([128, TILES, E])
        if k < 2:
            self.norm.vector(dve, b.x_late[:], self.xn, self.norm_banks, steps=(k,))
        elif k == 2:
            self.steps = steps = Chain(dve, self.chain)
            dve.wait_ge(self.affinity, 1)
            steps.link(v.tensor_tensor(self.biased[:], self.aff[:], b.expert_bias[:].unsqueeze(1).broadcast_to([128, TILES, E]), ALU.add))
            for t in range(TILES):
                ins = v.max(self.top[:, t, :], self.biased[:, t, :])
            steps.link(ins)
            for t in range(TILES):
                ins = v.match_replace(self.rest[:, t, :], self.top[:, t, :], self.biased[:, t, :], NEG)
            steps.link(ins)
            steps.link(v.tensor_tensor(self.chosen[:], self.rest[:], self.biased[:], ALU.not_equal))
        elif k == 3:
            steps, prob, parts = self.steps, self.prob, self.parts
            dve.wait_ge(self.negated, 1)
            steps.link(v.tensor_scalar(prob[:], prob[:], 1.0, None, ALU.add))
            steps.link(v.reciprocal(prob[:], prob[:]))
            steps.link(v.tensor_tensor(prob[:], prob[:], self.chosen[:], ALU.mult))
            steps.link(v.tensor_reduce(self.total, prob[:], AX, ALU.add))
            steps.link(v.tensor_scalar(self.total, self.total, 1e-8, None, ALU.add))
            steps.link(v.reciprocal(self.inverse, self.total))
            steps.link(v.tensor_tensor(prob[:], prob[:], spread_out(self.inverse), ALU.mult))
            steps.link(v.tensor_copy(parts[:, :, 0:E], prob[:]))
            steps.link(v.tensor_tensor(prob[:], prob[:], parts[:, :, 0:E], ALU.subtract))
            steps.link(v.tensor_copy(parts[:, :, E:2 * E], prob[:]))
            steps.link(v.tensor_tensor(prob[:], prob[:], parts[:, :, E:2 * E], ALU.subtract))
            v.tensor_copy(parts[:, :, 3 * E:4 * E], prob[:])
            v.tensor_copy(parts[:, :, 2 * E:3 * E], prob[:]).then_inc(self.split, 1)
        elif k == 4:
            dve.wait_ge(self.turned, 1)
            v.tensor_copy(self.high_mid, bank(b, self.BANKS[0]).bitcast(BF16)[:, 0:TOK])
            v.tensor_copy(self.low, bank(b, self.BANKS[2]).bitcast(BF16)[:, 0:TOK]).then_inc(self.copied, 1)
        elif k <= self.PRELUDE + PAIRS:
            p = k - self.PRELUDE
            rows = 128 if p < PAIRS else EF
            h = self.gate_h[p % 2][0:rows]
            dve.wait_ge(self.tanh, p + 1)
            if p >= 2:
                dve.wait_ge(self.down, p - 1)
            v.scalar_tensor_tensor(out=h, in0=self.tanh_h[0:rows], scalar=1.0, in1=bank(b, self.BANKS[0])[0:rows],
                                   op0=ALU.add, op1=ALU.mult).then_inc(self.silu, 1)
            if p < PAIRS:
                dve.wait_ge(self.silu, p + 1)
                dve.wait_ge(self.spread, p + 1)
                v.tensor_tensor(h, h, bank(b, self.BANKS[1]), ALU.mult).then_inc(self.gated, 1)
        elif k == self.STEPS - 1:
            dve.wait_ge(self.down, PAIRS + 1)
            v.scalar_tensor_tensor(out=b.x_late[:], in0=bank(b, self.BANKS[2]), scalar=0.25, in1=b.x_late[:],
                                   op0=ALU.mult, op1=ALU.add).then_inc(self.done, 1)


def first_and_third(nc, b, sems, name, early, late):
    carve = Carve(b)
    beside = Beside(Experts(nc, b, sems.stage(f"{name}_experts"), carve) if late else None)
    if early:
        ffn_stage(nc, b, sems.stage(f"{name}_ffn"), beside, carve.at)
    beside.rest(nc)
    sems.clear()


def second(nc, b, sems, scratch, early, late):
    carve = Carve(b)
    beside = Beside(StateSpace(nc, b, sems.stage("ssm"), carve) if late else None)
    if early:
        attn_stage(nc, b, sems.stage("attn"), scratch, beside, carve.at)
    beside.rest(nc)
    sems.clear()


class StateSpace:

    BANKS = (4, 5, 6, 7)
    PRELUDE = 6
    SCANS = 2 * STATES
    STEPS = PRELUDE + SCANS + 3 + 2

    def __init__(self, nc, b, sem, carve):
        self.nc, self.b = nc, b
        self.padded, self.projected, self.z_ready, self.gate_ready = sem("conv_padded"), sem("projected"), sem("conv_input_ready"), sem("gate_ready")
        self.conv_steps, self.conv_ready, self.x_ready, self.mixed = sem("conv_steps"), sem("conv_ready"), sem("conv_output_ready"), sem("dt_b_c_ready")
        self.dt_in, self.exped, self.plus_one, self.logged, self.rounding, self.pool_steps = (
            sem("dt_input_ready"), sem("softplus_exp"), sem("softplus_sum"), sem("softplus_log"), sem("softplus_rounding"), sem("gpsimd_steps"))
        self.act_steps, self.dt_ready, self.u_ready, self.split_steps, self.split_ready = (
            sem("scalar_steps"), sem("dt_ready"), sem("u_ready"), sem("split_steps"), sem("split_ready"))
        self.spread_b, self.spread_c, self.decay, self.driven, self.scanned, self.weighted, self.added = (
            sem("b_spread"), sem("c_spread"), sem("decay_ready"), sem("drive_ready"), sem("scanned"), sem("weighted_ready"), sem("state_added"))
        self.softplus_steps, self.gate_steps, self.y_ready, self.out = sem("softplus_steps"), sem("gate_steps"), sem("gated_ready"), sem("out_ready")
        chunked = lambda: carve(2 * TOK).rearrange("p (c n) -> p c n", c=2)
        self.gate, self.x_c, self.dt, self.u = (chunked() for _ in range(4))
        self.parts = carve(TOK, BF16)
        width = 1 + SEQ + 2
        early = carve(2 * GROUP_SEQS * width + 4 * TOK)
        at = 2 * GROUP_SEQS * width
        self.z = early[:, 0:at].rearrange("p (c s w) -> p c s w", c=2, s=GROUP_SEQS)
        self.conv, self.e = (early[:, at + n * 2 * TOK:at + (n + 1) * 2 * TOK].rearrange("p (c n) -> p c n", c=2) for n in range(2))
        self.w = early[:, 0:2 * TOK].rearrange("p (c n) -> p c n", c=2)
        self.bc, self.rest = self.u[:, 0], self.u[:, 1]
        self.high, self.mid = (self.e[:, 0, n * 256:(n + 1) * 256].bitcast(BF16) for n in range(2))
        self.xn = self.e[:, 1]
        self.norm = Norm(nc, b, sem, (self.conv[:, 0], self.conv[:, 1], self.e[:, 0]))
        self.decays = [early[:, n * TOK:(n + 1) * TOK] for n in range(2)]
        self.states = [early[:, n * TOK:(n + 1) * TOK] for n in range(2, 6)]

    def tensor(self, pe, k):
        nc, b = self.nc, self.b
        B, C = (bank(b, n) for n in self.BANKS[0:2])
        j = k - self.PRELUDE
        if k < 2:
            self.norm.tensor(pe, b.x_late[:], self.BANKS[0:2], steps=(k,))
        elif k == 2:
            pe.wait_ge(self.norm.done, 1)
            for c in range(4):
                nc.tensor.matmul(bank(b, self.BANKS[c]), b.in_w[:, c * 128:(c + 1) * 128], self.xn, start=True, stop=True).then_inc(self.projected, 1)
        elif k == 4:
            pe.wait_ge(self.x_ready, 2)
            pe.wait_ge(self.gate_ready, 2)
            for i in range(2):
                ins = nc.tensor.matmul(B[0:2 * STATES], b.bc_w[:, i], self.x_c[:, i], start=i == 0, stop=i == 1)
            ins.then_inc(self.mixed, 1)
            for c in range(2):
                for i in range(2):
                    ins = nc.tensor.matmul(bank(b, self.BANKS[2 + c]), b.dt_w[:, i, c * 128:(c + 1) * 128], self.x_c[:, i], start=i == 0, stop=i == 1)
                ins.then_inc(self.mixed, 1)
        elif 0 <= j <= self.SCANS + 2:
            if j == 0:
                pe.wait_ge(self.split_ready, 1)
                pe.wait_ge(self.dt_in, 1)
            if j % 2 == 0 and j < self.SCANS:
                if j >= 2:
                    pe.wait_ge(self.driven, j)
                n = j // 2
                nc.tensor.matmul(B, b.fold32_bf[0:96, n:n + 1].broadcast_to([96, 128]), self.parts[0:96], start=True, stop=True).then_inc(self.spread_b, 1)
            if j % 2 == 0 and 2 <= j <= self.SCANS:
                if j >= 4:
                    pe.wait_ge(self.weighted, j - 2)
                n = STATES + (j - 2) // 2
                nc.tensor.matmul(C, b.fold32_bf[0:96, n:n + 1].broadcast_to([96, 128]), self.parts[0:96], start=True, stop=True).then_inc(self.spread_c, 1)
            if j >= 3:
                i = j - 3
                pe.wait_ge(self.weighted, i + 1)
                nc.tensor.matmul(bank(b, self.BANKS[2 + i % 2]), b.ident[:], self.states[i % 4], start=i < 2, stop=i >= self.SCANS - 2).then_inc(self.added, 1)
        elif k == self.STEPS - 2:
            for i in range(2):
                pe.wait_ge(self.y_ready, i + 1)
                ins = nc.tensor.matmul(B, b.ssm_out_w[:, i], self.conv[:, i], start=i == 0, stop=i == 1)
            ins.then_inc(self.out, 1)

    def scalar(self, act, k):
        nc, b = self.nc, self.b
        j = k - self.PRELUDE
        if k < 2:
            self.norm.scalar(act, self.BANKS[0:2], steps=(k,))
        elif k == 2:
            act.wait_ge(self.padded, 1)
            for c in range(2):
                act.wait_ge(self.projected, c + 1)
                nc.scalar.activation(self.z[:, c, :, 1:1 + SEQ], bank(b, self.BANKS[c]).rearrange("p (s n) -> p s n", s=GROUP_SEQS), ACT.Identity,
                                     bias=vec(b, ("in_b", c))).then_inc(self.z_ready, 1)
            for c in range(2):
                act.wait_ge(self.projected, c + 3)
                nc.scalar.activation(self.gate[:, c], bank(b, self.BANKS[2 + c]), ACT.Silu, bias=vec(b, ("in_b", 2 + c))).then_inc(self.gate_ready, 1)
        elif k == 3:
            for c in range(2):
                act.wait_ge(self.conv_ready, c + 1)
                nc.scalar.activation(self.x_c[:, c], self.conv[:, c], ACT.Silu, bias=vec(b, ("conv_b", c))).then_inc(self.x_ready, 1)
        elif k == 4:
            steps = Chain(act, self.act_steps)
            act.wait_ge(self.dt_in, 1)
            steps.link(nc.scalar.activation(self.e, self.dt, ACT.Abs))
            nc.scalar.activation(self.e, self.e, ACT.Exp, scale=-1.0).then_inc(self.exped, 1)
        elif k == 5:
            act.wait_ge(self.plus_one, 1)
            act.wait_ge(self.split_ready, 1)
            nc.scalar.activation(self.u, self.w, ACT.Ln).then_inc(self.logged, 1)
        elif 0 <= j < self.SCANS:
            if j == 0:
                act.wait_ge(self.dt_ready, 1)
            if j >= 2:
                act.wait_ge(self.scanned, j - 1)
            nc.scalar.activation(self.decays[j % 2], self.dt[:, j % 2], ACT.Exp, scale=b.A[:, j % 2, j // 2:j // 2 + 1]).then_inc(self.decay, 1)

    def gpsimd(self, pool, k):
        if k == 0:
            pool.memset(self.z[:, :, :, 0:1], 0.0)
            pool.memset(self.z[:, :, :, 1 + SEQ:], 0.0).then_inc(self.padded, 1)
        elif k == 4:
            pool.wait_ge(self.exped, 1)
            pool.tensor_scalar(self.w, self.e, 1.0, None, ALU.add).then_inc(self.plus_one, 1)
        elif k == 5:
            pool.wait_ge(self.plus_one, 1)
            pool.tensor_scalar(self.conv, self.w, -1.0, None, ALU.add).then_inc(self.pool_steps, 1)
            pool.wait_ge(self.pool_steps, 1)
            pool.tensor_tensor(self.e, self.e, self.conv, ALU.subtract).then_inc(self.rounding, 1)

    def vector(self, dve, k):
        nc, b = self.nc, self.b
        v = nc.vector
        j = k - self.PRELUDE
        if k < 2:
            self.norm.vector(dve, b.x_late[:], self.xn, self.BANKS[0:2], steps=(k,))
        elif k == 3:
            steps = Chain(dve, self.conv_steps)
            for c in range(2):
                dve.wait_ge(self.z_ready, c + 1)
                dst = self.conv[:, c].rearrange("p (s n) -> p s n", s=GROUP_SEQS)
                tap = lambda n: vec(b, ("conv_w", 2 * n + c))
                steps.link(v.tensor_scalar(dst, self.z[:, c, :, 0:SEQ], tap(0), None, ALU.mult))
                for n in range(1, CONV):
                    ins = v.scalar_tensor_tensor(out=dst, in0=self.z[:, c, :, n:n + SEQ], scalar=tap(n), in1=dst, op0=ALU.mult, op1=ALU.add)
                    if n < CONV - 1:
                        steps.link(ins)
                    else:
                        ins.then_inc(self.conv_ready, 1)
        elif k == 4:
            bc, rest, high, mid, parts = self.bc, self.rest, self.high, self.mid, self.parts
            split = Chain(dve, self.split_steps)
            dve.wait_ge(self.mixed, 1)
            s = slice(0, 2 * STATES)
            split.link(v.tensor_scalar(bc[s], bank(b, self.BANKS[0])[s], vec(b, ("bc_b", 0), 2 * STATES), None, ALU.add))
            split.link(v.tensor_copy(high[s], bc[s]))
            split.link(v.tensor_tensor(rest[s], bc[s], high[s], ALU.subtract))
            split.link(v.tensor_copy(mid[s], rest[s]))
            split.link(v.tensor_tensor(bc[s], rest[s], mid[s], ALU.subtract))
            v.tensor_copy(parts[0:32], high[s])
            v.tensor_copy(parts[32:64], mid[s])
            v.tensor_copy(parts[64:96], bc[s]).then_inc(self.split_ready, 1)
            dve.wait_ge(self.mixed, 3)
            for c in range(2):
                ins = v.tensor_scalar(self.dt[:, c], bank(b, self.BANKS[2 + c]), vec(b, ("dt_b", c)), None, ALU.add)
            ins.then_inc(self.dt_in, 1)
        elif k == 5:
            dve.wait_ge(self.logged, 1)
            dve.wait_ge(self.rounding, 1)
            softplus = Chain(dve, self.softplus_steps)
            softplus.link(v.scalar_tensor_tensor(out=self.dt, in0=self.dt, scalar=0.0, in1=self.e, op0=ALU.max, op1=ALU.add))
            v.tensor_tensor(self.dt, self.dt, self.u, ALU.add).then_inc(self.dt_ready, 1)
            dve.wait_ge(self.dt_ready, 1)
            v.tensor_tensor(self.u, self.dt, self.x_c, ALU.mult).then_inc(self.u_ready, 1)
        elif 0 <= j <= self.SCANS + 1:
            if j == 0:
                dve.wait_ge(self.u_ready, 1)
            if j < self.SCANS:
                dve.wait_ge(self.spread_b, j // 2 + 1)
                if j >= 4:
                    dve.wait_ge(self.added, j - 3)
                v.tensor_tensor(self.states[j % 4], self.u[:, j % 2], bank(b, self.BANKS[0]), ALU.mult).then_inc(self.driven, 1)
            if 1 <= j <= self.SCANS:
                i = j - 1
                dve.wait_ge(self.driven, i + 1)
                dve.wait_ge(self.decay, i + 1)
                for q in range(GROUP_SEQS):
                    at = self.states[i % 4][:, q * SEQ:(q + 1) * SEQ]
                    ins = v.tensor_tensor_scan(at, self.decays[i % 2][:, q * SEQ:(q + 1) * SEQ], at, 0.0, ALU.mult, ALU.add)
                ins.then_inc(self.scanned, 1)
            if j >= 2:
                i = j - 2
                dve.wait_ge(self.scanned, i + 1)
                dve.wait_ge(self.spread_c, i // 2 + 1)
                v.tensor_tensor(self.states[i % 4], self.states[i % 4], bank(b, self.BANKS[1]), ALU.mult).then_inc(self.weighted, 1)
        elif k == self.STEPS - 2:
            dve.wait_ge(self.added, self.SCANS)
            dve.wait_ge(self.gate_ready, 2)
            gated = Chain(dve, self.gate_steps)
            for c in range(2):
                gated.link(v.scalar_tensor_tensor(out=self.conv[:, c], in0=self.x_c[:, c], scalar=vec(b, ("Dp", c)), in1=bank(b, self.BANKS[2 + c]),
                                                  op0=ALU.mult, op1=ALU.add))
                v.tensor_tensor(self.conv[:, c], self.conv[:, c], self.gate[:, c], ALU.mult).then_inc(self.y_ready, 1)
        elif k == self.STEPS - 1:
            dve.wait_ge(self.out, 1)
            v.scalar_tensor_tensor(out=b.x_late[:], in0=bank(b, self.BANKS[0]), scalar=vec(b, ("ssm_out_b", 0)), in1=b.x_late[:], op0=ALU.add, op1=ALU.add)


def attn_stage(nc, b, sem, scratch, beside, space):
    norm = Norm(nc, b, sem)
    v_ready, v_copied_a, v_copied_v = sem("v_ready"), sem("v_copied_scalar"), sem("v_copied_vector")
    q_ready, k_ready, q_biased, k_copied = sem("q_ready"), sem("k_ready"), sem("q_biased"), sem("k_copied")
    p_ready, p_copied, p_stored, p_loaded = sem("distance_scores_ready"), sem("distance_scores_copied"), sem("distance_scores_stored"), sem("position_scores_loaded")
    s_ready, summed, maxed, exped, inverted, normed = (sem("scores_ready"), sem("scores_summed"), sem("scores_maxed"), sem("scores_exped"),
                                                       sem("sums_inverted"), sem("probs_normed"))
    turned, t_copied, o_ready, o_copied, projected = sem("probs_turned"), sem("probs_copied"), sem("heads_ready"), sem("heads_copied"), sem("projected")
    carve = Carve(b)
    carve.at = space
    v_sb = carve(TILES * AH * AD).rearrange("p (t n) -> p t n", t=TILES)
    two = lambda n: [carve(n) for _ in range(2)]
    q_e, q_p, k_t = two(TOK), carve(TOK), two(TOK)
    pos = carve(TILES * SEQ).rearrange("p (t k) -> p t k", t=TILES)
    probs = [t.rearrange("p (t k) -> p t k", t=TILES) for t in two(TILES * SEQ)]
    dist = carve(TILES * 384).rearrange("p (t k) -> p t k", t=TILES)
    probs_t = carve(GROUP_SEQS * 2 * SEQ).rearrange("p (s c q) -> p s c q", s=GROUP_SEQS, c=2)
    o_t = carve(TOK)
    neg_max, sums, inv = (carve(2 * TILES).rearrange("p (a t) -> p a t", a=2) for _ in range(3))
    half = AH * AD // 2
    DIST_BANKS, SCORE_BANKS, TURN_BANKS = (1, 0, 2, 1), (0, 2), (1, 0)
    ROUNDS = AH + 3

    def shifted(slot):
        return bass.AP(tensor=scratch.tensor, offset=slot * TILES * 128 * 384 + 127,
                       ap=[[383, 128], [128 * 384, TILES], [1, SEQ]])

    with nc.Block() as block:
        @block.tensor
        def _(pe):
            norm.tensor(pe, b.x[:], (0, 1), steps=(0,))
            beside.tensor(pe)
            norm.tensor(pe, b.x[:], (0, 1), steps=(1,))
            beside.tensor(pe)
            pe.wait_ge(norm.done, 1)
            for n in range(2 * TILES):
                if n == 4:
                    beside.tensor(pe)
                if n >= 4:
                    pe.wait_ge(v_copied_v if n % 2 else v_copied_a, (n - 4) // 2 + 1)
                t, side = n // 2, n % 2
                nc.tensor.matmul(bank(b, n % 4), b.xn[:, t * 128:(t + 1) * 128], b.wv[:, side * half:(side + 1) * half],
                                 start=True, stop=True).then_inc(v_ready, 1)
            beside.tensor(pe)
            pe.wait_ge(v_copied_a, TILES)
            pe.wait_ge(v_copied_v, TILES)

            def heads(h):
                pe.wait_ge(t_copied, GROUP_SEQS * (h + 1))
                for s in range(GROUP_SEQS):
                    for c in range(2):
                        ins = nc.tensor.matmul(bank(b, 1)[:, s * SEQ:(s + 1) * SEQ], v_sb[:, 2 * s + c, h * AD:(h + 1) * AD],
                                               probs_t[:, s, c], start=c == 0, stop=c == 1)
                ins.then_inc(o_ready, 1)

            def project(h):
                pe.wait_ge(o_copied, h + 1)
                nc.tensor.matmul(bank(b, 3), b.w_out[:, h], o_t, start=h == 0, stop=h == AH - 1).then_inc(projected, 1)

            def queries_keys(h):
                w = slice(h * AD, (h + 1) * AD)
                if h >= 1:
                    pe.wait_ge(p_copied, TILES * h)
                nc.tensor.matmul(bank(b, 0), b.wq[:, w], b.xn[:], start=True, stop=True).then_inc(q_ready, 1)
                nc.tensor.matmul(bank(b, 2), b.wk[:, w], b.xn[:], start=True, stop=True).then_inc(k_ready, 1)

            def distances(h):
                pe.wait_ge(q_biased, h + 1)
                for t in range(TILES):
                    if t == 2:
                        pe.wait_ge(k_copied, h + 1)
                    if t == 3:
                        pe.wait_ge(p_copied, TILES * h + 1)
                    first = 128 if t % 2 == 0 else 0
                    nc.tensor.matmul(bank(b, DIST_BANKS[t])[:, 0:384], q_p[:, t * 128:(t + 1) * 128],
                                     b.rel_k[:, h, first:first + 384], start=True, stop=True).then_inc(p_ready, 1)

            def scores(h):
                for s in range(GROUP_SEQS):
                    if h + 1 < AH:
                        pe.wait_ge(p_copied, TILES * (h + 1) + 2 + s)
                    for t in range(2):
                        at = (2 * s + t) * 128
                        ins = nc.tensor.matmul(bank(b, SCORE_BANKS[s])[:, t * SEQ:(t + 1) * SEQ], q_e[h % 2][:, at:at + 128],
                                               k_t[h % 2][:, s * SEQ:(s + 1) * SEQ], start=True, stop=True)
                    ins.then_inc(s_ready, 1)

            def turn(h, s):
                if s == 0 and h + 2 < AH:
                    pe.wait_ge(p_copied, TILES * (h + 3))
                if s == 1 and h + 1 < AH:
                    pe.wait_ge(summed, GROUP_SEQS * (h + 1) + 1)
                pe.wait_ge(normed, GROUP_SEQS * h + s + 1)
                for t in range(2):
                    for c in range(2):
                        ins = nc.tensor.transpose(bank(b, TURN_BANKS[s])[:, c * SEQ + t * 128:c * SEQ + (t + 1) * 128],
                                                  probs[h % 2][:, 2 * s + t, c * 128:(c + 1) * 128], b.ident[:])
                ins.then_inc(turned, 1)

            for i in range(ROUNDS):
                if 2 <= i <= AH + 1:
                    pe.wait_ge(summed, GROUP_SEQS * (i - 1))
                if i >= 3:
                    heads(i - 3)
                if i < AH:
                    queries_keys(i)
                beside.tensor(pe)
                if i >= 3:
                    project(i - 3)
                if i < AH:
                    distances(i)
                beside.tensor(pe)
                if 1 <= i <= AH:
                    scores(i - 1)
                if 2 <= i <= AH + 1:
                    turn(i - 2, 0)
                beside.tensor(pe)
                if 2 <= i <= AH + 1:
                    turn(i - 2, 1)
                beside.tensor(pe)

        @block.sync
        def _(sp):
            for h in range(AH):
                slot = h % 2
                sp.wait_ge(p_copied, TILES * (h + 1))
                if h >= 2:
                    sp.wait_ge(p_loaded, 16 * (h - 1))
                sp.dma_start(scratch[slot].rearrange("t p k -> p t k"), dist).then_inc(p_stored, 16)
                sp.wait_ge(p_stored, 16 * (h + 1))
                if h >= 1:
                    sp.wait_ge(summed, GROUP_SEQS * h)
                sp.dma_start(pos, shifted(slot)).then_inc(p_loaded, 16)

        @block.gpsimd
        def _(pool):
            beside.gpsimd(pool, 100)

        @block.scalar
        def _(act):
            norm.scalar(act, (0, 1), steps=(0,))
            beside.scalar(act)
            norm.scalar(act, (0, 1), steps=(1,))
            beside.scalar(act)
            for n in range(0, 2 * TILES, 2):
                if n == 4:
                    beside.scalar(act)
                act.wait_ge(v_ready, n + 1)
                nc.scalar.copy(v_sb[:, n // 2, 0:half], bank(b, n % 4)).then_inc(v_copied_a, 1)
            beside.scalar(act)

            def queries_keys(h):
                act.wait_ge(q_ready, h + 1)
                if h >= 1:
                    act.wait_ge(p_ready, TILES * h)
                if h >= 2:
                    act.wait_ge(s_ready, GROUP_SEQS * (h - 1))
                scale = AD ** -0.5
                nc.scalar.activation(q_p, bank(b, 0), ACT.Identity, bias=vec(b, ("rel_pos", h)), scale=scale)
                nc.scalar.activation(q_e[h % 2], bank(b, 0), ACT.Identity, bias=vec(b, ("rel_embed", h)), scale=scale).then_inc(q_biased, 1)
                act.wait_ge(k_ready, h + 1)
                nc.scalar.copy(k_t[h % 2], bank(b, 2)).then_inc(k_copied, 1)

            def distances(h):
                if h >= 1:
                    act.wait_ge(p_stored, 16 * h)
                for t in range(TILES):
                    act.wait_ge(p_ready, h * TILES + t + 1)
                    nc.scalar.copy(dist[:, t, :], bank(b, DIST_BANKS[t])[:, 0:384]).then_inc(p_copied, 1)

            def exps(h):
                for s in range(GROUP_SEQS):
                    act.wait_ge(maxed, GROUP_SEQS * h + s + 1)
                    for t in range(2 * s, 2 * s + 2):
                        ins = nc.scalar.activation(probs[h % 2][:, t, :], probs[h % 2][:, t, :], ACT.Exp, bias=neg_max[:, h % 2, t:t + 1],
                                                   accum_out=sums[:, h % 2, t:t + 1])
                    ins.then_inc(exped, 1)

            def normalise(h):
                act.wait_ge(inverted, h + 1)
                for s in range(GROUP_SEQS):
                    for t in range(2 * s, 2 * s + 2):
                        ins = nc.scalar.activation(probs[h % 2][:, t, :], probs[h % 2][:, t, :], ACT.Identity, scale=inv[:, h % 2, t:t + 1])
                    ins.then_inc(normed, 1)

            for i in range(ROUNDS):
                if i < AH:
                    queries_keys(i)
                if 2 <= i <= AH + 1:
                    normalise(i - 2)
                beside.scalar(act)
                if i < AH:
                    distances(i)
                beside.scalar(act)
                if 1 <= i <= AH:
                    exps(i - 1)
                beside.scalar(act, 2)

        @block.vector
        def _(dve):
            v = nc.vector
            norm.vector(dve, b.x[:], b.xn[:], (0, 1), steps=(0,))
            beside.vector(dve)
            norm.vector(dve, b.x[:], b.xn[:], (0, 1), steps=(1,))
            beside.vector(dve)
            for n in range(1, 2 * TILES, 2):
                if n == 5:
                    beside.vector(dve)
                dve.wait_ge(v_ready, n + 1)
                v.tensor_copy(v_sb[:, n // 2, half:], bank(b, n % 4)).then_inc(v_copied_v, 1)
            beside.vector(dve)

            def sums_and_maxima(h):
                dve.wait_ge(p_loaded, 16 * (h + 1))
                if h >= 2:
                    dve.wait_ge(turned, GROUP_SEQS * (h - 1))
                for s in range(GROUP_SEQS):
                    n = GROUP_SEQS * h + s
                    dve.wait_ge(s_ready, n + 1)
                    pair = probs[h % 2][:, 2 * s:2 * s + 2, :]
                    v.tensor_tensor(pair, bank(b, SCORE_BANKS[s]).rearrange("p (t k) -> p t k", t=2),
                                    pos[:, 2 * s:2 * s + 2, :], ALU.add).then_inc(summed, 1)
                    dve.wait_ge(summed, n + 1)
                    v.tensor_reduce(neg_max[:, h % 2, 2 * s:2 * s + 2], pair, AX, ALU.max, negate=True).then_inc(maxed, 1)

            def copy_turned(h, s):
                dve.wait_ge(turned, GROUP_SEQS * h + s + 1)
                if h >= 1:
                    dve.wait_ge(o_ready, h)
                v.tensor_copy(probs_t[:, s], bank(b, TURN_BANKS[s]).rearrange("p (c q) -> p c q", c=2)).then_inc(t_copied, 1)

            for i in range(ROUNDS):
                if i >= 3:
                    dve.wait_ge(o_ready, i - 2)
                    if i >= 4:
                        dve.wait_ge(projected, i - 3)
                    v.tensor_copy(o_t, bank(b, 1)).then_inc(o_copied, 1)
                beside.vector(dve, 2)
                if 1 <= i <= AH:
                    sums_and_maxima(i - 1)
                if 2 <= i <= AH + 1:
                    copy_turned(i - 2, 0)
                beside.vector(dve)
                if 2 <= i <= AH + 1:
                    copy_turned(i - 2, 1)
                beside.vector(dve)
                if 1 <= i <= AH:
                    dve.wait_ge(exped, GROUP_SEQS * i)
                    v.reciprocal(inv[:, (i - 1) % 2], sums[:, (i - 1) % 2]).then_inc(inverted, 1)
            dve.wait_ge(projected, AH)
            v.scalar_tensor_tensor(out=b.x[:], in0=bank(b, 3), scalar=vec(b, ("b_out", 0)), in1=b.x[:], op0=ALU.add, op1=ALU.add)


def norm_block(nc, b, sem, src, dst):
    norm = Norm(nc, b, sem)
    with nc.Block() as block:
        @block.tensor
        def _(pe):
            norm.tensor(pe, src, (0, 1))

        @block.scalar
        def _(act):
            norm.scalar(act, (0, 1))

        @block.vector
        def _(dve):
            norm.vector(dve, src, dst, (0, 1))


def ffn_stage(nc, b, stage_sem, beside, space):
    prefixed = lambda prefix: (lambda name: stage_sem(f"{prefix}_{name}"))
    norm_block(nc, b, prefixed("entry"), b.x[:], b.y[:])
    for l in range(DEPTH):
        ffn_layer(nc, b, prefixed(f"layer{l}"), l, beside, space)


def ffn_layer(nc, b, sem, l, beside, space):
    norm = Norm(nc, b, sem)
    shifted, qk_ready, v_ready, qk_copied, v_copied = sem("shifted"), sem("qk_ready"), sem("v_ready"), sem("qk_copied"), sem("v_copied")
    squared, summed, clipped, logged, inv_norm = sem("qk_squared"), sem("squares_summed"), sem("sums_clipped"), sem("log_sums_ready"), sem("inverse_norms")
    split, added, rotated, zeroed = sem("rotary_parts_ready"), sem("parts_added"), sem("rotated"), sem("weights_zeroed")
    qk_turned, q_copied, k_copied = sem("qk_turned"), sem("q_copied"), sem("k_copied")
    s_ready, maxed, exped, p_turned = sem("scores_ready"), sem("scores_maxed"), sem("scores_exped"), sem("probs_turned")
    p_copied_a, p_copied_v = sem("probs_copied_scalar"), sem("probs_copied_vector")
    o_ready, inverted, scaled, o_turned = sem("heads_ready"), sem("sums_inverted"), sem("heads_scaled"), sem("heads_turned")
    o_copied_a, o_copied_v = sem("heads_copied_scalar"), sem("heads_copied_vector")
    mixed, y_ready, affine, hidden, gelu, gated, out = (sem("mixed"), sem("y_ready"), sem("affine_done"), sem("hidden_ready"),
                                                        sem("gelu_ready"), sem("gated"), sem("down_ready"))
    carve = Carve(b)
    carve.at = space
    h_t = b.xn[:]
    h3 = h_t.rearrange("p (s n) -> p s n", s=GROUP_SEQS)
    y3 = b.y[:].rearrange("p (s n) -> p s n", s=GROUP_SEQS)
    two = lambda n: [carve(n) for _ in range(2)]
    q_t, k_t = (carve(4 * TOK).rearrange("p (j n) -> p j n", j=4) for _ in range(2))
    v_sb = carve(TILES * INNER).rearrange("p (t n) -> p t n", t=TILES)
    raw_all = carve(4 * INNER)
    raw = [raw_all[:, 0:2 * INNER], raw_all[:, 2 * INNER:]]
    squares, cosine, sine_all = carve(2 * INNER), two(2 * INNER), carve(4 * INNER)
    sine = [sine_all[:, 0:2 * INNER], sine_all[:, 2 * INNER:]]
    probs_near = [t.rearrange("p (h k) -> p h k", h=4) for t in two(4 * 128)]
    probs_wide = [t.rearrange("p (h k) -> p h k", h=4) for t in two(4 * SEQ)]
    lens = [t.rearrange("p (a n) -> p a n", a=4) for t in two(4 * 16)]
    neg_max, sums = (carve(TILES * LH).rearrange("p (t h) -> p t h", t=TILES) for _ in range(2))
    probs_t = [t.rearrange("p (h c q) -> p h c q", h=4, c=2) for t in cosine]
    heads = sine_all.rearrange("p (t n) -> p t n", t=TILES)
    o_t = raw_all.rearrange("p (j n) -> p j n", j=4)
    gelu_t, gated_t = q_t, k_t
    UNITS = 2 * TILES
    SLOT_HEADS = (0, 2, 1, 3)

    def span(t):
        return (0, 128) if t % 2 == 0 else (64, 192)

    score_banks = bank(b, 0, 2).rearrange("p (h k) -> p h k", h=4)

    def prob_of(u):
        return (probs_wide if (u // 2) % 2 else probs_near)[u % 2]

    with nc.Block() as block:
        @block.tensor
        def _(pe):
            w = b.wqkv[:, l]
            pe.wait_ge(shifted, 1)

            def project(t):
                lhs = h_t[:, t * 128:(t + 1) * 128]
                if t >= 1:
                    pe.wait_ge(qk_copied, t)
                nc.tensor.matmul(bank(b, 0), lhs, w[:, 0:INNER], start=True, stop=True)
                nc.tensor.matmul(bank(b, 1), lhs, w[:, INNER:2 * INNER], start=True, stop=True).then_inc(qk_ready, 1)
                if t >= 1:
                    pe.wait_ge(v_copied, t)
                nc.tensor.matmul(bank(b, 2), lhs, w[:, 2 * INNER:], start=True, stop=True).then_inc(v_ready, 1)

            def turn(t):
                pe.wait_ge(rotated, t + 1)
                if t >= 1:
                    pe.wait_ge(q_copied, t)
                    pe.wait_ge(k_copied, t)
                for j in range(8):
                    ins = nc.tensor.transpose(bank(b, 3 + j // 4)[:, (j % 4) * 128:(j % 4 + 1) * 128],
                                              cosine[t % 2][:, j * 128:(j + 1) * 128], b.ident[:])
                ins.then_inc(qk_turned, 1)

            project(0)
            for t in range(TILES):
                if t + 1 < TILES:
                    project(t + 1)
                beside.tensor(pe)
                turn(t)

            def scores(u):
                t, half = u // 2, u % 2
                first, n = span(t)
                if u == 0:
                    pe.wait_ge(qk_copied, TILES)
                else:
                    pe.wait_ge(exped, u)
                keys = (t // 2) * SEQ + first
                mask = b.mask_bf[:, 0:128] if t % 2 == 0 else b.mask_bf[:, 128:320]
                for k in range(2):
                    nc.tensor.matmul(score_banks[:, 2 * k:2 * k + 2, first:first + n], b.ident_bf[:],
                                     mask.unsqueeze(1).broadcast_to([128, 2, n]), start=True, stop=False)
                for i in (0, 2, 1, 3):
                    head = 4 * half + SLOT_HEADS[i]
                    rows = slice(64 * (head % 2), 64 * (head % 2) + 64)
                    ins = nc.tensor.matmul(score_banks[:, i, first:first + n], q_t[rows, head // 2, t * 128:(t + 1) * 128],
                                           k_t[rows, head // 2, keys:keys + n], start=False, stop=i % 2 == 1)
                ins.then_inc(s_ready, 1)

            def turn_probs(u):
                t = u // 2
                pe.wait_ge(exped, u + 1)
                if u == 0:
                    pe.wait_ge(v_copied, TILES)
                else:
                    pe.wait_ge(p_copied_a, u)
                    pe.wait_ge(p_copied_v, u)
                for i in range(4):
                    for c in range(1 + t % 2):
                        at = (i % 2) * 256 + c * 128
                        ins = nc.tensor.transpose(bank(b, 2 + i // 2)[:, at:at + 128], prob_of(u)[:, i, c * 128:(c + 1) * 128], b.ident[:])
                ins.then_inc(p_turned, 1)

            def values(u):
                t, half = u // 2, u % 2
                pe.wait_ge(p_copied_a, u + 1)
                pe.wait_ge(p_copied_v, u + 1)
                if half == 0 and t >= 1:
                    pe.wait_ge(scaled, t)
                chunks = 1 + t % 2
                for i in range(4):
                    head = 4 * half + SLOT_HEADS[i]
                    for c in range(chunks):
                        ins = nc.tensor.matmul(bank(b, 4)[:, head * LD:(head + 1) * LD], probs_t[u % 2][:, i, c],
                                               v_sb[:, 2 * (t // 2) + c, head * LD:(head + 1) * LD], start=c == 0, stop=c == chunks - 1)
                ins.then_inc(o_ready, 1)

            pe.wait_ge(q_copied, TILES)
            pe.wait_ge(k_copied, TILES)
            scores(0)
            for u in range(UNITS + 1):
                beside.tensor(pe)
                if u < UNITS:
                    turn_probs(u)
                if u + 1 < UNITS:
                    scores(u + 1)
                if u >= 1:
                    values(u - 1)
            for t in range(TILES):
                pe.wait_ge(scaled, t + 1)
                for j in range(4):
                    ins = nc.tensor.transpose(bank(b, t)[:, j * 128:(j + 1) * 128], heads[:, t, j * 128:(j + 1) * 128], b.ident[:])
                ins.then_inc(o_turned, 1)
            beside.tensor(pe)
            pe.wait_ge(o_copied_a, 2)
            pe.wait_ge(o_copied_v, 2)
            for j in range(4):
                ins = nc.tensor.matmul(bank(b, 4), b.wo[:, l, j], o_t[:, j], start=j == 0, stop=j == 3)
            ins.then_inc(mixed, 1)
            beside.tensor(pe)
            pe.wait_ge(shifted, 2)
            norm.tensor(pe, h_t, (0, 1), steps=(0,))
            beside.tensor(pe)
            norm.tensor(pe, h_t, (0, 1), steps=(1,))
            beside.tensor(pe)
            pe.wait_ge(affine, 1)
            for n in range(6):
                at, rows = HC[n // 2]
                first = at + (HID if n % 2 == 0 else 0)
                if n == 5:
                    pe.wait_ge(gelu, 1)
                nc.tensor.matmul(bank(b, n % 5)[0:rows], b.w1[:, l, first:first + rows], b.sq[:], start=True, stop=True).then_inc(hidden, 1)
            beside.tensor(pe)
            for c in range(3):
                rows = HC[c][1]
                pe.wait_ge(gated, c + 1)
                ins = nc.tensor.matmul(bank(b, 1), b.w2[0:rows, l, c], gated_t[0:rows, c], start=c == 0, stop=c == 2)
            ins.then_inc(out, 1)

        @block.scalar
        def _(act):
            s = nc.scalar
            for t in range(TILES + 1):
                if t < TILES:
                    act.wait_ge(qk_ready, t + 1)
                    if t >= 2:
                        act.wait_ge(split, t - 1)
                    s.copy(raw[t % 2], bank(b, 0, 2)).then_inc(qk_copied, 1)
                    act.wait_ge(qk_copied, t + 1)
                    if t >= 1:
                        act.wait_ge(summed, t)
                    s.activation(squares, raw[t % 2], ACT.Square).then_inc(squared, 1)
                    act.wait_ge(v_ready, t + 1)
                    s.copy(v_sb[:, t], bank(b, 2)).then_inc(v_copied, 1)
                    act.wait_ge(clipped, t + 1)
                    s.activation(lens[t % 2][:, 1], lens[t % 2][:, 0], ACT.Ln, scale=LENGTH_SCALE).then_inc(logged, 1)
                    act.wait_ge(logged, t + 1)
                    s.activation(lens[t % 2][:, 2], lens[t % 2][:, 1], ACT.Exp, scale=-0.5).then_inc(inv_norm, 1)
                if t >= 1:
                    beside.scalar(act)
                    at = slice((t - 1) * 128, t * 128)
                    act.wait_ge(qk_turned, t)
                    s.copy(q_t[:, :, at], bank(b, 3).rearrange("p (j n) -> p j n", j=4)).then_inc(q_copied, 1)
                    s.copy(k_t[:, :, at], bank(b, 4).rearrange("p (j n) -> p j n", j=4)).then_inc(k_copied, 1)

            def exps(u):
                t, half = u // 2, u % 2
                first, n = span(t)
                act.wait_ge(maxed, u + 1)
                if u >= 2:
                    act.wait_ge(p_turned, u - 1)
                for i in range(4):
                    head = 4 * half + SLOT_HEADS[i]
                    ins = s.activation(prob_of(u)[:, i, first:first + n], score_banks[:, i, first:first + n], ACT.Exp,
                                       bias=neg_max[:, t, 4 * half + i:4 * half + i + 1], accum_out=sums[:, t, head:head + 1])
                ins.then_inc(exped, 1)

            def copy_probs(u):
                act.wait_ge(p_turned, u + 1)
                if u >= 2:
                    act.wait_ge(o_ready, u - 1)
                c = 1 + (u // 2) % 2
                s.copy(probs_t[u % 2][:, 0:2, 0:c], bank(b, 2).rearrange("p (h c q) -> p h c q", h=2, c=2)[:, :, 0:c]).then_inc(p_copied_a, 1)

            act.wait_ge(zeroed, 1)
            exps(0)
            for u in range(UNITS + 1):
                beside.scalar(act)
                if u < UNITS:
                    copy_probs(u)
                if u + 1 < UNITS:
                    exps(u + 1)
            for t in (0, 2):
                act.wait_ge(o_turned, t + 1)
                s.copy(o_t[:, :, t * 128:(t + 1) * 128], bank(b, t).rearrange("p (j n) -> p j n", j=4)).then_inc(o_copied_a, 1)
            beside.scalar(act, 2)
            norm.scalar(act, (0, 1), steps=(0,))
            beside.scalar(act)
            norm.scalar(act, (0, 1), steps=(1,))
            beside.scalar(act)
            for c in range(3):
                rows = HC[c][1]
                act.wait_ge(hidden, 2 * c + 1)
                s.activation(gelu_t[0:rows, c], bank(b, 2 * c)[0:rows], ACT.Gelu, bias=vec(b, (("b1_gate", c), l), rows)).then_inc(gelu, 1)
            beside.scalar(act)

        @block.gpsimd
        def _(pool):
            pool.memset(probs_wide[0][:, :, 0:64], 0.0)
            pool.memset(probs_wide[1][:, :, 0:64], 0.0).then_inc(zeroed, 1)
            for t in range(TILES):
                pool.wait_ge(split, t + 1)
                pool.tensor_tensor(cosine[t % 2], cosine[t % 2], sine[t % 2], ALU.add).then_inc(added, 1)
                pool.wait_ge(added, t + 1)
                pool.wait_ge(inv_norm, t + 1)
                both = cosine[t % 2].rearrange("p (h d) -> p h d", d=LD)
                pool.tensor_tensor(both, both, lens[t % 2][:, 2].unsqueeze(2).broadcast_to([128, 16, LD]), ALU.mult).then_inc(rotated, 1)

        @block.vector
        def _(dve):
            v = nc.vector

            def shift():
                v.tensor_copy(h3[0:64], y3[0:64])
                v.memset(h3[64:128, :, 0:1], 0.0)
                v.tensor_copy(h3[64:128, :, 1:], y3[64:128, :, :SEQ - 1]).then_inc(shifted, 1)

            shift()
            for t in range(TILES + 1):
                if t < TILES:
                    s, n = t % 2, lens[t % 2]
                    dve.wait_ge(squared, t + 1)
                    v.tensor_reduce(n[:, 3], squares.rearrange("p (h d) -> p h d", d=LD), AX, ALU.add).then_inc(summed, 1)
                    dve.wait_ge(summed, t + 1)
                    v.tensor_scalar(n[:, 0], n[:, 3], 1e-24, None, ALU.max).then_inc(clipped, 1)
                    if t >= 2:
                        dve.wait_ge(qk_turned, t - 1)
                    for k in range(2):
                        r8, c8, s8 = (x[t % 2][:, k * INNER:(k + 1) * INNER].rearrange("p (h d) -> p h d", d=LD) for x in (raw, cosine, sine))
                        table = lambda n, x0, x1: b.rope_w[:, l, n, s, x0:x1].unsqueeze(1).broadcast_to([128, LH, x1 - x0])
                        v.tensor_tensor(c8, r8, table(2 * k, 0, LD), ALU.mult)
                        v.tensor_tensor(s8[:, :, 0:32], r8[:, :, 32:64], table(2 * k + 1, 0, 32), ALU.mult)
                        ins = v.tensor_tensor(s8[:, :, 32:64], r8[:, :, 0:32], table(2 * k + 1, 32, 64), ALU.mult)
                    ins.then_inc(split, 1)
                if t >= 1:
                    beside.vector(dve)

            def maxima(u):
                t, half = u // 2, u % 2
                first, n = span(t)
                dve.wait_ge(s_ready, u + 1)
                v.tensor_reduce(neg_max[:, t, 4 * half:4 * half + 4], score_banks[:, :, first:first + n], AX, ALU.max, negate=True).then_inc(maxed, 1)

            def copy_probs(u):
                dve.wait_ge(p_turned, u + 1)
                if u >= 2:
                    dve.wait_ge(o_ready, u - 1)
                c = 1 + (u // 2) % 2
                v.tensor_copy(probs_t[u % 2][:, 2:4, 0:c], bank(b, 3).rearrange("p (h c q) -> p h c q", h=2, c=2)[:, :, 0:c]).then_inc(p_copied_v, 1)

            def scale_heads(t):
                dve.wait_ge(o_ready, 2 * t + 2)
                v.reciprocal(sums[:, t], sums[:, t]).then_inc(inverted, 1)
                dve.wait_ge(inverted, t + 1)
                v.tensor_tensor(heads[:, t].rearrange("p (h d) -> p h d", d=LD), bank(b, 4).rearrange("p (h d) -> p h d", d=LD),
                                sums[:, t].unsqueeze(2).broadcast_to([128, LH, LD]), ALU.mult).then_inc(scaled, 1)

            maxima(0)
            for u in range(UNITS + 1):
                beside.vector(dve)
                if u < UNITS:
                    copy_probs(u)
                if u + 1 < UNITS:
                    maxima(u + 1)
                if u % 2 == 0 and u >= 2:
                    scale_heads((u - 2) // 2)
            for t in (1, 3):
                dve.wait_ge(o_turned, t + 1)
                v.tensor_copy(o_t[:, :, t * 128:(t + 1) * 128], bank(b, t).rearrange("p (j n) -> p j n", j=4)).then_inc(o_copied_v, 1)
            beside.vector(dve)
            dve.wait_ge(mixed, 1)
            v.tensor_tensor(b.y[:], b.y[:], bank(b, 4), ALU.add).then_inc(y_ready, 1)
            dve.wait_ge(y_ready, 1)
            shift()
            dve.wait_ge(shifted, 2)
            beside.vector(dve)
            norm.vector(dve, h_t, b.xn[:], (0, 1), steps=(0,))
            beside.vector(dve)
            norm.vector(dve, h_t, b.xn[:], (0, 1), steps=(1,))
            dve.wait_ge(norm.done, 1)
            v.tensor_scalar(b.sq[:], b.xn[:], vec(b, ("ln_g", l)), vec(b, ("ln_b", l)), ALU.mult, ALU.add).then_inc(affine, 1)
            beside.vector(dve)
            for c in range(3):
                rows = HC[c][1]
                dve.wait_ge(hidden, 2 * c + 2)
                dve.wait_ge(gelu, c + 1)
                v.scalar_tensor_tensor(out=gated_t[0:rows, c], in0=bank(b, (1, 3, 0)[c])[0:rows], scalar=vec(b, (("b1_value", c), l), rows),
                                       in1=gelu_t[0:rows, c], op0=ALU.add, op1=ALU.mult).then_inc(gated, 1)
            beside.vector(dve)
            dve.wait_ge(out, 1)
            v.scalar_tensor_tensor(out=b.y[:], in0=bank(b, 1), scalar=vec(b, ("b2", l)), in1=b.y[:], op0=ALU.add, op1=ALU.add).then_inc(y_ready, 1)
            if l == DEPTH - 1:
                dve.wait_ge(y_ready, 2)
                v.scalar_tensor_tensor(out=b.x[:], in0=b.y[:], scalar=0.5, in1=b.x[:], op0=ALU.mult, op1=ALU.add)


def hand_over(nc, b, sem):
    moved = sem("stream_moved")
    with nc.Block() as block:
        @block.vector
        def _(dve):
            nc.vector.tensor_copy(b.x_late[:], b.x[:]).then_inc(moved, 1)


def build_program(nc, A, out):
    with ExitStack() as ctx:
        b = allocate(nc, ctx)
        weights(nc, b, A)
        src = A["L0_attn_q"].rearrange("b n d -> (b n) d")
        dst = out.rearrange("b n d -> (b n) d")
        sems = Semaphores(nc)
        ffn, attn, moe, mamba = ("ffn" in STAGES), ("attn" in STAGES), ("moe" in STAGES), ("mamba" in STAGES)

        def stages(g, early, late):
            if early:
                load_tokens(nc, b, sems.stage("load"), src, g)
            if ffn or moe:
                first_and_third(nc, b, sems, "first", early and ffn, late and moe)
            if attn or mamba:
                second(nc, b, sems, A["scratch"], early and attn, late and mamba)
            if ffn or moe:
                first_and_third(nc, b, sems, "third", early and ffn and STAGES.count("ffn") > 1, late and moe and STAGES.count("moe") > 1)
            if late:
                store_tokens(nc, b, sems.stage("store"), dst, g - 1)
            if early:
                hand_over(nc, b, sems.stage("hand_over"))
            sems.clear()

        stages(0, True, False)
        if GROUPS > 1:
            with nc.Fori(1, GROUPS) as g:
                stages(g, True, True)
        stages(GROUPS, False, True)


def constants():
    f = np.float32
    p = np.arange(128)
    fold64 = (p[:, None] % 64 == np.arange(64)[None, :]).astype(f)
    fold32 = (p[:, None] % 32 == np.arange(32)[None, :]).astype(f)
    near = p[:, None] - np.arange(128)[None, :]
    wide = p[:, None] + 64 - np.arange(192)[None, :]
    mask = np.concatenate([np.where((d >= 0) & (d <= WINDOW), 0.0, NEG) for d in (near, wide)], axis=1).astype(f)
    half = np.arange(0, LD, 2, dtype=f)
    inv_freq = (f(1.0) / f(10000.0) ** (half / f(LD))).astype(f)
    t = np.arange(SEQ, dtype=f)
    freqs = np.concatenate([t[:, None] * inv_freq[None, :]] * 2, axis=1).astype(f)
    base = ((half + f(0.4 * LD)) / f(1.4 * LD)).astype(f)
    power = ((t - SEQ // 2) / f(WINDOW // 2)).astype(f)
    scale = np.concatenate([base[None, :] ** power[:, None]] * 2, axis=1).astype(f)
    sign = np.where(np.arange(LD) < LD // 2, -1.0, 1.0).astype(f)
    cos, sin = np.cos(freqs), np.sin(freqs) * sign
    rope = np.stack([cos * scale * 8, sin * scale * 8, cos / scale, sin / scale]).astype(f)
    rope = rope.reshape(4, 2, 128, LD).transpose(2, 0, 1, 3) * f(LENGTH_SCALE ** 0.5)
    dist = np.arange(-SEQ + 1, SEQ, dtype=np.float64)
    n = REL // 6
    absd = np.abs(dist)[:, None]
    half_life = 2.0 ** np.linspace(3.0, math.log(SEQ) / math.log(2.0), n)
    feat_exp = np.exp(-math.log(2.0) / half_life[None, :] * absd)
    widths = 2.0 ** np.arange(1, n + 1) - 1.0
    feat_cm = (widths[None, :] > absd).astype(np.float64)
    stddev = SEQ / (2.0 * n)
    mean = np.linspace(SEQ / n, float(SEQ), n)[None, :]
    conc, rate = (mean / stddev) ** 2, mean / stddev ** 2
    log_d = np.log(np.maximum(absd, 1e-300))
    log_norm = np.array([[math.lgamma(c) for c in conc[0]]]) - conc * np.log(rate)
    probs = np.where(absd > 0, np.exp((conc - 1.0) * log_d - rate * absd - log_norm), 0.0) + 1e-8
    feat_gamma = probs / probs.max(axis=-1, keepdims=True)
    emb = np.concatenate([feat_exp, feat_cm, feat_gamma], axis=-1)
    emb = np.concatenate([emb, np.sign(dist)[:, None] * emb], axis=-1)
    pos = np.zeros((REL, 2 * SEQ), f)
    pos[:, 0:2 * SEQ - 1] = emb.T
    return {"const_ident": np.eye(128, dtype=f), "const_fold64": fold64, "const_fold32": fold32, "const_mask": mask,
            "const_rope": np.ascontiguousarray(rope), "const_pos": pos}


def kernel(**inputs):
    import concourse.bacc as bacc
    from concourse.bass_utils import run_bass_kernel_spmd as run

    nc = bacc.Bacc("TRN2", target_bir_lowering=False, num_devices=1)
    arrays, A = {}, {}
    for name, a in {**inputs, **constants()}.items():
        a = np.ascontiguousarray(a)
        arrays[f"in_{name}"] = a
        A[name] = nc.dram_tensor(f"in_{name}", a.shape, mybir.dt.from_np(a.dtype), kind="ExternalInput").ap()
    A["scratch"] = nc.dram_tensor("position_scores", (2, TILES, 128, 384), F32, kind="Internal").ap()
    out = nc.dram_tensor("out", (BATCH, SEQ, DIM), F32, kind="ExternalOutput").ap()
    build_program(nc, A, out)
    result = run(nc, [arrays], core_ids=[0])
    return result.results[0]["out"]
```

```python
import math
from contextlib import ExitStack

import numpy as np

import concourse.bass as bass
from concourse import mybir

F32 = mybir.dt.float32
BF16 = mybir.dt.bfloat16
ALU = mybir.AluOpType
ACT = mybir.ActivationFunctionType
AX = mybir.AxisListType.X

BATCH, SEQ, DIM = 16, 256, 128
GROUP_SEQS = 2
TOK = GROUP_SEQS * SEQ
TILES = TOK // 128
GROUPS = BATCH // GROUP_SEQS

DEPTH, LH, LD, WINDOW = 2, 8, 64, 64
INNER = LH * LD
HID = 341
HC = [(c * 128, min(128, HID - c * 128)) for c in range(3)]
AH, AD, REL = 8, 128, 192
EXPERTS, EF, TOP_K = 64, 64, 8
PAIRS = EXPERTS // 2
CH, STATES, CONV = 256, 16, 4
NEG = -3.0e38



class Signal:

    def __init__(self, sem):
        self.sem, self.n = sem, 0

    def mark(self, instruction):
        instruction.then_inc(self.sem, 1)
        self.n += 1
        return self.n


class Chain(Signal):

    def __init__(self, engine, sem):
        super().__init__(sem)
        self.engine = engine

    def link(self, instruction):
        self.engine.wait_ge(self.sem, self.mark(instruction))


class Buffers:
    pass


def allocate(nc, ctx):
    b = Buffers()

    def sb(name, shape, dt=F32):
        t = ctx.enter_context(nc.sbuf_tensor(name, shape, dt))
        return t

    b.ident = sb("ident", [128, 128])
    b.ident_bf = sb("ident_bf", [128, 128], BF16)
    b.mean_w = sb("mean_w", [128, 128])
    b.eps = sb("eps", [128, 1])
    b.minus_half = sb("minus_half", [128, 1])
    b.mask_bf = sb("mask_bf", [128, 320], BF16)
    b.pair_sel = sb("pair_sel", [128, PAIRS // 2, 2, 64], BF16)
    b.fold32 = sb("fold32", [128, 32])
    b.fold32_bf = sb("fold32_bf", [128, 32], BF16)
    b.x = sb("x", [128, TOK])
    b.x_late = sb("x_late", [128, TOK])
    b.y = sb("y", [128, TOK])
    b.xn = sb("xn", [128, TOK])
    b.cent = sb("cent", [128, TOK])
    b.sq = sb("sq", [128, TOK])
    b.rstd = sb("rstd", [128, TOK])
    b.rows = sb("rows", [128, TILES, 128])
    b.wqkv = sb("wqkv", [128, DEPTH, 3 * INNER])
    b.wo = sb("wo", [128, DEPTH, 4, DIM])
    b.w1 = sb("w1", [128, DEPTH, 2 * HID])
    b.w2 = sb("w2", [128, DEPTH, 3, DIM])
    b.rope_w = sb("rope_w", [128, DEPTH, 4, 2, 64])
    b.wq = sb("wq", [128, AH * AD])
    b.wk = sb("wk", [128, AH * AD])
    b.wv = sb("wv", [128, AH * AD])
    b.w_out = sb("w_out", [128, AH, DIM])
    b.rel_k = sb("rel_k", [128, AH, 512])
    b.w_up = sb("w_up", [128, EXPERTS * EF])
    b.w_down = sb("w_down", [128, PAIRS, DIM])
    b.ws_up = sb("ws_up", [128, EF])
    b.ws_down = sb("ws_down", [EF, DIM])
    b.centroids_t = sb("centroids_t", [128, EXPERTS])
    b.expert_bias = sb("expert_bias", [128, EXPERTS])
    b.in_w = sb("in_w", [128, 2 * CH])
    b.A = sb("A", [128, 2, STATES])
    b.bc_w = sb("bc_w", [128, 2, 2 * STATES])
    b.dt_w = sb("dt_w", [128, 2, CH])
    b.ssm_out_w = sb("ssm_out_w", [128, 2, DIM])
    b.vec_cols = sb("vec_cols", [128, 128])
    b.vec_at = {}
    b.work = sb("work", [128, WORK])
    b.psum = ctx.enter_context(nc.psum_tensor("psum", [128, 8 * 512], F32))
    return b


WORK = 21984
STAGED = 2 * 512 + 2 * AH * AD + DIM


def bank(b, i, n=1):
    return b.psum[:, i * 512:(i + n) * 512]


def vec(b, name, n=128):
    at = b.vec_at[name]
    return b.vec_cols[0:n, at:at + 1]


class Carve:

    def __init__(self, b):
        self.b, self.at = b, 0

    def __call__(self, columns, dt=F32):
        words = columns if dt == F32 else columns // 2
        piece = self.b.work[:, self.at:self.at + words]
        self.at += words
        assert self.at <= WORK, self.at
        return piece if dt == F32 else piece.bitcast(dt)


def staged(b):
    carve = Carve(b)
    carve.at = WORK - STAGED
    return (carve(2 * 512).rearrange("p (c n) -> p c n", c=2), carve(2 * AH * AD).rearrange("p (c n) -> p c n", c=2),
            carve(DIM)[0:EXPERTS])


def weights(nc, b, A):
    with ExitStack() as ctx:
        sem = lambda name: ctx.enter_context(nc.semaphore(name))
        loaded, zeroed, products = sem("weights_loaded"), sem("rows_zeroed"), sem("setup_products")
        carve = Carve(b)
        mask_f, vec_rows = carve(320), carve(128)
        rope = carve(4 * 2 * LD).rearrange("p (k s d) -> p k s d", k=4, s=2)
        pos, w_rel, centroids = staged(b)
        qk_scale = carve(2 * DEPTH * LD).rearrange("p (k l d) -> p k l d", k=2, l=DEPTH)
        rows_at, vector_loads = [0], []

        def vectors_of(name, source):
            first, n = rows_at[0], source.shape[0]
            for k in range(n):
                b.vec_at[name, k] = first + k
            vector_loads.append((vec_rows[first:first + n, 0:source.shape[1]], source))
            rows_at[0] += n

        rows_of = lambda ap: ap.rearrange("(c p) -> c p", p=128)
        row = lambda ap: ap.rearrange("(a p) -> a p", a=1)
        vectors_of("rel_embed", A["L0_attn_rel_embed_bias"].rearrange("a h b p -> (a b h) p"))
        vectors_of("rel_pos", A["L0_attn_rel_pos_bias"].rearrange("a h b p -> (a b h) p"))
        vectors_of("b_out", row(A["L0_attn_b_out"]))
        vectors_of("in_b", rows_of(A["L1_attn_in_b"]))
        vectors_of("conv_w", A["L1_attn_conv_w"].rearrange("k a (c p) -> (k a c) p", p=128))
        vectors_of("conv_b", rows_of(A["L1_attn_conv_b"]))
        vectors_of("Dp", rows_of(A["L1_attn_Dp"]))
        vectors_of("dt_b", rows_of(A["L1_attn_dt_b"]))
        vectors_of("ssm_out_b", row(A["L1_attn_out_b"]))
        vectors_of("ln_g", A["L0_ffn_ln_g"])
        vectors_of("ln_b", A["L0_ffn_ln_b"])
        vectors_of("b2", A["L0_ffn_b2"])
        for c, (at, n) in enumerate(HC):
            vectors_of(("b1_value", c), A["L0_ffn_b1"][:, at:at + n])
            vectors_of(("b1_gate", c), A["L0_ffn_b1"][:, HID + at:HID + at + n])
        bc_row = rows_at[0]
        b.vec_at["bc_b", 0] = bc_row
        vector_loads += [(vec_rows[bc_row:bc_row + 1, 0:STATES], row(A["L1_attn_B_b"])),
                         (vec_rows[bc_row:bc_row + 1, STATES:2 * STATES], row(A["L1_attn_C_b"]))]
        loads = [
            (b.ident[:], A["const_ident"]), (b.fold32[:], A["const_fold32"]),
            (mask_f, A["const_mask"]), (rope, A["const_rope"]),
            (b.wqkv[:, 0], A["L0_ffn_wqkv"][0]), (b.w1[:], A["L0_ffn_w1"].rearrange("l p n -> p l n")),
            (b.wqkv[:, 1], A["L0_ffn_wqkv"][1]),
        ]
        for l in range(DEPTH):
            loads += [
                (b.wo[:, l], A["L0_ffn_wo"][l].rearrange("(c p) n -> p c n", p=128)),
                (qk_scale[:, 0, l], A["L0_ffn_q_scale"][l].partition_broadcast(128)),
                (qk_scale[:, 1, l], A["L0_ffn_k_scale"][l].partition_broadcast(128)),
            ]
            for c, (at, n) in enumerate(HC):
                loads += [(b.w2[0:n, l, c], A["L0_ffn_w2"][l, at:at + n, :])]
        n_loads = len(loads) + len(vector_loads)
        later = [
            (b.wq[:], A["L0_attn_w_qs"]), (b.wk[:], A["L0_attn_w_ks"]), (b.wv[:], A["L0_attn_w_vs"]),
            (b.w_out[:], A["L0_attn_w_out"].rearrange("(h p) n -> p h n", p=128)),
            (pos[:, 0, :], A["const_pos"][0:128, :]), (pos[0:64, 1, :], A["const_pos"][128:192, :]),
            (w_rel[:, 0, :], A["L0_attn_w_rel_pos_k"][0:128, :]), (w_rel[0:64, 1, :], A["L0_attn_w_rel_pos_k"][128:192, :]),
            (b.w_up[:].rearrange("p (e f) -> p e f", f=EF), A["L1_ffn_W_up"].rearrange("e p f -> p e f")),
            (b.w_down[:], A["L1_ffn_W_down"].rearrange("(q a) f n -> (a f) q n", a=2)),
            (b.ws_up[:], A["L1_ffn_Ws_up"]), (b.ws_down[:], A["L1_ffn_Ws_down"]),
            (centroids, A["L1_ffn_centroids"]),
            (b.expert_bias[:], A["L1_ffn_expert_biases"].partition_broadcast(128)),
            (b.in_w[:], A["L1_attn_in_w"]),
            (b.A[:], A["L1_attn_A"].rearrange("(c p) s -> p c s", p=128)),
            (b.bc_w[:, :, 0:STATES], A["L1_attn_B_w"].rearrange("(c p) s -> p c s", p=128)),
            (b.bc_w[:, :, STATES:], A["L1_attn_C_w"].rearrange("(c p) s -> p c s", p=128)),
            (b.dt_w[:], A["L1_attn_dt_w"].rearrange("(c p) n -> p c n", p=128)),
            (b.ssm_out_w[:], A["L1_attn_out_w"].rearrange("(c p) n -> p c n", p=128)),
        ]

        with nc.Block() as block:
            @block.sync
            def _(sp):
                for dst, src in loads[0::2]:
                    sp.dma_start(dst, src).then_inc(loaded, 16)
                sp.wait_ge(zeroed, 1)
                for dst, src in vector_loads:
                    sp.dma_start(dst, src).then_inc(loaded, 16)

            @block.gpsimd
            def _(pool):
                pool.memset(vec_rows, 0.0).then_inc(zeroed, 1)
                pool.memset(b.mean_w[:], 1.0 / DIM)
                pool.memset(b.eps[:], 1e-5)
                pool.memset(b.minus_half[:], -0.5)

            @block.scalar
            def _(act):
                for dst, src in loads[1::2]:
                    act.dma_start(dst, src).then_inc(loaded, 16)

            @block.tensor
            def _(pe):
                pe.wait_ge(loaded, 16 * n_loads)
                nc.tensor.transpose(bank(b, 1)[:, 0:128], vec_rows, b.ident[:]).then_inc(products, 1)

            @block.vector
            def _(dve):
                dve.wait_ge(loaded, 16 * n_loads)
                dve.wait_ge(products, 1)
                nc.vector.tensor_copy(b.vec_cols[:], bank(b, 1)[:, 0:128])
                nc.vector.tensor_copy(b.ident_bf[:], b.ident[:])
                nc.vector.tensor_copy(b.mask_bf[:], mask_f)
                for p in range(PAIRS // 2):
                    nc.vector.tensor_copy(b.pair_sel[:, p], b.fold32[:, 2 * p:2 * p + 2].unsqueeze(2).broadcast_to([128, 2, 64]))
                nc.vector.tensor_copy(b.fold32_bf[:], b.fold32[:])
                for l in range(DEPTH):
                    for qk in range(2):
                        sc = qk_scale[:, qk, l]
                        for s in range(2):
                            nc.vector.tensor_tensor(b.rope_w[:, l, 2 * qk, s], rope[:, 2 * qk, s], sc, ALU.mult)
                            nc.vector.tensor_tensor(b.rope_w[:, l, 2 * qk + 1, s, 0:32], rope[:, 2 * qk + 1, s, 0:32], sc[:, 32:64], ALU.mult)
                            nc.vector.tensor_tensor(b.rope_w[:, l, 2 * qk + 1, s, 32:64], rope[:, 2 * qk + 1, s, 32:64], sc[:, 0:32], ALU.mult)
        return later


def rest_of_weights(nc, b, sem, later_loaded, transfers):
    turned, copied, products, keys_copied = sem("centroids_turned"), sem("centroids_copied"), sem("products"), sem("keys_copied")
    pos, w_rel, centroids = staged(b)
    with nc.Block() as block:
        @block.tensor
        def _(pe):
            pe.wait_ge(later_loaded, 16 * transfers)
            nc.tensor.transpose(bank(b, 0)[:, 0:EXPERTS], centroids, b.ident[0:EXPERTS, 0:EXPERTS]).then_inc(turned, 1)
            pe.wait_ge(copied, 1)
            for h in range(AH):
                nc.tensor.matmul(bank(b, h), w_rel[:, 0, h * AD:(h + 1) * AD], pos[:, 0, :], start=True, stop=False)
                nc.tensor.matmul(bank(b, h), w_rel[0:64, 1, h * AD:(h + 1) * AD], pos[0:64, 1, :],
                                 start=False, stop=True).then_inc(products, 1)

        @block.vector
        def _(dve):
            dve.wait_ge(turned, 1)
            nc.vector.tensor_copy(b.centroids_t[:], bank(b, 0)[:, 0:EXPERTS]).then_inc(copied, 1)

        @block.scalar
        def _(act):
            for h in range(AH):
                act.wait_ge(products, h + 1)
                nc.scalar.copy(b.rel_k[:, h, :], bank(b, h)).then_inc(keys_copied, 1)


class Norm:

    def __init__(self, nc, b, sem, buffers=None):
        self.nc, self.b = nc, b
        self.cent, self.sq, self.rstd = buffers or (b.cent[:], b.sq[:], b.rstd[:])
        self.mean, self.centred, self.squared, self.variance, self.logged, self.inverse, self.done = (
            sem(n) for n in ("mean_ready", "centred_ready", "squares_ready", "variance_ready",
                             "log_variance_ready", "rstd_ready", "norm_done"))

    def tensor(self, pe, src, banks, steps=(0, 1)):
        b = self.b
        if 0 in steps:
            self.nc.tensor.matmul(bank(b, banks[0]), b.mean_w[:], src, start=True, stop=True).then_inc(self.mean, 1)
        if 1 in steps:
            pe.wait_ge(self.squared, 1)
            self.nc.tensor.matmul(bank(b, banks[1]), b.mean_w[:], self.sq, start=True, stop=True).then_inc(self.variance, 1)

    def vector(self, dve, src, dst, banks, steps=(0, 1)):
        b, v = self.b, self.nc.vector
        if 0 in steps:
            dve.wait_ge(self.mean, 1)
            v.tensor_tensor(self.cent, src, bank(b, banks[0]), ALU.subtract).then_inc(self.centred, 1)
        if 1 in steps:
            dve.wait_ge(self.inverse, 1)
            v.tensor_tensor(dst, self.cent, self.rstd, ALU.mult).then_inc(self.done, 1)

    def scalar(self, act, banks, steps=(0, 1)):
        b, s = self.b, self.nc.scalar
        if 0 in steps:
            act.wait_ge(self.centred, 1)
            s.activation(self.sq, self.cent, ACT.Square).then_inc(self.squared, 1)
        if 1 in steps:
            act.wait_ge(self.variance, 1)
            s.activation(self.rstd, bank(b, banks[1]), ACT.Ln, bias=b.eps[:]).then_inc(self.logged, 1)
            act.wait_ge(self.logged, 1)
            s.activation(self.rstd, self.rstd, ACT.Exp, scale=-0.5).then_inc(self.inverse, 1)


class Semaphores:

    def __init__(self, nc):
        self.nc, self.ctx, self.held = nc, ExitStack(), []
        with nc.semaphore("lowest") as lowest:
            self.first = lowest.num

    def stage(self, prefix):
        def sem(name):
            self.held.append(self.ctx.enter_context(self.nc.semaphore(f"{prefix}_{name}", num=self.first + len(self.held))))
            return self.held[-1]
        return sem

    def clear(self):
        self.nc.all_engine_barrier(sems_to_clear=range(self.first, self.first + len(self.held)))
        self.ctx.close()
        self.held = []
        self.ctx = ExitStack()


def load_tokens(nc, b, sem, src, g, beside):
    rows_in, turned, copied = sem("rows_in"), sem("rows_turned"), sem("x_copied")
    with nc.Block() as block:
        @block.sync
        def _(sp):
            sp.dma_start(b.rows[:], src[bass.ds(g * TOK, TOK), :].rearrange("(t p) d -> p t d", p=128)).then_inc(rows_in, 16)

        @block.tensor
        def _(pe):
            beside.tensor(pe)
            pe.wait_ge(rows_in, 16)
            for t in range(TILES):
                ins = nc.tensor.transpose(bank(b, 0)[:, t * 128:(t + 1) * 128], b.rows[:, t, :], b.ident[:])
            ins.then_inc(turned, 1)

        @block.scalar
        def _(act):
            beside.scalar(act)

        @block.vector
        def _(dve):
            beside.vector(dve)
            dve.wait_ge(turned, 1)
            nc.vector.tensor_copy(b.x[:], bank(b, 0)).then_inc(copied, 1)


def store_tokens(nc, b, sem, dst, g, hand_over):
    turned, copied, rows_out = sem("out_turned"), sem("out_copied"), sem("rows_out")
    with nc.Block() as block:
        @block.sync
        def _(sp):
            sp.wait_ge(copied, 1)
            sp.dma_start(dst[bass.ds(g * TOK, TOK), :].rearrange("(t p) d -> p t d", p=128), b.rows[:]).then_inc(rows_out, 16)
            sp.wait_ge(rows_out, 16)

        @block.tensor
        def _(pe):
            for t in range(TILES):
                ins = nc.tensor.transpose(bank(b, 0)[:, t * 128:(t + 1) * 128], b.x_late[:, t * 128:(t + 1) * 128], b.ident[:])
            ins.then_inc(turned, 1)

        @block.vector
        def _(dve):
            dve.wait_ge(turned, 1)
            nc.vector.tensor_copy(b.rows[:], bank(b, 0).rearrange("p (t d) -> p t d", t=TILES)).then_inc(copied, 1)
            if hand_over:
                nc.vector.tensor_copy(b.x_late[:], b.x[:])


class Beside:

    def __init__(self, guest):
        self.guest = guest
        self.at = {"tensor": 0, "scalar": 0, "vector": 0, "gpsimd": 0}

    def steps(self, part, n, upto):
        first = self.at[part]
        last = max(first, upto) if upto else first + n
        last = min(last, self.guest.STEPS) if self.guest else first
        self.at[part] = last
        return range(first, last)

    def tensor(self, pe, n=1, upto=None):
        for k in self.steps("tensor", n, upto):
            self.guest.tensor(pe, k)

    def scalar(self, act, n=1, upto=None):
        for k in self.steps("scalar", n, upto):
            self.guest.scalar(act, k)

    def vector(self, dve, n=1, upto=None):
        for k in self.steps("vector", n, upto):
            self.guest.vector(dve, k)

    def gpsimd(self, pool, n=1, upto=None):
        for k in self.steps("gpsimd", n, upto):
            self.guest.gpsimd(pool, k)

    def rest(self, nc):
        if self.guest is None:
            return
        n = self.guest.STEPS
        with nc.Block() as block:
            @block.tensor
            def _(pe):
                self.tensor(pe, n)

            @block.scalar
            def _(act):
                self.scalar(act, n)

            @block.vector
            def _(dve):
                self.vector(dve, n)

            @block.gpsimd
            def _(pool):
                self.gpsimd(pool, n)


class Experts:

    BESIDE = ((5,), (6,), 7)
    ALONE = ((5, 0), (6, 1), 7)
    PRELUDE = 5
    STEPS = PRELUDE + PAIRS + 3

    def __init__(self, nc, b, sem, carve, alone):
        self.nc, self.b = nc, b
        self.ups, self.spreads, self.sum_bank = self.ALONE if alone else self.BESIDE
        self.turns = len(self.ups)
        (self.affinity, self.negated, self.chain, self.split, self.turned, self.copied) = (
            sem(n) for n in ("affinity_ready", "affinity_exp", "routing_steps", "routing_split", "split_turned", "split_copied"))
        (self.up, self.spread, self.tanh, self.silu, self.gated, self.down, self.done) = (
            sem(n) for n in ("up_ready", "weights_spread", "tanh_ready", "silu_ready", "gated_ready", "down_ready", "experts_done"))
        self.parts_t = [carve(TOK, BF16) for _ in range(2)]
        self.xn = carve(TOK)
        gates, self.tanh_h = carve(2 * TOK), [carve(TOK) for _ in range(self.turns)]
        self.gate_h = [gates[:, 0:TOK], gates[:, TOK:]]
        self.biased, self.rest, self.chosen, self.prob = (
            gates[:, n * TILES * EXPERTS:(n + 1) * TILES * EXPERTS].rearrange("p (t e) -> p t e", t=TILES) for n in range(4))
        self.parts = self.tanh_h[0].bitcast(BF16).rearrange("p (t e) -> p t e", t=TILES)
        self.top = carve(TILES * TOP_K).rearrange("p (t e) -> p t e", t=TILES)
        self.total, self.inverse = carve(TILES), carve(TILES)
        self.norm = Norm(nc, b, sem, (self.gate_h[0], self.gate_h[1], self.tanh_h[0]))
        self.aff = bank(b, self.spreads[0])[:, 0:TILES * EXPERTS].rearrange("p (t e) -> p t e", t=TILES)
        self.norm_banks = (self.ups[0], self.spreads[0])

    def tensor(self, pe, k):
        nc, b = self.nc, self.b
        p = k - self.PRELUDE
        UP, SPREAD, SUM = bank(b, self.ups[p % self.turns]), bank(b, self.spreads[p % self.turns]), bank(b, self.sum_bank)
        if k < 2:
            self.norm.tensor(pe, b.x_late[:], self.norm_banks, steps=(k,))
        elif k == 2:
            pe.wait_ge(self.norm.done, 1)
            for t in range(TILES):
                ins = nc.tensor.matmul(self.aff[:, t, :], self.xn[:, t * 128:(t + 1) * 128], b.centroids_t[:], start=True, stop=True)
            ins.then_inc(self.affinity, 1)
        elif k == 4:
            pe.wait_ge(self.split, 1)
            for half, out in enumerate((bank(b, self.ups[0]), SUM)):
                for t in range(TILES):
                    ins = nc.tensor.transpose(out.bitcast(BF16)[0:96, t * 128:(t + 1) * 128],
                                              self.parts[:, t, half * 128:half * 128 + 96], b.ident_bf[:])
            ins.then_inc(self.turned, 1)
        elif self.PRELUDE <= k <= self.PRELUDE + PAIRS + 1:
            if p == 0:
                pe.wait_ge(self.copied, 1)
            if self.turns <= p <= PAIRS:
                pe.wait_ge(self.gated, p - self.turns + 1)
            if p < PAIRS:
                nc.tensor.matmul(SPREAD, b.pair_sel[0:96, p % (PAIRS // 2)], self.parts_t[p // (PAIRS // 2)][0:96],
                                 start=True, stop=True).then_inc(self.spread, 1)
                nc.tensor.matmul(UP, b.w_up[:, p * 128:(p + 1) * 128], self.xn, start=True, stop=True).then_inc(self.up, 1)
            elif p == PAIRS:
                nc.tensor.matmul(UP[0:EF], b.ws_up[:], self.xn, start=True, stop=True).then_inc(self.up, 1)
            if 1 <= p <= PAIRS:
                pe.wait_ge(self.gated, p)
                nc.tensor.matmul(SUM, b.w_down[:, p - 1], self.gate_h[(p - 1) % 2], start=p == 1, stop=False).then_inc(self.down, 1)
            elif p == PAIRS + 1:
                pe.wait_ge(self.silu, PAIRS + 1)
                nc.tensor.matmul(SUM, b.ws_down[:], self.gate_h[PAIRS % 2][0:EF], start=False, stop=True).then_inc(self.down, 1)

    def scalar(self, act, k):
        nc, b = self.nc, self.b
        if k < 2:
            self.norm.scalar(act, self.norm_banks, steps=(k,))
        elif k == 2:
            act.wait_ge(self.chain, 1)
            nc.scalar.activation(self.prob[:], self.aff[:], ACT.Exp, scale=-1.0).then_inc(self.negated, 1)
        elif self.PRELUDE <= k <= self.PRELUDE + PAIRS:
            p = k - self.PRELUDE
            rows = 128 if p < PAIRS else EF
            act.wait_ge(self.up, p + 1)
            nc.scalar.activation(self.tanh_h[p % self.turns][0:rows], bank(b, self.ups[p % self.turns])[0:rows], ACT.Tanh, scale=0.5).then_inc(self.tanh, 1)

    def gpsimd(self, pool, k):
        pass

    def vector(self, dve, k):
        nc, b = self.nc, self.b
        v, E = nc.vector, EXPERTS
        spread_out = lambda ap: ap.unsqueeze(2).broadcast_to([128, TILES, E])
        if k < 2:
            self.norm.vector(dve, b.x_late[:], self.xn, self.norm_banks, steps=(k,))
        elif k == 2:
            self.steps = steps = Chain(dve, self.chain)
            dve.wait_ge(self.affinity, 1)
            steps.link(v.tensor_tensor(self.biased[:], self.aff[:], b.expert_bias[:].unsqueeze(1).broadcast_to([128, TILES, E]), ALU.add))
            for t in range(TILES):
                ins = v.max(self.top[:, t, :], self.biased[:, t, :])
            steps.link(ins)
            for t in range(TILES):
                ins = v.match_replace(self.rest[:, t, :], self.top[:, t, :], self.biased[:, t, :], NEG)
            steps.link(ins)
            steps.link(v.tensor_tensor(self.chosen[:], self.rest[:], self.biased[:], ALU.not_equal))
        elif k == 3:
            steps, prob, parts = self.steps, self.prob, self.parts
            dve.wait_ge(self.negated, 1)
            steps.link(v.tensor_scalar(prob[:], prob[:], 1.0, None, ALU.add))
            steps.link(v.reciprocal(prob[:], prob[:]))
            steps.link(v.tensor_tensor(prob[:], prob[:], self.chosen[:], ALU.mult))
            steps.link(v.tensor_reduce(self.total, prob[:], AX, ALU.add))
            steps.link(v.tensor_scalar(self.total, self.total, 1e-8, None, ALU.add))
            steps.link(v.reciprocal(self.inverse, self.total))
            steps.link(v.tensor_tensor(prob[:], prob[:], spread_out(self.inverse), ALU.mult))
            sides = prob.rearrange("p t (h e) -> p t h e", h=2)
            part = lambda n: parts.rearrange("p t (h e) -> p t h e", h=2)[:, :, :, n * 32:(n + 1) * 32]
            steps.link(v.tensor_copy(part(0), sides))
            steps.link(v.tensor_tensor(sides, sides, part(0), ALU.subtract))
            steps.link(v.tensor_copy(part(1), sides))
            steps.link(v.tensor_tensor(sides, sides, part(1), ALU.subtract))
            v.tensor_copy(part(2), sides).then_inc(self.split, 1)
        elif k == 4:
            dve.wait_ge(self.turned, 1)
            v.tensor_copy(self.parts_t[0][0:96], bank(b, self.ups[0]).bitcast(BF16)[0:96, 0:TOK])
            v.tensor_copy(self.parts_t[1][0:96], bank(b, self.sum_bank).bitcast(BF16)[0:96, 0:TOK]).then_inc(self.copied, 1)
        elif k <= self.PRELUDE + PAIRS:
            p = k - self.PRELUDE
            rows = 128 if p < PAIRS else EF
            h = self.gate_h[p % 2][0:rows]
            dve.wait_ge(self.tanh, p + 1)
            if p >= 2:
                dve.wait_ge(self.down, p - 1)
            v.scalar_tensor_tensor(out=h, in0=self.tanh_h[p % self.turns][0:rows], scalar=1.0, in1=bank(b, self.ups[p % self.turns])[0:rows],
                                   op0=ALU.add, op1=ALU.mult).then_inc(self.silu, 1)
            if p < PAIRS:
                dve.wait_ge(self.silu, p + 1)
                dve.wait_ge(self.spread, p + 1)
                v.tensor_tensor(h, h, bank(b, self.spreads[p % self.turns]), ALU.mult).then_inc(self.gated, 1)
        elif k == self.STEPS - 1:
            dve.wait_ge(self.down, PAIRS + 1)
            v.scalar_tensor_tensor(out=b.x_late[:], in0=bank(b, self.sum_bank), scalar=0.25, in1=b.x_late[:],
                                   op0=ALU.mult, op1=ALU.add).then_inc(self.done, 1)


def first_and_third(nc, b, sems, name, early, late, load=None, transfers=([], None)):
    carve = Carve(b)
    beside = Beside(Experts(nc, b, sems.stage(f"{name}_experts"), carve, alone=not early) if late else None)
    if load:
        load(beside)
    if early:
        ffn_stage(nc, b, sems.stage(f"{name}_ffn"), beside, carve.at, transfers)
    beside.rest(nc)
    sems.clear()


def second(nc, b, sems, scratch, early, late):
    carve = Carve(b)
    beside = Beside(StateSpace(nc, b, sems.stage("ssm"), carve, alone=not early) if late else None)
    if early:
        attn_stage(nc, b, sems.stage("attn"), scratch, beside, carve.at)
    beside.rest(nc)
    sems.clear()


class StateSpace:

    BANKS = (4, 5, 6, 7)
    PRELUDE = 6
    SCANS = 2 * STATES
    STEPS = PRELUDE + SCANS + 2 + 2

    def __init__(self, nc, b, sem, carve, alone):
        self.nc, self.b, self.alone = nc, b, alone
        self.padded, self.projected, self.z_ready, self.gate_ready = sem("conv_padded"), sem("projected"), sem("conv_input_ready"), sem("gate_ready")
        self.conv_steps, self.conv_ready, self.x_ready, self.mixed = sem("conv_steps"), sem("conv_ready"), sem("conv_output_ready"), sem("dt_b_c_ready")
        self.dt_in, self.exped, self.plus_one, self.logged = (
            sem("dt_input_ready"), sem("softplus_exp"), sem("softplus_sum"), sem("softplus_log"))
        self.act_steps, self.dt_ready, self.u_ready, self.split_steps, self.split_ready = (
            sem("scalar_steps"), sem("dt_ready"), sem("u_ready"), sem("split_steps"), sem("split_ready"))
        self.spread_b, self.spread_c, self.c_copied, self.decay, self.driven, self.scanned, self.weighted, self.added = (
            sem("b_spread"), sem("c_spread"), sem("c_copied"), sem("decay_ready"), sem("drive_ready"), sem("scanned"), sem("weighted_ready"), sem("state_added"))
        self.softplus_steps, self.gate_steps, self.y_ready, self.out = sem("softplus_steps"), sem("gate_steps"), sem("gated_ready"), sem("out_ready")
        chunked = lambda: carve(2 * TOK).rearrange("p (c n) -> p c n", c=2)
        self.gate, self.x_c, self.dt, self.u = (chunked() for _ in range(4))
        self.parts = carve(TOK, BF16)
        width = 1 + SEQ + 2
        early = carve(2 * GROUP_SEQS * width + 4 * TOK)
        at = 2 * GROUP_SEQS * width
        self.z = early[:, 0:at].rearrange("p (c s w) -> p c s w", c=2, s=GROUP_SEQS)
        self.conv, self.e = (early[:, at + n * 2 * TOK:at + (n + 1) * 2 * TOK].rearrange("p (c n) -> p c n", c=2) for n in range(2))
        self.w = early[:, 0:2 * TOK].rearrange("p (c n) -> p c n", c=2)
        self.bc, self.rest = self.u[:, 0], self.u[:, 1]
        self.high, self.mid = (self.e[:, 0, n * 256:(n + 1) * 256].bitcast(BF16) for n in range(2))
        self.xn = self.e[:, 1]
        self.norm = Norm(nc, b, sem, (self.conv[:, 0], self.conv[:, 1], self.e[:, 0]))
        self.sums, self.c_sb = (b.y[:], b.rows[:].rearrange("p t d -> p (t d)")), (b.cent[:], b.sq[:])
        self.decays = [early[:, n * TOK:(n + 1) * TOK] for n in range(2)]
        self.states = [early[:, n * TOK:(n + 1) * TOK] for n in range(2, 6)]

    def tensor(self, pe, k):
        nc, b = self.nc, self.b
        spread = lambda out, row: nc.tensor.matmul(out, b.fold32_bf[0:96, row:row + 1].broadcast_to([96, 128]), self.parts[0:96], start=True, stop=True)
        j = k - self.PRELUDE
        if k < 2:
            self.norm.tensor(pe, b.x_late[:], self.BANKS[0:2], steps=(k,))
        elif k == 2:
            pe.wait_ge(self.norm.done, 1)
            for c in range(4):
                nc.tensor.matmul(bank(b, self.BANKS[c]), b.in_w[:, c * 128:(c + 1) * 128], self.xn, start=True, stop=True).then_inc(self.projected, 1)
        elif k == 3:
            pe.wait_ge(self.gate_ready, 2)
        elif k == 4:
            pe.wait_ge(self.x_ready, 2)
            for i in range(2):
                ins = nc.tensor.matmul(bank(b, self.BANKS[0])[0:2 * STATES], b.bc_w[:, i], self.x_c[:, i], start=i == 0, stop=i == 1)
            ins.then_inc(self.mixed, 1)
            for c in range(2):
                if c == 1:
                    pe.wait_ge(self.split_steps, 1)
                for i in range(2):
                    ins = nc.tensor.matmul(bank(b, self.BANKS[1 - c]), b.dt_w[:, i, c * 128:(c + 1) * 128], self.x_c[:, i], start=i == 0, stop=i == 1)
                ins.then_inc(self.mixed, 1)
        elif 0 <= j < self.SCANS:
            if j == 0:
                pe.wait_ge(self.split_ready, 1)
                pe.wait_ge(self.dt_in, 1)
            if j % 2 == 0 and j < self.SCANS:
                n = j // 2
                if n >= 1:
                    pe.wait_ge(self.driven, 2 * n)
                spread(bank(b, self.BANKS[0]), n).then_inc(self.spread_b, 1)
                if n >= 1:
                    pe.wait_ge(self.c_copied, n)
                spread(bank(b, self.BANKS[1]), STATES + n).then_inc(self.spread_c, 1)
        elif k == self.STEPS - 2:
            for i in range(2):
                pe.wait_ge(self.y_ready, i + 1)
                ins = nc.tensor.matmul(bank(b, self.BANKS[0]), b.ssm_out_w[:, i], self.conv[:, i], start=i == 0, stop=i == 1)
            ins.then_inc(self.out, 1)

    def scalar(self, act, k):
        nc, b = self.nc, self.b
        j = k - self.PRELUDE
        if k < 2:
            self.norm.scalar(act, self.BANKS[0:2], steps=(k,))
        elif k == 2:
            act.wait_ge(self.padded, 1)
            for c in range(2):
                act.wait_ge(self.projected, c + 1)
                nc.scalar.activation(self.z[:, c, :, 1:1 + SEQ], bank(b, self.BANKS[c]).rearrange("p (s n) -> p s n", s=GROUP_SEQS), ACT.Identity,
                                     bias=vec(b, ("in_b", c))).then_inc(self.z_ready, 1)
            for c in range(2):
                act.wait_ge(self.projected, c + 3)
                nc.scalar.activation(self.gate[:, c], bank(b, self.BANKS[2 + c]), ACT.Silu, bias=vec(b, ("in_b", 2 + c))).then_inc(self.gate_ready, 1)
        elif k == 3:
            for c in range(2):
                act.wait_ge(self.conv_ready, c + 1)
                nc.scalar.activation(self.x_c[:, c], self.conv[:, c], ACT.Silu, bias=vec(b, ("conv_b", c))).then_inc(self.x_ready, 1)
        elif k == 4:
            steps = Chain(act, self.act_steps)
            act.wait_ge(self.dt_in, 1)
            steps.link(nc.scalar.activation(self.e, self.dt, ACT.Abs))
            nc.scalar.activation(self.e, self.e, ACT.Exp, scale=-1.0).then_inc(self.exped, 1)
        elif k == 5:
            act.wait_ge(self.plus_one, 1)
            act.wait_ge(self.split_ready, 1)
            nc.scalar.activation(self.u, self.w, ACT.Ln).then_inc(self.logged, 1)
        elif 0 <= j < self.SCANS:
            if j == 0:
                act.wait_ge(self.dt_ready, 1)
            if j >= 2:
                act.wait_ge(self.scanned, j - 1)
            if j % 2 == 0:
                n = j // 2
                act.wait_ge(self.spread_c, n + 1)
                if n >= 2:
                    act.wait_ge(self.weighted, 2 * (n - 1))
                nc.scalar.copy(self.c_sb[n % 2], bank(b, self.BANKS[1])).then_inc(self.c_copied, 1)
            nc.scalar.activation(self.decays[j % 2], self.dt[:, j % 2], ACT.Exp, scale=b.A[:, j % 2, j // 2:j // 2 + 1]).then_inc(self.decay, 1)

    def weight(self, queue, engine, i):
        queue.wait_ge(self.scanned, i + 1)
        queue.wait_ge(self.c_copied, i // 2 + 1)
        engine.tensor_tensor(self.states[i % 4], self.states[i % 4], self.c_sb[i // 2 % 2], ALU.mult).then_inc(self.weighted, 1)

    def gpsimd(self, pool, k):
        j = k - self.PRELUDE
        if k == 0:
            pool.memset(self.z[:, :, :, 0:1], 0.0)
            pool.memset(self.z[:, :, :, 1 + SEQ:], 0.0).then_inc(self.padded, 1)
        elif k == 5:
            for c in range(2):
                pool.memset(self.sums[c], 0.0).then_inc(self.added, 1)
        elif 2 <= j <= self.SCANS + 1:
            i = j - 2
            if not self.alone:
                self.weight(pool, pool, i)
            pool.wait_ge(self.weighted, i + 1)
            pool.wait_ge(self.added, i + 1)
            pool.tensor_tensor(self.sums[i % 2], self.sums[i % 2], self.states[i % 4], ALU.add).then_inc(self.added, 1)

    def vector(self, dve, k):
        nc, b = self.nc, self.b
        v = nc.vector
        j = k - self.PRELUDE
        if k < 2:
            self.norm.vector(dve, b.x_late[:], self.xn, self.BANKS[0:2], steps=(k,))
        elif k == 3:
            steps = Chain(dve, self.conv_steps)
            for c in range(2):
                dve.wait_ge(self.z_ready, c + 1)
                dst = self.conv[:, c].rearrange("p (s n) -> p s n", s=GROUP_SEQS)
                tap = lambda n: vec(b, ("conv_w", 2 * n + c))
                steps.link(v.tensor_scalar(dst, self.z[:, c, :, 0:SEQ], tap(0), None, ALU.mult))
                for n in range(1, CONV):
                    ins = v.scalar_tensor_tensor(out=dst, in0=self.z[:, c, :, n:n + SEQ], scalar=tap(n), in1=dst, op0=ALU.mult, op1=ALU.add)
                    if n < CONV - 1:
                        steps.link(ins)
                    else:
                        ins.then_inc(self.conv_ready, 1)
        elif k == 4:
            bc, rest, high, mid, parts = self.bc, self.rest, self.high, self.mid, self.parts
            split = Chain(dve, self.split_steps)
            dve.wait_ge(self.mixed, 1)
            s = slice(0, 2 * STATES)
            split.link(v.tensor_scalar(bc[s], bank(b, self.BANKS[0])[s], vec(b, ("bc_b", 0), 2 * STATES), None, ALU.add))
            split.link(v.tensor_copy(high[s], bc[s]))
            split.link(v.tensor_tensor(rest[s], bc[s], high[s], ALU.subtract))
            split.link(v.tensor_copy(mid[s], rest[s]))
            split.link(v.tensor_tensor(bc[s], rest[s], mid[s], ALU.subtract))
            v.tensor_copy(parts[0:32], high[s])
            v.tensor_copy(parts[32:64], mid[s])
            v.tensor_copy(parts[64:96], bc[s]).then_inc(self.split_ready, 1)
            dve.wait_ge(self.mixed, 3)
            for c in range(2):
                ins = v.tensor_scalar(self.dt[:, c], bank(b, self.BANKS[1 - c]), vec(b, ("dt_b", c)), None, ALU.add)
            ins.then_inc(self.dt_in, 1)
        elif k == 5:
            softplus = Chain(dve, self.softplus_steps)
            dve.wait_ge(self.exped, 1)
            v.tensor_scalar(self.w, self.e, 1.0, None, ALU.add).then_inc(self.plus_one, 1)
            dve.wait_ge(self.plus_one, 1)
            softplus.link(v.scalar_tensor_tensor(out=self.e, in0=self.w, scalar=-1.0, in1=self.e, op0=ALU.add, op1=ALU.subtract))
            softplus.link(v.scalar_tensor_tensor(out=self.dt, in0=self.dt, scalar=0.0, in1=self.e, op0=ALU.max, op1=ALU.subtract))
            dve.wait_ge(self.logged, 1)
            v.tensor_tensor(self.dt, self.dt, self.u, ALU.add).then_inc(self.dt_ready, 1)
            dve.wait_ge(self.dt_ready, 1)
            v.tensor_tensor(self.u, self.dt, self.x_c, ALU.mult).then_inc(self.u_ready, 1)
        elif 0 <= j <= self.SCANS + 1:
            if j == 0:
                dve.wait_ge(self.u_ready, 1)
            if 1 <= j <= self.SCANS:
                i = j - 1
                dve.wait_ge(self.driven, i + 1)
                dve.wait_ge(self.decay, i + 1)
                for q in range(GROUP_SEQS):
                    at = self.states[i % 4][:, q * SEQ:(q + 1) * SEQ]
                    ins = v.tensor_tensor_scan(at, self.decays[i % 2][:, q * SEQ:(q + 1) * SEQ], at, 0.0, ALU.mult, ALU.add)
                ins.then_inc(self.scanned, 1)
            if j < self.SCANS:
                dve.wait_ge(self.spread_b, j // 2 + 1)
                if j >= 4:
                    dve.wait_ge(self.added, 2 + j - 3)
                v.tensor_tensor(self.states[j % 4], self.u[:, j % 2], bank(b, self.BANKS[0]), ALU.mult).then_inc(self.driven, 1)
            if self.alone and j >= 2:
                self.weight(dve, v, j - 2)
        elif k == self.STEPS - 2:
            dve.wait_ge(self.added, 2 + self.SCANS)
            dve.wait_ge(self.gate_ready, 2)
            gated = Chain(dve, self.gate_steps)
            for c in range(2):
                gated.link(v.scalar_tensor_tensor(out=self.conv[:, c], in0=self.x_c[:, c], scalar=vec(b, ("Dp", c)), in1=self.sums[c],
                                                  op0=ALU.mult, op1=ALU.add))
                v.tensor_tensor(self.conv[:, c], self.conv[:, c], self.gate[:, c], ALU.mult).then_inc(self.y_ready, 1)
        elif k == self.STEPS - 1:
            dve.wait_ge(self.out, 1)
            v.scalar_tensor_tensor(out=b.x_late[:], in0=bank(b, self.BANKS[0]), scalar=vec(b, ("ssm_out_b", 0)), in1=b.x_late[:], op0=ALU.add, op1=ALU.add)


def attn_stage(nc, b, sem, scratch, beside, space):
    norm = Norm(nc, b, sem)
    v_ready, v_copied_a, v_copied_v = sem("v_ready"), sem("v_copied_scalar"), sem("v_copied_vector")
    q_ready, k_ready, q_biased, k_copied = sem("q_ready"), sem("k_ready"), sem("q_biased"), sem("k_copied")
    p_ready, p_copied, p_stored, p_loaded = sem("distance_scores_ready"), sem("distance_scores_copied"), sem("distance_scores_stored"), sem("position_scores_loaded")
    s_ready, summed, maxed, exped, inverted, normed = (sem("scores_ready"), sem("scores_summed"), sem("scores_maxed"), sem("scores_exped"),
                                                       sem("sums_inverted"), sem("probs_normed"))
    turned, t_copied, o_ready, o_copied, projected = sem("probs_turned"), sem("probs_copied"), sem("heads_ready"), sem("heads_copied"), sem("projected")
    carve = Carve(b)
    carve.at = space
    v_sb = carve(TILES * AH * AD).rearrange("p (t n) -> p t n", t=TILES)
    two = lambda n: [carve(n) for _ in range(2)]
    q_e, q_p, k_t = two(TOK), carve(TOK), two(TOK)
    pos = carve(TILES * SEQ).rearrange("p (t k) -> p t k", t=TILES)
    probs = [t.rearrange("p (t k) -> p t k", t=TILES) for t in two(TILES * SEQ)]
    dist = carve(TILES * 384).rearrange("p (t k) -> p t k", t=TILES)
    probs_t = carve(GROUP_SEQS * 2 * SEQ).rearrange("p (s c q) -> p s c q", s=GROUP_SEQS, c=2)
    o_t = carve(TOK)
    neg_max, sums, inv = (carve(2 * TILES).rearrange("p (a t) -> p a t", a=2) for _ in range(3))
    half = AH * AD // 2
    DIST_BANKS, SCORE_BANKS, TURN_BANKS = (2, 0, 1, 2), (6, 7), (1, 0)
    ROUNDS = AH + 2

    def shifted(slot):
        return bass.AP(tensor=scratch.tensor, offset=slot * TILES * 128 * 384 + 127,
                       ap=[[383, 128], [128 * 384, TILES], [1, SEQ]])

    with nc.Block() as block:
        @block.tensor
        def _(pe):
            norm.tensor(pe, b.x[:], (0, 1), steps=(0,))
            beside.tensor(pe)
            norm.tensor(pe, b.x[:], (0, 1), steps=(1,))
            beside.tensor(pe)
            pe.wait_ge(norm.done, 1)
            for n in range(2 * TILES):
                if n == 4:
                    beside.tensor(pe)
                if n >= 4:
                    pe.wait_ge(v_copied_v if n % 2 else v_copied_a, (n - 4) // 2 + 1)
                t, side = n // 2, n % 2
                nc.tensor.matmul(bank(b, n % 4), b.xn[:, t * 128:(t + 1) * 128], b.wv[:, side * half:(side + 1) * half],
                                 start=True, stop=True).then_inc(v_ready, 1)
            beside.tensor(pe)
            pe.wait_ge(v_copied_a, TILES)
            pe.wait_ge(v_copied_v, TILES)

            def heads(h):
                pe.wait_ge(t_copied, GROUP_SEQS * (h + 1))
                for s in range(GROUP_SEQS):
                    for c in range(2):
                        ins = nc.tensor.matmul(bank(b, 1)[:, s * SEQ:(s + 1) * SEQ], v_sb[:, 2 * s + c, h * AD:(h + 1) * AD],
                                               probs_t[:, s, c], start=c == 0, stop=c == 1)
                ins.then_inc(o_ready, 1)

            def project(h):
                pe.wait_ge(o_copied, h + 1)
                nc.tensor.matmul(bank(b, 3), b.w_out[:, h], o_t, start=h == 0, stop=h == AH - 1).then_inc(projected, 1)

            def queries_keys(h):
                w = slice(h * AD, (h + 1) * AD)
                if h >= 2:
                    pe.wait_ge(summed, GROUP_SEQS * (h - 1))
                elif h == 1:
                    pe.wait_ge(k_copied, 1)
                nc.tensor.matmul(bank(b, 6), b.wq[:, w], b.xn[:], start=True, stop=True).then_inc(q_ready, 1)
                nc.tensor.matmul(bank(b, 7), b.wk[:, w], b.xn[:], start=True, stop=True).then_inc(k_ready, 1)

            def distances(h, tiles):
                pe.wait_ge(q_biased, h + 1)
                if h >= 1:
                    pe.wait_ge(p_copied, TILES * h)
                for t in tiles:
                    if t == 3:
                        pe.wait_ge(p_copied, TILES * h + 1)
                    first = 128 if t % 2 == 0 else 0
                    nc.tensor.matmul(bank(b, DIST_BANKS[t])[:, 0:384], q_p[:, t * 128:(t + 1) * 128],
                                     b.rel_k[:, h, first:first + 384], start=True, stop=True).then_inc(p_ready, 1)

            def scores(h):
                pe.wait_ge(k_copied, h + 1)
                for s in range(GROUP_SEQS):
                    for t in range(2):
                        at = (2 * s + t) * 128
                        ins = nc.tensor.matmul(bank(b, SCORE_BANKS[s])[:, t * SEQ:(t + 1) * SEQ], q_e[h % 2][:, at:at + 128],
                                               k_t[h % 2][:, s * SEQ:(s + 1) * SEQ], start=True, stop=True)
                    ins.then_inc(s_ready, 1)

            def turn(h, s):
                if h + 2 < AH:
                    pe.wait_ge(p_copied, TILES * (h + 2) + 3 - s)
                pe.wait_ge(normed, GROUP_SEQS * h + s + 1)
                for t in range(2):
                    for c in range(2):
                        ins = nc.tensor.transpose(bank(b, TURN_BANKS[s])[:, c * SEQ + t * 128:c * SEQ + (t + 1) * 128],
                                                  probs[h % 2][:, 2 * s + t, c * 128:(c + 1) * 128], b.ident[:])
                ins.then_inc(turned, 1)

            queries_keys(0)
            beside.tensor(pe)
            distances(0, (0, 1, 2, 3))
            beside.tensor(pe)
            for i in range(ROUNDS):
                if 1 <= i <= AH:
                    scores(i - 1)
                if i >= 2:
                    turn(i - 2, 0)
                    turn(i - 2, 1)
                beside.tensor(pe)
                if i + 1 < AH:
                    queries_keys(i + 1)
                beside.tensor(pe)
                if i >= 2:
                    heads(i - 2)
                if i + 1 < AH:
                    distances(i + 1, (0, 1))
                beside.tensor(pe)
                if i >= 2:
                    project(i - 2)
                if i + 1 < AH:
                    distances(i + 1, (2, 3))
                beside.tensor(pe)

        @block.sync
        def _(sp):
            for h in range(AH):
                slot = h % 2
                sp.wait_ge(p_copied, TILES * (h + 1))
                if h >= 2:
                    sp.wait_ge(p_loaded, 16 * (h - 1))
                sp.dma_start(scratch[slot].rearrange("t p k -> p t k"), dist).then_inc(p_stored, 16)
                sp.wait_ge(p_stored, 16 * (h + 1))
                if h >= 1:
                    sp.wait_ge(summed, GROUP_SEQS * h)
                sp.dma_start(pos, shifted(slot)).then_inc(p_loaded, 16)

        @block.gpsimd
        def _(pool):
            beside.gpsimd(pool, StateSpace.STEPS)

        @block.scalar
        def _(act):
            norm.scalar(act, (0, 1), steps=(0,))
            beside.scalar(act)
            norm.scalar(act, (0, 1), steps=(1,))
            beside.scalar(act)
            for n in range(0, 2 * TILES, 2):
                if n == 4:
                    beside.scalar(act)
                act.wait_ge(v_ready, n + 1)
                nc.scalar.copy(v_sb[:, n // 2, 0:half], bank(b, n % 4)).then_inc(v_copied_a, 1)
            beside.scalar(act)

            def queries_keys(h):
                act.wait_ge(q_ready, h + 1)
                if h >= 1:
                    act.wait_ge(p_ready, TILES * h)
                if h >= 2:
                    act.wait_ge(s_ready, GROUP_SEQS * (h - 1))
                scale = AD ** -0.5
                nc.scalar.activation(q_p, bank(b, 6), ACT.Identity, bias=vec(b, ("rel_pos", h)), scale=scale)
                nc.scalar.activation(q_e[h % 2], bank(b, 6), ACT.Identity, bias=vec(b, ("rel_embed", h)), scale=scale).then_inc(q_biased, 1)
                act.wait_ge(k_ready, h + 1)
                nc.scalar.copy(k_t[h % 2], bank(b, 7)).then_inc(k_copied, 1)

            def distances(h, tiles):
                if h >= 1:
                    act.wait_ge(p_stored, 16 * h)
                for t in tiles:
                    act.wait_ge(p_ready, h * TILES + t + 1)
                    nc.scalar.copy(dist[:, t, :], bank(b, DIST_BANKS[t])[:, 0:384]).then_inc(p_copied, 1)

            def exps(h):
                for s in range(GROUP_SEQS):
                    act.wait_ge(maxed, GROUP_SEQS * h + s + 1)
                    for t in range(2 * s, 2 * s + 2):
                        ins = nc.scalar.activation(probs[h % 2][:, t, :], probs[h % 2][:, t, :], ACT.Exp, bias=neg_max[:, h % 2, t:t + 1],
                                                   accum_out=sums[:, h % 2, t:t + 1])
                    ins.then_inc(exped, 1)

            def normalise(h):
                act.wait_ge(inverted, h + 1)
                for s in range(GROUP_SEQS):
                    for t in range(2 * s, 2 * s + 2):
                        ins = nc.scalar.activation(probs[h % 2][:, t, :], probs[h % 2][:, t, :], ACT.Identity, scale=inv[:, h % 2, t:t + 1])
                    ins.then_inc(normed, 1)

            queries_keys(0)
            beside.scalar(act)
            distances(0, (0, 1, 2, 3))
            beside.scalar(act)
            for i in range(ROUNDS):
                if 1 <= i <= AH:
                    exps(i - 1)
                if i + 1 < AH:
                    queries_keys(i + 1)
                beside.scalar(act, 2)
                if i + 1 < AH:
                    distances(i + 1, (0, 1))
                beside.scalar(act)
                if i + 1 < AH:
                    distances(i + 1, (2, 3))
                if 1 <= i <= AH:
                    normalise(i - 1)
                beside.scalar(act)

        @block.vector
        def _(dve):
            v = nc.vector
            norm.vector(dve, b.x[:], b.xn[:], (0, 1), steps=(0,))
            beside.vector(dve)
            norm.vector(dve, b.x[:], b.xn[:], (0, 1), steps=(1,))
            beside.vector(dve)
            for n in range(1, 2 * TILES, 2):
                if n == 5:
                    beside.vector(dve)
                dve.wait_ge(v_ready, n + 1)
                v.tensor_copy(v_sb[:, n // 2, half:], bank(b, n % 4)).then_inc(v_copied_v, 1)
            beside.vector(dve)

            def sums_and_maxima(h):
                dve.wait_ge(p_loaded, 16 * (h + 1))
                if h >= 2:
                    dve.wait_ge(turned, GROUP_SEQS * (h - 1))
                for s in range(GROUP_SEQS):
                    n = GROUP_SEQS * h + s
                    dve.wait_ge(s_ready, n + 1)
                    pair = probs[h % 2][:, 2 * s:2 * s + 2, :]
                    v.tensor_tensor(pair, bank(b, SCORE_BANKS[s]).rearrange("p (t k) -> p t k", t=2),
                                    pos[:, 2 * s:2 * s + 2, :], ALU.add).then_inc(summed, 1)
                    dve.wait_ge(summed, n + 1)
                    v.tensor_reduce(neg_max[:, h % 2, 2 * s:2 * s + 2], pair, AX, ALU.max, negate=True).then_inc(maxed, 1)

            def copy_turned(h, s):
                dve.wait_ge(turned, GROUP_SEQS * h + s + 1)
                if h >= 1:
                    dve.wait_ge(o_ready, h)
                v.tensor_copy(probs_t[:, s], bank(b, TURN_BANKS[s]).rearrange("p (c q) -> p c q", c=2)).then_inc(t_copied, 1)

            beside.vector(dve, 2)
            for i in range(ROUNDS):
                if 1 <= i <= AH:
                    sums_and_maxima(i - 1)
                if i >= 2:
                    copy_turned(i - 2, 0)
                    copy_turned(i - 2, 1)
                beside.vector(dve)
                if 1 <= i <= AH:
                    dve.wait_ge(exped, GROUP_SEQS * i)
                    v.reciprocal(inv[:, (i - 1) % 2], sums[:, (i - 1) % 2]).then_inc(inverted, 1)
                if i >= 2:
                    dve.wait_ge(o_ready, i - 1)
                    if i >= 3:
                        dve.wait_ge(projected, i - 2)
                    v.tensor_copy(o_t, bank(b, 1)).then_inc(o_copied, 1)
                beside.vector(dve, 3)
            dve.wait_ge(projected, AH)
            v.scalar_tensor_tensor(out=b.x[:], in0=bank(b, 3), scalar=vec(b, ("b_out", 0)), in1=b.x[:], op0=ALU.add, op1=ALU.add)


def norm_block(nc, b, sem, src, dst, beside):
    norm = Norm(nc, b, sem)
    with nc.Block() as block:
        @block.tensor
        def _(pe):
            norm.tensor(pe, src, (0, 1), steps=(0,))
            beside.tensor(pe, upto=2)
            norm.tensor(pe, src, (0, 1), steps=(1,))
            beside.tensor(pe, upto=3)

        @block.scalar
        def _(act):
            norm.scalar(act, (0, 1), steps=(0,))
            beside.scalar(act, upto=2)
            norm.scalar(act, (0, 1), steps=(1,))
            beside.scalar(act, upto=3)

        @block.vector
        def _(dve):
            norm.vector(dve, src, dst, (0, 1), steps=(0,))
            beside.vector(dve, upto=2)
            norm.vector(dve, src, dst, (0, 1), steps=(1,))
            beside.vector(dve, upto=3)


def ffn_stage(nc, b, stage_sem, beside, space, transfers):
    prefixed = lambda prefix: (lambda name: stage_sem(f"{prefix}_{name}"))
    norm_block(nc, b, prefixed("entry"), b.x[:], b.y[:], beside)
    for l in range(DEPTH):
        ffn_layer(nc, b, prefixed(f"layer{l}"), l, beside, space, transfers if l == 0 else ([], None))


def ffn_layer(nc, b, sem, l, beside, space, transfers):
    norm = Norm(nc, b, sem)
    shifted, qk_ready, v_ready, qk_copied, v_copied = sem("shifted"), sem("qk_ready"), sem("v_ready"), sem("qk_copied"), sem("v_copied")
    squared, summed, clipped, inv_norm = sem("qk_squared"), sem("squares_summed"), sem("sums_clipped"), sem("inverse_norms")
    split, k_split, added, k_added, rotated, zeroed = (sem("query_parts_ready"), sem("key_parts_ready"), sem("query_parts_added"),
                                                       sem("key_parts_added"), sem("rotated"), sem("weights_zeroed"))
    qk_turned, q_copied, k_copied = sem("qk_turned"), sem("q_copied"), sem("k_copied")
    s_ready, maxed, exped, p_turned = sem("scores_ready"), sem("scores_maxed"), sem("scores_exped"), sem("probs_turned")
    p_copied_a, p_copied_v = sem("probs_copied_scalar"), sem("probs_copied_vector")
    o_ready, inverted, scaled, o_turned = sem("heads_ready"), sem("sums_inverted"), sem("heads_scaled"), sem("heads_turned")
    o_copied_a, o_copied_v = sem("heads_copied_scalar"), sem("heads_copied_vector")
    mixed, y_ready, affine, hidden, gelu, gated, out = (sem("mixed"), sem("y_ready"), sem("affine_done"), sem("hidden_ready"),
                                                        sem("gelu_ready"), sem("gated"), sem("down_ready"))
    carve = Carve(b)
    carve.at = space
    h_t = b.xn[:]
    h3 = h_t.rearrange("p (s n) -> p s n", s=GROUP_SEQS)
    y3 = b.y[:].rearrange("p (s n) -> p s n", s=GROUP_SEQS)
    two = lambda n: [carve(n) for _ in range(2)]
    q_t, k_t = (carve(4 * TOK).rearrange("p (j n) -> p j n", j=4) for _ in range(2))
    v_sb = carve(TILES * INNER).rearrange("p (t n) -> p t n", t=TILES)
    raw_all = carve(4 * INNER)
    raw = [raw_all[:, 0:2 * INNER], raw_all[:, 2 * INNER:]]
    squares, cosine, sine_all = carve(2 * INNER), two(2 * INNER), carve(4 * INNER)
    sine = [sine_all[:, 0:2 * INNER], sine_all[:, 2 * INNER:]]
    probs_near = [t.rearrange("p (h k) -> p h k", h=4) for t in two(4 * 128)]
    probs_wide = [t.rearrange("p (h k) -> p h k", h=4) for t in two(4 * SEQ)]
    lens = two(16)
    neg_max, sums = (carve(TILES * LH).rearrange("p (t h) -> p t h", t=TILES) for _ in range(2))
    probs_t = [t.rearrange("p (h c q) -> p h c q", h=4, c=2) for t in cosine]
    heads = sine_all.rearrange("p (t n) -> p t n", t=TILES)
    o_t = raw_all.rearrange("p (j n) -> p j n", j=4)
    gelu_t, gated_t = q_t, k_t
    UNITS = 2 * TILES
    SLOT_HEADS = (0, 2, 1, 3)

    def span(t):
        return (0, 128) if t % 2 == 0 else (64, 192)

    score_banks = bank(b, 0, 2).rearrange("p (h k) -> p h k", h=4)

    def prob_of(u):
        return (probs_wide if (u // 2) % 2 else probs_near)[u % 2]

    with nc.Block() as block:
        @block.sync
        def _(sp):
            for dst, src in transfers[0]:
                sp.dma_start(dst, src).then_inc(transfers[1], 16)

        @block.tensor
        def _(pe):
            w = b.wqkv[:, l]
            pe.wait_ge(shifted, 1)

            def project(t):
                lhs = h_t[:, t * 128:(t + 1) * 128]
                if t >= 1:
                    pe.wait_ge(qk_copied, t)
                nc.tensor.matmul(bank(b, 0), lhs, w[:, 0:INNER], start=True, stop=True)
                nc.tensor.matmul(bank(b, 1), lhs, w[:, INNER:2 * INNER], start=True, stop=True).then_inc(qk_ready, 1)
                if t >= 1:
                    pe.wait_ge(v_copied, t)
                nc.tensor.matmul(bank(b, 2), lhs, w[:, 2 * INNER:], start=True, stop=True).then_inc(v_ready, 1)

            def turn(t):
                pe.wait_ge(rotated, t + 1)
                if t >= 1:
                    pe.wait_ge(q_copied, t)
                    pe.wait_ge(k_copied, t)
                for j in range(8):
                    ins = nc.tensor.transpose(bank(b, 3 + j // 4)[:, (j % 4) * 128:(j % 4 + 1) * 128],
                                              cosine[t % 2][:, j * 128:(j + 1) * 128], b.ident[:])
                ins.then_inc(qk_turned, 1)

            project(0)
            beside.tensor(pe)
            for t in range(TILES):
                if t + 1 < TILES:
                    project(t + 1)
                beside.tensor(pe, 2 if t == 3 else 1)
                turn(t)

            def scores(u):
                t, half = u // 2, u % 2
                first, n = span(t)
                if u == 0:
                    pe.wait_ge(qk_copied, TILES)
                else:
                    pe.wait_ge(exped, u)
                keys = (t // 2) * SEQ + first
                mask = b.mask_bf[:, 0:128] if t % 2 == 0 else b.mask_bf[:, 128:320]
                for k in range(2):
                    nc.tensor.matmul(score_banks[:, 2 * k:2 * k + 2, first:first + n], b.ident_bf[:],
                                     mask.unsqueeze(1).broadcast_to([128, 2, n]), start=True, stop=False)
                for i in (0, 2, 1, 3):
                    head = 4 * half + SLOT_HEADS[i]
                    rows = slice(64 * (head % 2), 64 * (head % 2) + 64)
                    ins = nc.tensor.matmul(score_banks[:, i, first:first + n], q_t[rows, head // 2, t * 128:(t + 1) * 128],
                                           k_t[rows, head // 2, keys:keys + n], start=False, stop=i % 2 == 1)
                ins.then_inc(s_ready, 1)

            def turn_probs(u):
                t = u // 2
                pe.wait_ge(exped, u + 1)
                if u == 0:
                    pe.wait_ge(v_copied, TILES)
                else:
                    pe.wait_ge(p_copied_a, u)
                    pe.wait_ge(p_copied_v, u)
                for i in range(4):
                    for c in range(1 + t % 2):
                        at = (i % 2) * 256 + c * 128
                        ins = nc.tensor.transpose(bank(b, 2 + i // 2)[:, at:at + 128], prob_of(u)[:, i, c * 128:(c + 1) * 128], b.ident[:])
                ins.then_inc(p_turned, 1)

            def values(u):
                t, half = u // 2, u % 2
                pe.wait_ge(p_copied_a, u + 1)
                pe.wait_ge(p_copied_v, u + 1)
                if half == 0 and t >= 1:
                    pe.wait_ge(scaled, t)
                chunks = 1 + t % 2
                for i in range(4):
                    head = 4 * half + SLOT_HEADS[i]
                    for c in range(chunks):
                        ins = nc.tensor.matmul(bank(b, 4)[:, head * LD:(head + 1) * LD], probs_t[u % 2][:, i, c],
                                               v_sb[:, 2 * (t // 2) + c, head * LD:(head + 1) * LD], start=c == 0, stop=c == chunks - 1)
                ins.then_inc(o_ready, 1)

            pe.wait_ge(q_copied, TILES)
            pe.wait_ge(k_copied, TILES)
            scores(0)
            for u in range(UNITS + 1):
                if u < UNITS:
                    beside.tensor(pe)
                    turn_probs(u)
                if u + 1 < UNITS:
                    scores(u + 1)
                if u >= 1:
                    values(u - 1)
            for t in range(TILES):
                pe.wait_ge(scaled, t + 1)
                for j in range(4):
                    ins = nc.tensor.transpose(bank(b, t)[:, j * 128:(j + 1) * 128], heads[:, t, j * 128:(j + 1) * 128], b.ident[:])
                ins.then_inc(o_turned, 1)
            beside.tensor(pe)
            pe.wait_ge(o_copied_a, 2)
            pe.wait_ge(o_copied_v, 2)
            for j in range(4):
                ins = nc.tensor.matmul(bank(b, 4), b.wo[:, l, j], o_t[:, j], start=j == 0, stop=j == 3)
            ins.then_inc(mixed, 1)
            beside.tensor(pe)
            pe.wait_ge(shifted, 2)
            norm.tensor(pe, h_t, (0, 1), steps=(0,))
            beside.tensor(pe)
            norm.tensor(pe, h_t, (0, 1), steps=(1,))
            beside.tensor(pe)
            pe.wait_ge(affine, 1)
            for n in range(6):
                at, rows = HC[n // 2]
                first = at + (HID if n % 2 == 0 else 0)
                if n == 5:
                    pe.wait_ge(gelu, 1)
                nc.tensor.matmul(bank(b, n % 5)[0:rows], b.w1[:, l, first:first + rows], b.sq[:], start=True, stop=True).then_inc(hidden, 1)
            beside.tensor(pe)
            for c in range(3):
                rows = HC[c][1]
                pe.wait_ge(gated, c + 1)
                ins = nc.tensor.matmul(bank(b, 1), b.w2[0:rows, l, c], gated_t[0:rows, c], start=c == 0, stop=c == 2)
            ins.then_inc(out, 1)

        @block.scalar
        def _(act):
            s = nc.scalar
            for t in range(TILES + 1):
                if t < TILES:
                    act.wait_ge(qk_ready, t + 1)
                    if t >= 2:
                        act.wait_ge(split, t - 1)
                    s.copy(raw[t % 2], bank(b, 0, 2)).then_inc(qk_copied, 1)
                    act.wait_ge(qk_copied, t + 1)
                    if t >= 1:
                        act.wait_ge(summed, t)
                    s.activation(squares, raw[t % 2], ACT.Square).then_inc(squared, 1)
                    act.wait_ge(v_ready, t + 1)
                    s.copy(v_sb[:, t], bank(b, 2)).then_inc(v_copied, 1)
                if t == 0:
                    beside.scalar(act)
                else:
                    beside.scalar(act, 2 if t == 4 else 1)
                    at = slice((t - 1) * 128, t * 128)
                    act.wait_ge(qk_turned, t)
                    s.copy(q_t[:, :, at], bank(b, 3).rearrange("p (j n) -> p j n", j=4)).then_inc(q_copied, 1)
                    s.copy(k_t[:, :, at], bank(b, 4).rearrange("p (j n) -> p j n", j=4)).then_inc(k_copied, 1)

            def exps(u):
                t, half = u // 2, u % 2
                first, n = span(t)
                act.wait_ge(maxed, u + 1)
                if u >= 2:
                    act.wait_ge(p_turned, u - 1)
                for i in range(4):
                    head = 4 * half + SLOT_HEADS[i]
                    ins = s.activation(prob_of(u)[:, i, first:first + n], score_banks[:, i, first:first + n], ACT.Exp,
                                       bias=neg_max[:, t, 4 * half + i:4 * half + i + 1], accum_out=sums[:, t, head:head + 1])
                ins.then_inc(exped, 1)

            def copy_probs(u):
                act.wait_ge(p_turned, u + 1)
                if u >= 2:
                    act.wait_ge(o_ready, u - 1)
                c = 1 + (u // 2) % 2
                s.copy(probs_t[u % 2][:, 0:2, 0:c], bank(b, 2).rearrange("p (h c q) -> p h c q", h=2, c=2)[:, :, 0:c]).then_inc(p_copied_a, 1)

            act.wait_ge(zeroed, 1)
            exps(0)
            for u in range(UNITS + 1):
                if u < UNITS:
                    beside.scalar(act)
                    copy_probs(u)
                if u + 1 < UNITS:
                    exps(u + 1)
            for t in (0, 2):
                act.wait_ge(o_turned, t + 1)
                s.copy(o_t[:, :, t * 128:(t + 1) * 128], bank(b, t).rearrange("p (j n) -> p j n", j=4)).then_inc(o_copied_a, 1)
            beside.scalar(act, 2)
            norm.scalar(act, (0, 1), steps=(0,))
            beside.scalar(act)
            norm.scalar(act, (0, 1), steps=(1,))
            beside.scalar(act)
            for c in range(3):
                rows = HC[c][1]
                act.wait_ge(hidden, 2 * c + 1)
                s.activation(gelu_t[0:rows, c], bank(b, 2 * c)[0:rows], ACT.Gelu, bias=vec(b, (("b1_gate", c), l), rows)).then_inc(gelu, 1)
            beside.scalar(act)

        @block.gpsimd
        def _(pool):
            pool.memset(probs_wide[0][:, :, 0:64], 0.0)
            pool.memset(probs_wide[1][:, :, 0:64], 0.0).then_inc(zeroed, 1)
            for t in range(TILES):
                pool.wait_ge(summed, t + 1)
                pool.tensor_scalar(lens[t % 2], lens[t % 2], 1e-24, None, ALU.max).then_inc(clipped, 1)
                pool.wait_ge(clipped, t + 1)
                pool.tensor_tensor(lens[t % 2], lens[t % 2], b.minus_half[:].broadcast_to([128, 16]), ALU.pow).then_inc(inv_norm, 1)
                pool.wait_ge(split, t + 1)
                pool.tensor_tensor(cosine[t % 2][:, 0:INNER], cosine[t % 2][:, 0:INNER], sine[t % 2][:, 0:INNER], ALU.add).then_inc(added, 1)
                pool.wait_ge(added, t + 1)
                pool.wait_ge(k_added, t + 1)
                pool.wait_ge(inv_norm, t + 1)
                both = cosine[t % 2].rearrange("p (h d) -> p h d", d=LD)
                pool.tensor_tensor(both, both, lens[t % 2].unsqueeze(2).broadcast_to([128, 16, LD]), ALU.mult).then_inc(rotated, 1)

        @block.vector
        def _(dve):
            v = nc.vector

            def shift():
                v.tensor_copy(h3[0:64], y3[0:64])
                v.memset(h3[64:128, :, 0:1], 0.0)
                v.tensor_copy(h3[64:128, :, 1:], y3[64:128, :, :SEQ - 1]).then_inc(shifted, 1)

            shift()
            if l == 0:
                beside.vector(dve)
            for t in range(TILES + 1):
                if t < TILES:
                    s = t % 2
                    dve.wait_ge(squared, t + 1)
                    if t >= 2:
                        dve.wait_ge(rotated, t - 1)
                    v.tensor_reduce(lens[t % 2], squares.rearrange("p (h d) -> p h d", d=LD), AX, ALU.add).then_inc(summed, 1)
                if t >= 1:
                    beside.vector(dve, 2 if t == 4 else 1)
                elif l > 0:
                    beside.vector(dve)
                if t < TILES:
                    if t >= 2:
                        dve.wait_ge(qk_turned, t - 1)
                    for k in (1, 0):
                        r8, c8, s8 = (x[t % 2][:, k * INNER:(k + 1) * INNER].rearrange("p (h d) -> p h d", d=LD) for x in (raw, cosine, sine))
                        table = lambda n, x0, x1: b.rope_w[:, l, n, s, x0:x1].unsqueeze(1).broadcast_to([128, LH, x1 - x0])
                        v.tensor_tensor(c8, r8, table(2 * k, 0, LD), ALU.mult)
                        v.tensor_tensor(s8[:, :, 0:32], r8[:, :, 32:64], table(2 * k + 1, 0, 32), ALU.mult)
                        ins = v.tensor_tensor(s8[:, :, 32:64], r8[:, :, 0:32], table(2 * k + 1, 32, 64), ALU.mult)
                        ins.then_inc(split if k == 0 else k_split, 1)
                    dve.wait_ge(k_split, t + 1)
                    keys = slice(INNER, 2 * INNER)
                    v.tensor_tensor(cosine[t % 2][:, keys], cosine[t % 2][:, keys], sine[t % 2][:, keys], ALU.add).then_inc(k_added, 1)

            def maxima(u):
                t, half = u // 2, u % 2
                first, n = span(t)
                dve.wait_ge(s_ready, u + 1)
                v.tensor_reduce(neg_max[:, t, 4 * half:4 * half + 4], score_banks[:, :, first:first + n], AX, ALU.max, negate=True).then_inc(maxed, 1)

            def copy_probs(u):
                dve.wait_ge(p_turned, u + 1)
                if u >= 2:
                    dve.wait_ge(o_ready, u - 1)
                c = 1 + (u // 2) % 2
                v.tensor_copy(probs_t[u % 2][:, 2:4, 0:c], bank(b, 3).rearrange("p (h c q) -> p h c q", h=2, c=2)[:, :, 0:c]).then_inc(p_copied_v, 1)

            def scale_heads(t):
                dve.wait_ge(o_ready, 2 * t + 2)
                v.reciprocal(sums[:, t], sums[:, t]).then_inc(inverted, 1)
                dve.wait_ge(inverted, t + 1)
                v.tensor_tensor(heads[:, t].rearrange("p (h d) -> p h d", d=LD), bank(b, 4).rearrange("p (h d) -> p h d", d=LD),
                                sums[:, t].unsqueeze(2).broadcast_to([128, LH, LD]), ALU.mult).then_inc(scaled, 1)

            maxima(0)
            for u in range(UNITS + 1):
                if u < UNITS:
                    beside.vector(dve)
                    copy_probs(u)
                if u + 1 < UNITS:
                    maxima(u + 1)
                if u % 2 == 0 and u >= 2:
                    scale_heads((u - 2) // 2)
            for t in (1, 3):
                dve.wait_ge(o_turned, t + 1)
                v.tensor_copy(o_t[:, :, t * 128:(t + 1) * 128], bank(b, t).rearrange("p (j n) -> p j n", j=4)).then_inc(o_copied_v, 1)
            beside.vector(dve)
            dve.wait_ge(mixed, 1)
            v.tensor_tensor(b.y[:], b.y[:], bank(b, 4), ALU.add).then_inc(y_ready, 1)
            dve.wait_ge(y_ready, 1)
            shift()
            dve.wait_ge(shifted, 2)
            beside.vector(dve)
            norm.vector(dve, h_t, b.xn[:], (0, 1), steps=(0,))
            beside.vector(dve)
            norm.vector(dve, h_t, b.xn[:], (0, 1), steps=(1,))
            dve.wait_ge(norm.done, 1)
            v.tensor_scalar(b.sq[:], b.xn[:], vec(b, ("ln_g", l)), vec(b, ("ln_b", l)), ALU.mult, ALU.add).then_inc(affine, 1)
            beside.vector(dve)
            for c in range(3):
                rows = HC[c][1]
                dve.wait_ge(hidden, 2 * c + 2)
                dve.wait_ge(gelu, c + 1)
                v.scalar_tensor_tensor(out=gated_t[0:rows, c], in0=bank(b, (1, 3, 0)[c])[0:rows], scalar=vec(b, (("b1_value", c), l), rows),
                                       in1=gelu_t[0:rows, c], op0=ALU.add, op1=ALU.mult).then_inc(gated, 1)
            beside.vector(dve)
            dve.wait_ge(out, 1)
            v.scalar_tensor_tensor(out=b.y[:], in0=bank(b, 1), scalar=vec(b, ("b2", l)), in1=b.y[:], op0=ALU.add, op1=ALU.add).then_inc(y_ready, 1)
            if l == DEPTH - 1:
                dve.wait_ge(y_ready, 2)
                v.scalar_tensor_tensor(out=b.x[:], in0=b.y[:], scalar=0.5, in1=b.x[:], op0=ALU.mult, op1=ALU.add)


def hand_over(nc, b, sem):
    moved = sem("stream_moved")
    with nc.Block() as block:
        @block.vector
        def _(dve):
            nc.vector.tensor_copy(b.x_late[:], b.x[:]).then_inc(moved, 1)


def build_program(nc, A, out):
    with ExitStack() as ctx:
        b = allocate(nc, ctx)
        later_loaded = ctx.enter_context(nc.semaphore("later_weights_loaded"))
        later = weights(nc, b, A)
        src = A["L0_attn_q"].rearrange("b n d -> (b n) d")
        dst = out.rearrange("b n d -> (b n) d")
        sems = Semaphores(nc)

        def stages(g, early, late):
            load = lambda beside: load_tokens(nc, b, sems.stage("load"), src, g, beside)
            first_and_third(nc, b, sems, "first", early, late, load if early else None,
                            transfers=(later, later_loaded) if early and not late else ([], None))
            if early and not late:
                rest_of_weights(nc, b, sems.stage("rest"), later_loaded, len(later))
            second(nc, b, sems, A["scratch"], early, late)
            first_and_third(nc, b, sems, "third", early, late)
            if late:
                store_tokens(nc, b, sems.stage("store"), dst, g - 1, early)
            else:
                hand_over(nc, b, sems.stage("hand_over"))
            sems.clear()

        stages(0, True, False)
        with nc.Fori(1, GROUPS) as g:
            stages(g, True, True)
        stages(GROUPS, False, True)


def constants():
    f = np.float32
    p = np.arange(128)
    fold32 = (p[:, None] % 32 == np.arange(32)[None, :]).astype(f)
    near = p[:, None] - np.arange(128)[None, :]
    wide = p[:, None] + 64 - np.arange(192)[None, :]
    mask = np.concatenate([np.where((d >= 0) & (d <= WINDOW), 0.0, NEG) for d in (near, wide)], axis=1).astype(f)
    half = np.arange(0, LD, 2, dtype=f)
    inv_freq = (f(1.0) / f(10000.0) ** (half / f(LD))).astype(f)
    t = np.arange(SEQ, dtype=f)
    freqs = np.concatenate([t[:, None] * inv_freq[None, :]] * 2, axis=1).astype(f)
    base = ((half + f(0.4 * LD)) / f(1.4 * LD)).astype(f)
    power = ((t - SEQ // 2) / f(WINDOW // 2)).astype(f)
    scale = np.concatenate([base[None, :] ** power[:, None]] * 2, axis=1).astype(f)
    sign = np.where(np.arange(LD) < LD // 2, -1.0, 1.0).astype(f)
    cos, sin = np.cos(freqs), np.sin(freqs) * sign
    rope = np.stack([cos * scale * 8, sin * scale * 8, cos / scale, sin / scale]).astype(f)
    rope = rope.reshape(4, 2, 128, LD).transpose(2, 0, 1, 3)
    dist = np.arange(-SEQ + 1, SEQ, dtype=np.float64)
    n = REL // 6
    absd = np.abs(dist)[:, None]
    half_life = 2.0 ** np.linspace(3.0, math.log(SEQ) / math.log(2.0), n)
    feat_exp = np.exp(-math.log(2.0) / half_life[None, :] * absd)
    widths = 2.0 ** np.arange(1, n + 1) - 1.0
    feat_cm = (widths[None, :] > absd).astype(np.float64)
    stddev = SEQ / (2.0 * n)
    mean = np.linspace(SEQ / n, float(SEQ), n)[None, :]
    conc, rate = (mean / stddev) ** 2, mean / stddev ** 2
    log_d = np.log(np.maximum(absd, 1e-300))
    log_norm = np.array([[math.lgamma(c) for c in conc[0]]]) - conc * np.log(rate)
    probs = np.where(absd > 0, np.exp((conc - 1.0) * log_d - rate * absd - log_norm), 0.0) + 1e-8
    feat_gamma = probs / probs.max(axis=-1, keepdims=True)
    emb = np.concatenate([feat_exp, feat_cm, feat_gamma], axis=-1)
    emb = np.concatenate([emb, np.sign(dist)[:, None] * emb], axis=-1)
    pos = np.zeros((REL, 2 * SEQ), f)
    pos[:, 0:2 * SEQ - 1] = emb.T
    return {"const_ident": np.eye(128, dtype=f), "const_fold32": fold32, "const_mask": mask,
            "const_rope": np.ascontiguousarray(rope), "const_pos": pos}


def kernel(**inputs):
    import concourse.bacc as bacc
    from concourse.bass_utils import run_bass_kernel_spmd as run

    nc = bacc.Bacc("TRN2", target_bir_lowering=False, num_devices=1)
    arrays, A = {}, {}
    for name, a in {**inputs, **constants()}.items():
        a = np.ascontiguousarray(a)
        arrays[f"in_{name}"] = a
        A[name] = nc.dram_tensor(f"in_{name}", a.shape, mybir.dt.from_np(a.dtype), kind="ExternalInput").ap()
    A["scratch"] = nc.dram_tensor("position_scores", (2, TILES, 128, 384), F32, kind="Internal").ap()
    out = nc.dram_tensor("out", (BATCH, SEQ, DIM), F32, kind="ExternalOutput").ap()
    build_program(nc, A, out)
    result = run(nc, [arrays], core_ids=[0])
    return result.results[0]["out"]
```
